# Optimizing a Trainium2 kernel written in Bass

```python
import numpy as np
import jax
import jax.numpy as jnp

def _softmax(x, axis=-1):
    return jax.nn.softmax(x, axis=axis)

def _gelu(x):
    return jax.nn.gelu(x, approximate=True)

def _silu(x):
    return jax.nn.silu(x)

def _sigmoid(x):
    return jax.nn.sigmoid(x)

def _layernorm(x, axis=-1, eps=1e-05):
    m = jnp.mean(x, axis=axis, keepdims=True)
    v = jnp.var(x, axis=axis, keepdims=True)
    return (x - m) / jnp.sqrt(v + eps)

def _scatter_add(tgt, idx, src, axis=0):
    return tgt.at[idx].add(src)

def _segment_sum(src, seg, n):
    return jax.ops.segment_sum(src, seg, n)
kernel_name = 'mk_xattn_ffn_d2_seqx_r8_6fc798'

def setup_inputs(seed: int=0):
    np.random.seed(seed)
    _w = jnp.asarray

    def _rec_inputs():
        import jax
        import jax.numpy as jnp
        _rk = jax.random.key(seed)
        x = 7.22e-05 + 1 * jax.random.normal(jax.random.fold_in(_rk, 1), (4, 512, 128), jnp.float32)
        _lenS = 512 - jax.random.randint(jax.random.fold_in(_rk, 7), (4,), 0, max(1, 512 // 4) + 1, jnp.int32)
        _lenS2 = 77 - jax.random.randint(jax.random.fold_in(_rk, 8), (4,), 0, max(1, 77 // 4) + 1, jnp.int32)
        _ctx_1024P = jax.random.normal(jax.random.fold_in(_rk, 11), (4, 16, 128), jnp.float32)
        _ctx_1024c = jax.random.dirichlet(jax.random.fold_in(_rk, 511), 0.3 * jnp.ones((16,), jnp.float32), (4, 77))
        _ctx_1024t = jnp.einsum('bsk,bkd->bsd', _ctx_1024c, _ctx_1024P)
        _ctx_1024t = _ctx_1024t * jax.lax.rsqrt(jnp.mean(jnp.square(_ctx_1024t)) + 1e-12) * 0.953939
        ctx_1024 = 4.13588e-05 + 0.999923 * (_ctx_1024t + 0.3 * jax.random.normal(jax.random.fold_in(_rk, 611), (4, 77, 128), jnp.float32))
        _validS = jnp.arange(512)[None, :] < _lenS[:, None]
        _validS2 = jnp.arange(77)[None, :] < _lenS2[:, None]
        _causal = jnp.tril(jnp.ones((512, 512), dtype=bool))
        mask_Bx1xSxS2_fk0 = jnp.where(jnp.broadcast_to(_validS2[:, None, None, :], (4, 1, 512, 77)), 0.0, 1.0).astype(jnp.float32)
        return (x, ctx_1024, mask_Bx1xSxS2_fk0)
    x, ctx_1024, mask_Bx1xSxS2_fk0 = _rec_inputs()

    def _L0_xattn_setup():
        import jax, jax.numpy as jnp
        import numpy as np
        B, L, D, H = (4, 256, 128, 16)
        HD = D // H
        NEG = -1000000000000000.0

        def _split_heads(x):
            b, l, _ = x.shape
            return x.reshape(b, l, H, HD).transpose(0, 2, 1, 3)
        key = jax.random.key(seed)
        ks = jax.random.split(key, 13)
        s = 1.0 / np.sqrt(D)
        inp = {'q': jax.random.normal(ks[0], (B, L, D), jnp.float32), 'k': jax.random.normal(ks[1], (B, L, D), jnp.float32), 'v': jax.random.normal(ks[2], (B, L, D), jnp.float32), 'mask': (jax.random.uniform(ks[3], (B, 1, L, L)) < 0.1).astype(jnp.float32), 'Wq': jax.random.normal(ks[4], (D, D), jnp.float32) * s, 'bq': jnp.zeros((D,), jnp.float32), 'Wk': jax.random.normal(ks[5], (D, D), jnp.float32) * s, 'bk': jnp.zeros((D,), jnp.float32), 'Wv': jax.random.normal(ks[6], (D, D), jnp.float32) * s, 'bv': jnp.zeros((D,), jnp.float32), 'Wo': jax.random.normal(ks[7], (D, D), jnp.float32) * s, 'bo': jnp.zeros((D,), jnp.float32)}
        return inp
    _L0_xattn_all = _L0_xattn_setup()
    _L0_xattn_in = {k: v for k, v in _L0_xattn_all.items() if k in ('Wq', 'bq', 'Wk', 'bk', 'Wv', 'bv', 'Wo', 'bo')}
    del _L0_xattn_all

    def _L0_ffn_setup():
        import jax, jax.numpy as jnp
        import numpy as np
        DIM = 128
        DEPTH = 2
        HEADS = 8
        DIM_HEAD = 64
        WINDOW = 64
        INNER = HEADS * DIM_HEAD
        HID = int(DIM * 4 * 2 / 3)
        B, N = (2, 1024)
        QK_SCALE = 8.0

        def shift_token(t):
            t1, t2 = jnp.split(t, 2, axis=-1)
            t2 = jnp.pad(t2, ((0, 0), (1, 0), (0, 0)))[:, :-1]
            return jnp.concatenate([t1, t2], axis=-1)

        def l2norm(t):
            return t / jnp.clip(jnp.linalg.norm(t, axis=-1, keepdims=True), 1e-12)

        def rotate_half(x):
            x1, x2 = jnp.split(x, 2, axis=-1)
            return jnp.concatenate([-x2, x1], axis=-1)

        def rotary_xpos(q, k):
            n = q.shape[-2]
            half_idx = jnp.arange(0, DIM_HEAD, 2, dtype=jnp.float32)
            inv_freq = 1.0 / 10000.0 ** (half_idx / DIM_HEAD)
            t = jnp.arange(n, dtype=jnp.float32)
            freqs = t[:, None] * inv_freq[None, :]
            freqs = jnp.concatenate([freqs, freqs], axis=-1)
            base = (half_idx + 0.4 * DIM_HEAD) / (1.4 * DIM_HEAD)
            power = (t - n // 2) / float(WINDOW // 2)
            scale = base[None, :] ** power[:, None]
            scale = jnp.concatenate([scale, scale], axis=-1)
            cos, sin = (jnp.cos(freqs), jnp.sin(freqs))
            q = q * cos * scale + rotate_half(q) * sin * scale
            k = k * cos / scale + rotate_half(k) * sin / scale
            return (q, k)

        def local_attention(q, k, v):
            b, h, n, d = q.shape
            w = n // WINDOW
            bq = q.reshape(b, h, w, WINDOW, d) * QK_SCALE
            bk = k.reshape(b, h, w, WINDOW, d)
            bv = v.reshape(b, h, w, WINDOW, d)

            def look_around(t):
                p = jnp.pad(t, ((0, 0), (0, 0), (1, 0), (0, 0), (0, 0)))
                return jnp.concatenate([p[:, :, :w], p[:, :, 1:]], axis=3)
            bk, bv = (look_around(bk), look_around(bv))
            bt = jnp.arange(n).reshape(w, WINDOW)
            btp = jnp.pad(bt, ((1, 0), (0, 0)), constant_values=-1)
            btk = jnp.concatenate([btp[:w], btp[1:]], axis=1)
            sim = jnp.einsum('bhwid,bhwjd->bhwij', bq, bk)
            i = bt[:, :, None]
            j = btk[:, None, :]
            mask = (i < j) | (i > j + WINDOW) | (j == -1)
            sim = jnp.where(mask, -jnp.finfo(sim.dtype).max, sim)
            attn = jax.nn.softmax(sim, axis=-1)
            out = jnp.einsum('bhwij,bhwjd->bhwid', attn, bv)
            return out.reshape(b, h, n, d)

        def _layer(x, wqkv, qs, ksc, wo, lg, lb, w1, b1, w2, b2):
            b, n, _ = x.shape
            h = shift_token(x)
            qkv = h @ wqkv
            q, k, v = jnp.split(qkv, 3, axis=-1)
            to_heads = lambda t: t.reshape(b, n, HEADS, DIM_HEAD).transpose(0, 2, 1, 3)
            q, k, v = (to_heads(q), to_heads(k), to_heads(v))
            q = l2norm(q) * qs
            k = l2norm(k) * ksc
            q, k = rotary_xpos(q, k)
            o = local_attention(q, k, v)
            o = o.transpose(0, 2, 1, 3).reshape(b, n, INNER)
            x = x + o @ wo
            h = shift_token(x)
            mu = h.mean(-1, keepdims=True)
            var = h.var(-1, keepdims=True)
            h = (h - mu) / jnp.sqrt(var + 1e-05) * lg + lb
            h = h @ w1 + b1
            a, g = jnp.split(h, 2, axis=-1)
            h = a * jax.nn.gelu(g, approximate=False)
            x = x + h @ w2 + b2
            return x
        key = jax.random.key(seed)
        ks = jax.random.split(key, 6)
        return {'x': jax.random.normal(ks[0], (B, N, DIM), jnp.float32), 'wqkv': jax.random.normal(ks[1], (DEPTH, DIM, 3 * INNER), jnp.float32) * 0.02, 'q_scale': jnp.ones((DEPTH, DIM_HEAD), jnp.float32), 'k_scale': jnp.ones((DEPTH, DIM_HEAD), jnp.float32), 'wo': jax.random.normal(ks[2], (DEPTH, INNER, DIM), jnp.float32) * 0.02, 'ln_g': jnp.ones((DEPTH, DIM), jnp.float32), 'ln_b': jnp.zeros((DEPTH, DIM), jnp.float32), 'w1': jax.random.normal(ks[3], (DEPTH, DIM, 2 * HID), jnp.float32) * 0.02, 'b1': jnp.zeros((DEPTH, 2 * HID), jnp.float32), 'w2': jax.random.normal(ks[4], (DEPTH, HID, DIM), jnp.float32) * 0.02, 'b2': jnp.zeros((DEPTH, DIM), jnp.float32)}
    _L0_ffn_all = _L0_ffn_setup()
    _L0_ffn_in = {k: v for k, v in _L0_ffn_all.items() if k in ('wqkv', 'q_scale', 'k_scale', 'wo', 'ln_g', 'ln_b', 'w1', 'b1', 'w2', 'b2')}
    del _L0_ffn_all

    def _L1_xattn_setup():
        import jax, jax.numpy as jnp
        import numpy as np
        import math
        D_MODEL = 128
        NHEAD = 16
        FACTOR = 1
        B, L = (2, 512)

        def _autocorr_forward(query, key, value, Wq, bq, Wk, bk, Wv, bv, Wo, bo):
            Bq, Lq, d = query.shape
            Lk = key.shape[1]
            H = NHEAD
            Dk = d // H
            Q = (query @ Wq + bq).reshape(Bq, Lq, H, Dk).transpose(0, 2, 1, 3)
            K = (key @ Wk + bk).reshape(Bq, Lk, H, Dk).transpose(0, 2, 1, 3)
            V = (value @ Wv + bv).reshape(Bq, Lk, H, Dk).transpose(0, 2, 1, 3)
            if Lk > Lq:
                K = K[:, :, :Lq, :]
                V = V[:, :, :Lq, :]
            elif Lq > Lk:
                pad = [(0, 0), (0, 0), (0, Lq - Lk), (0, 0)]
                K = jnp.pad(K, pad)
                V = jnp.pad(V, pad)
            Lloc = Lq
            Qf = jnp.fft.rfft(Q, axis=2)
            Kf = jnp.fft.rfft(K, axis=2)
            corr = jnp.fft.irfft(Qf * jnp.conj(Kf), n=Lloc, axis=2)
            corr_mean = corr.mean(axis=-1)
            top_k = min(max(1, int(FACTOR * math.log(Lloc + 1))), Lloc)
            w, idx = jax.lax.top_k(corr_mean, top_k)
            w = jax.nn.softmax(w, axis=-1)
            ar = jnp.arange(Lloc)
            shifted = (ar[None, None, None, :] + idx[..., None]) % Lloc
            rolled = jnp.take_along_axis(V[:, :, None, :, :], shifted[..., None], axis=3)
            out = jnp.einsum('bhk,bhkld->bhld', w, rolled)
            out = out.transpose(0, 2, 1, 3).reshape(Bq, Lq, d)
            return out @ Wo + bo
        key = jax.random.key(seed)
        ks = jax.random.split(key, 12)
        s = 0.02
        inp = {'query': jax.random.normal(ks[0], (B, L, D_MODEL), dtype=jnp.float32), 'key': jax.random.normal(ks[1], (B, L, D_MODEL), dtype=jnp.float32), 'value': jax.random.normal(ks[2], (B, L, D_MODEL), dtype=jnp.float32), 'Wq': jax.random.normal(ks[3], (D_MODEL, D_MODEL), dtype=jnp.float32) * s, 'bq': jnp.zeros((D_MODEL,), dtype=jnp.float32), 'Wk': jax.random.normal(ks[4], (D_MODEL, D_MODEL), dtype=jnp.float32) * s, 'bk': jnp.zeros((D_MODEL,), dtype=jnp.float32), 'Wv': jax.random.normal(ks[5], (D_MODEL, D_MODEL), dtype=jnp.float32) * s, 'bv': jnp.zeros((D_MODEL,), dtype=jnp.float32), 'Wo': jax.random.normal(ks[6], (D_MODEL, D_MODEL), dtype=jnp.float32) * s, 'bo': jnp.zeros((D_MODEL,), dtype=jnp.float32)}
        return inp
    _L1_xattn_all = _L1_xattn_setup()
    _L1_xattn_in = {k: v for k, v in _L1_xattn_all.items() if k in ('Wq', 'bq', 'Wk', 'bk', 'Wv', 'bv', 'Wo', 'bo')}
    del _L1_xattn_all

    def _L1_ffn_setup():
        import jax, jax.numpy as jnp
        import numpy as np
        D_MODEL = 128
        N_HEADS = 16
        HEAD_DIM = D_MODEL // N_HEADS
        FFN_DIM = 512
        N_EXPERTS = 8
        TOP_K = 2
        BATCH = 4
        SEQ = 128

        def _layernorm(x, w, b, eps=1e-05):
            mu = jnp.mean(x, axis=-1, keepdims=True)
            var = jnp.mean(jnp.square(x - mu), axis=-1, keepdims=True)
            return (x - mu) * jax.lax.rsqrt(var + eps) * w + b

        def _causal_attention(nx, Wqkv, bqkv, Wo, bo):
            B, S, D = nx.shape
            qkv = nx @ Wqkv + bqkv
            q, k, v = jnp.split(qkv, 3, axis=-1)
            q = q.reshape(B, S, N_HEADS, HEAD_DIM)
            k = k.reshape(B, S, N_HEADS, HEAD_DIM)
            v = v.reshape(B, S, N_HEADS, HEAD_DIM)
            scores = jnp.einsum('bqhd,bkhd->bhqk', q, k) / jnp.sqrt(jnp.float32(HEAD_DIM))
            causal = jnp.tril(jnp.ones((S, S), bool))
            scores = jnp.where(causal, scores, jnp.finfo(scores.dtype).min)
            attn = jax.nn.softmax(scores, axis=-1)
            out = jnp.einsum('bhqk,bkhd->bqhd', attn, v).reshape(B, S, D)
            return out @ Wo + bo

        def _moe_ffn(nx, gate_W, fc1_w, fc1_b, fc2_w, fc2_b):
            gate_logits = nx @ gate_W
            topk_vals, topk_idx = jax.lax.top_k(gate_logits, TOP_K)
            gate_w = jax.nn.softmax(topk_vals, axis=-1)
            dense_gates = jnp.sum(jax.nn.one_hot(topk_idx, N_EXPERTS, dtype=nx.dtype) * gate_w[..., None], axis=-2)
            moe_out = jnp.zeros_like(nx)
            for e in range(N_EXPERTS):
                h = jax.nn.gelu(jnp.einsum('bsd,fd->bsf', nx, fc1_w[e]) + fc1_b[e], approximate=False)
                y = jnp.einsum('bsf,df->bsd', h, fc2_w[e]) + fc2_b[e]
                moe_out = moe_out + y * dense_gates[..., e:e + 1]
            return moe_out
        key = jax.random.key(seed)
        ks = jax.random.split(key, 12)
        s = lambda k, shape, scale: jax.random.normal(k, shape, dtype=jnp.float32) * scale
        inp = {'x': s(ks[0], (BATCH, SEQ, D_MODEL), 1.0), 'ln1_w': jnp.ones((D_MODEL,), jnp.float32), 'ln1_b': jnp.zeros((D_MODEL,), jnp.float32), 'ln2_w': jnp.ones((D_MODEL,), jnp.float32), 'ln2_b': jnp.zeros((D_MODEL,), jnp.float32), 'Wqkv': s(ks[1], (D_MODEL, 3 * D_MODEL), 0.02), 'bqkv': jnp.zeros((3 * D_MODEL,), jnp.float32), 'Wo': s(ks[2], (D_MODEL, D_MODEL), 0.02), 'bo': jnp.zeros((D_MODEL,), jnp.float32), 'gate_W': s(ks[3], (D_MODEL, N_EXPERTS), 0.02), 'fc1_w': s(ks[4], (N_EXPERTS, FFN_DIM, D_MODEL), (2.0 / D_MODEL) ** 0.5), 'fc1_b': jnp.zeros((N_EXPERTS, FFN_DIM), jnp.float32), 'fc2_w': s(ks[5], (N_EXPERTS, D_MODEL, FFN_DIM), (1.0 / FFN_DIM) ** 0.5), 'fc2_b': jnp.zeros((N_EXPERTS, D_MODEL), jnp.float32)}
        return inp
    _L1_ffn_all = _L1_ffn_setup()
    _L1_ffn_in = {k: v for k, v in _L1_ffn_all.items() if k in ('ln1_w', 'ln1_b', 'ln2_w', 'ln2_b', 'Wqkv', 'bqkv', 'Wo', 'bo', 'gate_W', 'fc1_w', 'fc1_b', 'fc2_w', 'fc2_b')}
    del _L1_ffn_all
    return {'x': x, 'ctx_1024': ctx_1024, 'mask_Bx1xSxS2_fk0': mask_Bx1xSxS2_fk0, 'L0_xattn_Wq': _L0_xattn_in['Wq'], 'L0_xattn_bq': _L0_xattn_in['bq'], 'L0_xattn_Wk': _L0_xattn_in['Wk'], 'L0_xattn_bk': _L0_xattn_in['bk'], 'L0_xattn_Wv': _L0_xattn_in['Wv'], 'L0_xattn_bv': _L0_xattn_in['bv'], 'L0_xattn_Wo': _L0_xattn_in['Wo'], 'L0_xattn_bo': _L0_xattn_in['bo'], 'L0_ffn_wqkv': _L0_ffn_in['wqkv'], 'L0_ffn_q_scale': _L0_ffn_in['q_scale'], 'L0_ffn_k_scale': _L0_ffn_in['k_scale'], 'L0_ffn_wo': _L0_ffn_in['wo'], 'L0_ffn_ln_g': _L0_ffn_in['ln_g'], 'L0_ffn_ln_b': _L0_ffn_in['ln_b'], 'L0_ffn_w1': _L0_ffn_in['w1'], 'L0_ffn_b1': _L0_ffn_in['b1'], 'L0_ffn_w2': _L0_ffn_in['w2'], 'L0_ffn_b2': _L0_ffn_in['b2'], 'L1_xattn_Wq': _L1_xattn_in['Wq'], 'L1_xattn_bq': _L1_xattn_in['bq'], 'L1_xattn_Wk': _L1_xattn_in['Wk'], 'L1_xattn_bk': _L1_xattn_in['bk'], 'L1_xattn_Wv': _L1_xattn_in['Wv'], 'L1_xattn_bv': _L1_xattn_in['bv'], 'L1_xattn_Wo': _L1_xattn_in['Wo'], 'L1_xattn_bo': _L1_xattn_in['bo'], 'L1_ffn_ln1_w': _L1_ffn_in['ln1_w'], 'L1_ffn_ln1_b': _L1_ffn_in['ln1_b'], 'L1_ffn_ln2_w': _L1_ffn_in['ln2_w'], 'L1_ffn_ln2_b': _L1_ffn_in['ln2_b'], 'L1_ffn_Wqkv': _L1_ffn_in['Wqkv'], 'L1_ffn_bqkv': _L1_ffn_in['bqkv'], 'L1_ffn_Wo': _L1_ffn_in['Wo'], 'L1_ffn_bo': _L1_ffn_in['bo'], 'L1_ffn_gate_W': _L1_ffn_in['gate_W'], 'L1_ffn_fc1_w': _L1_ffn_in['fc1_w'], 'L1_ffn_fc1_b': _L1_ffn_in['fc1_b'], 'L1_ffn_fc2_w': _L1_ffn_in['fc2_w'], 'L1_ffn_fc2_b': _L1_ffn_in['fc2_b']}

def reference(x, ctx_1024, mask_Bx1xSxS2_fk0, L0_xattn_Wq, L0_xattn_bq, L0_xattn_Wk, L0_xattn_bk, L0_xattn_Wv, L0_xattn_bv, L0_xattn_Wo, L0_xattn_bo, L0_ffn_wqkv, L0_ffn_q_scale, L0_ffn_k_scale, L0_ffn_wo, L0_ffn_ln_g, L0_ffn_ln_b, L0_ffn_w1, L0_ffn_b1, L0_ffn_w2, L0_ffn_b2, L1_xattn_Wq, L1_xattn_bq, L1_xattn_Wk, L1_xattn_bk, L1_xattn_Wv, L1_xattn_bv, L1_xattn_Wo, L1_xattn_bo, L1_ffn_ln1_w, L1_ffn_ln1_b, L1_ffn_ln2_w, L1_ffn_ln2_b, L1_ffn_Wqkv, L1_ffn_bqkv, L1_ffn_Wo, L1_ffn_bo, L1_ffn_gate_W, L1_ffn_fc1_w, L1_ffn_fc1_b, L1_ffn_fc2_w, L1_ffn_fc2_b):
    import jax
    import jax.numpy as jnp

    def _L0_xattn_ref(q, k, v, mask, Wq, bq, Wk, bk, Wv, bv, Wo, bo):
        import jax, jax.numpy as jnp
        import numpy as np
        B, L, D, H = (4, 256, 128, 16)
        HD = D // H
        NEG = -1000000000000000.0

        def _split_heads(x):
            b, l, _ = x.shape
            return x.reshape(b, l, H, HD).transpose(0, 2, 1, 3)
        qw = q @ Wq + bq
        kw = k @ Wk + bk
        vw = v @ Wv + bv
        qh = _split_heads(qw)
        kh = _split_heads(kw)
        vh = _split_heads(vw)
        scale = 1.0 / jnp.sqrt(jnp.float32(HD))
        scores = jnp.einsum('bhqd,bhkd->bhqk', qh, kh) * scale
        scores = scores + mask * NEG
        weights = jax.nn.softmax(scores, axis=-1)
        out = jnp.einsum('bhqk,bhkd->bhqd', weights, vh)
        out = out.transpose(0, 2, 1, 3).reshape(q.shape[0], q.shape[1], D)
        return out @ Wo + bo

    def _L0_ffn_ref(x, wqkv, q_scale, k_scale, wo, ln_g, ln_b, w1, b1, w2, b2):
        import jax, jax.numpy as jnp
        import numpy as np
        DIM = 128
        DEPTH = 2
        HEADS = 8
        DIM_HEAD = 64
        WINDOW = 64
        INNER = HEADS * DIM_HEAD
        HID = int(DIM * 4 * 2 / 3)
        B, N = (2, 1024)
        QK_SCALE = 8.0

        def shift_token(t):
            t1, t2 = jnp.split(t, 2, axis=-1)
            t2 = jnp.pad(t2, ((0, 0), (1, 0), (0, 0)))[:, :-1]
            return jnp.concatenate([t1, t2], axis=-1)

        def l2norm(t):
            return t / jnp.clip(jnp.linalg.norm(t, axis=-1, keepdims=True), 1e-12)

        def rotate_half(x):
            x1, x2 = jnp.split(x, 2, axis=-1)
            return jnp.concatenate([-x2, x1], axis=-1)

        def rotary_xpos(q, k):
            n = q.shape[-2]
            half_idx = jnp.arange(0, DIM_HEAD, 2, dtype=jnp.float32)
            inv_freq = 1.0 / 10000.0 ** (half_idx / DIM_HEAD)
            t = jnp.arange(n, dtype=jnp.float32)
            freqs = t[:, None] * inv_freq[None, :]
            freqs = jnp.concatenate([freqs, freqs], axis=-1)
            base = (half_idx + 0.4 * DIM_HEAD) / (1.4 * DIM_HEAD)
            power = (t - n // 2) / float(WINDOW // 2)
            scale = base[None, :] ** power[:, None]
            scale = jnp.concatenate([scale, scale], axis=-1)
            cos, sin = (jnp.cos(freqs), jnp.sin(freqs))
            q = q * cos * scale + rotate_half(q) * sin * scale
            k = k * cos / scale + rotate_half(k) * sin / scale
            return (q, k)

        def local_attention(q, k, v):
            b, h, n, d = q.shape
            w = n // WINDOW
            bq = q.reshape(b, h, w, WINDOW, d) * QK_SCALE
            bk = k.reshape(b, h, w, WINDOW, d)
            bv = v.reshape(b, h, w, WINDOW, d)

            def look_around(t):
                p = jnp.pad(t, ((0, 0), (0, 0), (1, 0), (0, 0), (0, 0)))
                return jnp.concatenate([p[:, :, :w], p[:, :, 1:]], axis=3)
            bk, bv = (look_around(bk), look_around(bv))
            bt = jnp.arange(n).reshape(w, WINDOW)
            btp = jnp.pad(bt, ((1, 0), (0, 0)), constant_values=-1)
            btk = jnp.concatenate([btp[:w], btp[1:]], axis=1)
            sim = jnp.einsum('bhwid,bhwjd->bhwij', bq, bk)
            i = bt[:, :, None]
            j = btk[:, None, :]
            mask = (i < j) | (i > j + WINDOW) | (j == -1)
            sim = jnp.where(mask, -jnp.finfo(sim.dtype).max, sim)
            attn = jax.nn.softmax(sim, axis=-1)
            out = jnp.einsum('bhwij,bhwjd->bhwid', attn, bv)
            return out.reshape(b, h, n, d)

        def _layer(x, wqkv, qs, ksc, wo, lg, lb, w1, b1, w2, b2):
            b, n, _ = x.shape
            h = shift_token(x)
            qkv = h @ wqkv
            q, k, v = jnp.split(qkv, 3, axis=-1)
            to_heads = lambda t: t.reshape(b, n, HEADS, DIM_HEAD).transpose(0, 2, 1, 3)
            q, k, v = (to_heads(q), to_heads(k), to_heads(v))
            q = l2norm(q) * qs
            k = l2norm(k) * ksc
            q, k = rotary_xpos(q, k)
            o = local_attention(q, k, v)
            o = o.transpose(0, 2, 1, 3).reshape(b, n, INNER)
            x = x + o @ wo
            h = shift_token(x)
            mu = h.mean(-1, keepdims=True)
            var = h.var(-1, keepdims=True)
            h = (h - mu) / jnp.sqrt(var + 1e-05) * lg + lb
            h = h @ w1 + b1
            a, g = jnp.split(h, 2, axis=-1)
            h = a * jax.nn.gelu(g, approximate=False)
            x = x + h @ w2 + b2
            return x
        for l in range(DEPTH):
            x = _layer(x, wqkv[l], q_scale[l], k_scale[l], wo[l], ln_g[l], ln_b[l], w1[l], b1[l], w2[l], b2[l])
        return x

    def _L1_xattn_ref(query, key, value, Wq, bq, Wk, bk, Wv, bv, Wo, bo):
        import jax, jax.numpy as jnp
        import numpy as np
        import math
        D_MODEL = 128
        NHEAD = 16
        FACTOR = 1
        B, L = (2, 512)

        def _autocorr_forward(query, key, value, Wq, bq, Wk, bk, Wv, bv, Wo, bo):
            Bq, Lq, d = query.shape
            Lk = key.shape[1]
            H = NHEAD
            Dk = d // H
            Q = (query @ Wq + bq).reshape(Bq, Lq, H, Dk).transpose(0, 2, 1, 3)
            K = (key @ Wk + bk).reshape(Bq, Lk, H, Dk).transpose(0, 2, 1, 3)
            V = (value @ Wv + bv).reshape(Bq, Lk, H, Dk).transpose(0, 2, 1, 3)
            if Lk > Lq:
                K = K[:, :, :Lq, :]
                V = V[:, :, :Lq, :]
            elif Lq > Lk:
                pad = [(0, 0), (0, 0), (0, Lq - Lk), (0, 0)]
                K = jnp.pad(K, pad)
                V = jnp.pad(V, pad)
            Lloc = Lq
            Qf = jnp.fft.rfft(Q, axis=2)
            Kf = jnp.fft.rfft(K, axis=2)
            corr = jnp.fft.irfft(Qf * jnp.conj(Kf), n=Lloc, axis=2)
            corr_mean = corr.mean(axis=-1)
            top_k = min(max(1, int(FACTOR * math.log(Lloc + 1))), Lloc)
            w, idx = jax.lax.top_k(corr_mean, top_k)
            w = jax.nn.softmax(w, axis=-1)
            ar = jnp.arange(Lloc)
            shifted = (ar[None, None, None, :] + idx[..., None]) % Lloc
            rolled = jnp.take_along_axis(V[:, :, None, :, :], shifted[..., None], axis=3)
            out = jnp.einsum('bhk,bhkld->bhld', w, rolled)
            out = out.transpose(0, 2, 1, 3).reshape(Bq, Lq, d)
            return out @ Wo + bo
        return _autocorr_forward(query, key, value, Wq, bq, Wk, bk, Wv, bv, Wo, bo)

    def _L1_ffn_ref(x, ln1_w, ln1_b, ln2_w, ln2_b, Wqkv, bqkv, Wo, bo, gate_W, fc1_w, fc1_b, fc2_w, fc2_b):
        import jax, jax.numpy as jnp
        import numpy as np
        D_MODEL = 128
        N_HEADS = 16
        HEAD_DIM = D_MODEL // N_HEADS
        FFN_DIM = 512
        N_EXPERTS = 8
        TOP_K = 2
        BATCH = 4
        SEQ = 128

        def _layernorm(x, w, b, eps=1e-05):
            mu = jnp.mean(x, axis=-1, keepdims=True)
            var = jnp.mean(jnp.square(x - mu), axis=-1, keepdims=True)
            return (x - mu) * jax.lax.rsqrt(var + eps) * w + b

        def _causal_attention(nx, Wqkv, bqkv, Wo, bo):
            B, S, D = nx.shape
            qkv = nx @ Wqkv + bqkv
            q, k, v = jnp.split(qkv, 3, axis=-1)
            q = q.reshape(B, S, N_HEADS, HEAD_DIM)
            k = k.reshape(B, S, N_HEADS, HEAD_DIM)
            v = v.reshape(B, S, N_HEADS, HEAD_DIM)
            scores = jnp.einsum('bqhd,bkhd->bhqk', q, k) / jnp.sqrt(jnp.float32(HEAD_DIM))
            causal = jnp.tril(jnp.ones((S, S), bool))
            scores = jnp.where(causal, scores, jnp.finfo(scores.dtype).min)
            attn = jax.nn.softmax(scores, axis=-1)
            out = jnp.einsum('bhqk,bkhd->bqhd', attn, v).reshape(B, S, D)
            return out @ Wo + bo

        def _moe_ffn(nx, gate_W, fc1_w, fc1_b, fc2_w, fc2_b):
            gate_logits = nx @ gate_W
            topk_vals, topk_idx = jax.lax.top_k(gate_logits, TOP_K)
            gate_w = jax.nn.softmax(topk_vals, axis=-1)
            dense_gates = jnp.sum(jax.nn.one_hot(topk_idx, N_EXPERTS, dtype=nx.dtype) * gate_w[..., None], axis=-2)
            moe_out = jnp.zeros_like(nx)
            for e in range(N_EXPERTS):
                h = jax.nn.gelu(jnp.einsum('bsd,fd->bsf', nx, fc1_w[e]) + fc1_b[e], approximate=False)
                y = jnp.einsum('bsf,df->bsd', h, fc2_w[e]) + fc2_b[e]
                moe_out = moe_out + y * dense_gates[..., e:e + 1]
            return moe_out
        nx = _layernorm(x, ln1_w, ln1_b)
        attn_out = _causal_attention(nx, Wqkv, bqkv, Wo, bo)
        x = x + attn_out
        nx2 = _layernorm(x, ln2_w, ln2_b)
        moe_out = _moe_ffn(nx2, gate_W, fc1_w, fc1_b, fc2_w, fc2_b)
        return x + moe_out
    x = x + _L0_xattn_ref(_layernorm(x, axis=-1), ctx_1024, ctx_1024, mask_Bx1xSxS2_fk0, L0_xattn_Wq, L0_xattn_bq, L0_xattn_Wk, L0_xattn_bk, L0_xattn_Wv, L0_xattn_bv, L0_xattn_Wo, L0_xattn_bo)
    x = x + _L0_ffn_ref(_layernorm(x, axis=-1), L0_ffn_wqkv, L0_ffn_q_scale, L0_ffn_k_scale, L0_ffn_wo, L0_ffn_ln_g, L0_ffn_ln_b, L0_ffn_w1, L0_ffn_b1, L0_ffn_w2, L0_ffn_b2)
    x = x + _L1_xattn_ref(_layernorm(x, axis=-1), ctx_1024, ctx_1024, L1_xattn_Wq, L1_xattn_bq, L1_xattn_Wk, L1_xattn_bk, L1_xattn_Wv, L1_xattn_bv, L1_xattn_Wo, L1_xattn_bo)
    x = x + _L1_ffn_ref(_layernorm(x, axis=-1), L1_ffn_ln1_w, L1_ffn_ln1_b, L1_ffn_ln2_w, L1_ffn_ln2_b, L1_ffn_Wqkv, L1_ffn_bqkv, L1_ffn_Wo, L1_ffn_bo, L1_ffn_gate_W, L1_ffn_fc1_w, L1_ffn_fc1_b, L1_ffn_fc2_w, L1_ffn_fc2_b)
    return x

_drawn_inputs = setup_inputs


def setup_inputs(seed=0):
    import zlib

    import numpy as np

    out = dict(_drawn_inputs(seed))
    spreads = {'L0_xattn_bq': (0.0, 0.1),
     'L0_xattn_bk': (0.0, 0.8),
     'L0_xattn_bv': (0.0, 0.1),
     'L0_xattn_bo': (0.0, 0.1),
     'L0_ffn_q_scale': (1.0, 0.6),
     'L0_ffn_k_scale': (1.0, 0.6),
     'L0_ffn_ln_g': (1.0, 0.6),
     'L0_ffn_ln_b': (0.0, 0.8),
     'L0_ffn_b1': (0.0, 0.598),
     'L0_ffn_b2': (0.0, 0.1),
     'L1_xattn_bq': (0.0, 0.8),
     'L1_xattn_bk': (0.0, 0.683),
     'L1_xattn_bv': (0.0, 0.701),
     'L1_xattn_bo': (0.0, 0.1),
     'L1_ffn_ln1_w': (1.0, 0.6),
     'L1_ffn_ln1_b': (0.0, 0.48),
     'L1_ffn_ln2_w': (1.0, 0.2),
     'L1_ffn_ln2_b': (0.0, 0.1),
     'L1_ffn_bqkv': (0.0, 0.1),
     'L1_ffn_bo': (0.0, 0.1),
     'L1_ffn_fc1_b': (0.0, 0.524),
     'L1_ffn_fc2_b': (0.0, 0.357)}
    factors = {'L0_ffn_w1': 3.025,
     'L0_ffn_w2': 2.761,
     'L1_xattn_Wq': 5.097,
     'L1_xattn_Wk': 4.228,
     'L1_xattn_Wv': 4.534,
     'L1_xattn_Wo': 3.976}
    for name, (base, spread) in spreads.items():
        noise = np.random.default_rng([zlib.crc32(name.encode()), seed]).standard_normal(out[name].shape)
        drawn = base * np.exp(spread * noise) if base else spread * noise
        out[name] = jnp.asarray(drawn.astype(out[name].dtype))
    for name, factor in factors.items():
        out[name] = (out[name] * factor).astype(out[name].dtype)
    return out
```

```python
from contextlib import ExitStack

import concourse.bass as bass
from concourse import mybir
from concourse.alu_op_type import AluOpType as ALU

F32 = mybir.dt.float32
ACT = mybir.ActivationFunctionType
X_AXIS = mybir.AxisListType.X

P = 128
BATCH, SEQ, CTX = 4, 512, 77
TILES = SEQ // P
HEADS, HD = 16, 8
LAYERS, LHEADS, LHD, WIN = 2, 8, 64, 64
PAIRS = LHEADS // 2
HID = 341
CHUNKS = [(0, 128), (128, 128), (256, HID - 256)]
EXPERTS, FFN = 8, 512
FC = FFN // P
TOPK = 6
HALF = SEQ // 2
SCALE = float(HD) ** -0.5
QK_SCALE = 8.0
EPS = 1e-5
NEG = -1e15
SENTINEL = -3.0e38
REPLACED = -3.3e38

WEIGHTS = (
    [("aq", P), ("ak", P), ("av", P), ("ao", P), ("abq", 1), ("abk", 1), ("abv", P), ("abo", P)]
    + [(f"{n}{l}", c) for l in range(LAYERS) for n, c in (
        ("qkv", 3 * 512), ("qs", LHD), ("ks", LHD), ("bwo", PAIRS * P), ("lng", 1), ("lnb", 1),
        ("w1", 2 * HID), ("b1a", 3), ("b1g", 3), ("w2", 3 * P), ("b2", P))]
    + [("cq", P), ("ck", P), ("cv", P), ("co", P), ("cbq", P), ("cbk", P), ("cbv", P), ("cbo", P)]
    + [("ln1w", 1), ("ln1b", 1), ("ln2w", 1), ("ln2b", 1), ("dqkv", 3 * P), ("dbq", 1), ("dbk", 1), ("dbv", P),
       ("dwo", P), ("dbo", P), ("gate", EXPERTS), ("fc2b", P), ("fc1b", EXPERTS * FC),
       ("fc1", EXPERTS * FFN), ("fc2", EXPERTS * FFN)])
CONSTS = [("ident", P), ("nident", P), ("headmask", 4), ("ind", HEADS), ("nind", HEADS), ("local", 2 * P),
          ("causal", SEQ), ("rot", TILES * 2 * 2 * LHD), ("dft", TILES * SEQ), ("idft", TILES * SEQ)]


def columns(parts):
    at, out = 0, {}
    for name, n in parts:
        out[name] = (at, at + n)
        at += n
    return out, at


WCOL, WTOTAL = columns(WEIGHTS)
CCOL, CTOTAL = columns(CONSTS)
GROUPS = [("aq", "abo"), ("qkv0", "b20"), ("qkv1", "b21"), ("cq", "cbo"), ("ln1w", "fc1b"), ("fc1", "fc2")]

CAUSAL_UNITS = []
for _t in range(TILES):
    _per = {0: 4, 1: 2, 2: 1, 3: 1}[_t]
    for _g in (0, 2):
        for _i in range(0, 4, _per):
            CAUSAL_UNITS.append((_t, [[4 * _g + _i + j for j in range(_per)],
                                      [4 * (_g + 1) + _i + j for j in range(_per)]]))


class Ring:

    def __init__(self, sem, name, slots, keys):
        self.full = [sem(f"{name}_full{i}") for i in range(slots)]
        self.free = [sem(f"{name}_free{i}") for i in range(slots)]
        self.at = {k: (i % slots, i // slots) for i, k in enumerate(keys)}
        assert len(self.at) == len(keys)

    def slot(self, key):
        return self.at[key][0]

    def filled(self, key):
        s, n = self.at[key]
        return self.full[s], n + 1

    def emptied(self, key):
        s, n = self.at[key]
        return self.free[s], n + 1

    def reused(self, key):
        s, n = self.at[key]
        return (self.free[s], n) if n else None

    def fill(self, key):
        return self.full[self.slot(key)]

    def empty(self, key):
        return self.free[self.slot(key)]


class Marks:

    def __init__(self, sem, name, keys):
        self.sem = sem(name)
        self.n = {k: i + 1 for i, k in enumerate(keys)}

    def done(self, key):
        return self.sem, self.n[key]


def program(nc, x_dram, ctxT_dram, mask_dram, weights_dram, consts_dram, out_dram, last_stage="D"):
    with ExitStack() as stack:
        sems = []

        def sem(name):
            s = stack.enter_context(nc.semaphore(name))
            sems.append(s)
            return s

        def sb(name, shape):
            return stack.enter_context(nc.sbuf_tensor(name, shape, F32))

        wt = sb("wt", [P, WTOTAL])
        cs = sb("cs", [P, CTOTAL])

        def w(name, rows=P):
            a, b = WCOL[name]
            return wt[0:rows, a:b]

        def c(name, rows=P):
            a, b = CCOL[name]
            return cs[0:rows, a:b]

        ident = c("ident")
        dft = c("dft").rearrange("p (t f) -> p t f", t=TILES)
        idft = c("idft").rearrange("p (t f) -> p t f", t=TILES)
        x = sb("x", [P, TILES, P])
        y = sb("y", [P, TILES, P])
        ctxT = sb("ctxT", [P, CTX])
        maskb = sb("maskb", [P, TILES, CTX])
        ntok = sb("ntok", [P, TILES, P])
        otok = sb("otok", [P, TILES, P])
        nT = sb("nT", [P, SEQ])
        hT = sb("hT", [P, SEQ])
        QT = sb("QT", [P, SEQ])
        kTmA = sb("kTmA", [P, 4, CTX])
        vA = sb("vA", [CTX, HEADS, HD + 1])
        qT = sb("qT", [P, PAIRS, SEQ])
        oT = qT
        kT = sb("kT", [P, PAIRS, WIN + SEQ])
        kTmD = qT
        vnat = sb("vnat", [P, TILES, LHEADS, LHD + 1])
        vmix = sb("vmix", [P, TILES, LHEADS, LHD + 1])
        vD = sb("vD", [P, TILES, HEADS, HD + 1])
        rot_base = c("rot").rearrange("p (t q a d) -> p t q a d", t=TILES, q=2, a=2)
        rot = [sb("rot", [P, TILES, 2, 2, LHD])[:], rot_base]
        qr = sb("qr", [P, 2, 2, 512])
        probs = sb("probs", [P, 2, 1024])
        probsT = sb("probsT", [P, 4, 512])
        o8 = sb("o8", [P, 2, 512])
        gl = o8
        hid = sb("hid", [P, 2, FC, SEQ])
        sq, qn = hid[:, 0, 0:2, :], hid[:, 0, 2:4, :]
        t1, t2 = hid[:, 1, 0:2, :], hid[:, 1, 2:4, :]
        qf, p1, p2, wf = (hid[:, 0, i, :] for i in range(4))
        ktok, vtok = hid[0:CTX, 1, 0, 0:P], hid[0:CTX, 1, 0, P:2 * P]
        wx, of = hid[:, 1, 1, :], hid[:, 1, 2, :]
        corr = sb("corr", [HEADS, SEQ + 2])
        rep = sb("rep", [HEADS, SEQ + 2])
        ew = sb("ew", [HEADS, SEQ])
        G = sb("G", [P, 4, HEADS])
        top = sb("top", [HEADS, 24])
        stats = sb("stats", [P, TILES, 6])
        mv = sb("mv", [P, TILES, 2])
        small = sb("small", [P, 8])
        rstd = sb("rstd", [P, TILES])
        mhalf = sb("mhalf", [P, 16])
        ss = sb("ss", [P, 2, 16])
        rn = sb("rn", [P, 2, 16])
        mx = sb("mx", [P, 2, 8])
        nm = sb("nm", [P, 2, 8])
        rden = sb("rden", [P, 2, 16])
        logit = sb("logit", [P, TILES, 16])
        lrep = sb("lrep", [P, TILES, 16])
        gtop = sb("gtop", [P, TILES, 8])
        gtwo = sb("gtwo", [P, TILES, 8])
        gex = sb("gex", [P, TILES, 8])
        gsum = sb("gsum", [P, TILES])
        gates = sb("gates", [P, TILES, 8])
        gT = sb("gT", [EXPERTS, SEQ])

        psS = stack.enter_context(nc.psum_tensor("psS", [P, 2, 2, 512], F32))
        psT = stack.enter_context(nc.psum_tensor("psT", [P, 2, 512], F32))
        psM = stack.enter_context(nc.psum_tensor("psM", [P, 2, 512], F32))

        NA, ND = 2 * TILES, len(CAUSAL_UNITS)
        LT = [(l, t) for l in range(LAYERS) for t in range(TILES)]
        s_keys = [("A", u) for u in range(NA)]
        t_keys = ["A n"] + [("A p", u, j) for u in range(NA) for j in range(2)] + ["A o"]
        m_keys = ["A kv", "A q"] + [("A o", t) for t in range(TILES)] + ["A wo"]
        for l in range(LAYERS):
            s_keys += [("B qk", l, t) for t in range(TILES)] + [("B s", l, t) for t in range(TILES)]
            s_keys += [("B w1", l, i) for i in range(3)]
            t_keys += [("B y", l)] + [("B qk", l, t, j) for t in range(TILES) for j in range(2)]
            for i in range(TILES + 3):
                if 1 <= i <= TILES:
                    t_keys += [("B p", l, i - 1, 0), ("B p", l, i - 1, 1)]
                if i >= 3:
                    t_keys += [("B o", l, i - 3)]
            t_keys += [("B y2", l), ("B tok", l), ("B n", l)]
            m_keys += [("B v", l, t) for t in range(TILES)]
            m_keys += [("B o", l, t, j) for t in range(TILES) for j in range(2)]
            m_keys += [("B wo", l), ("B w2", l)]
        t_keys += ["C n", "C w"]
        m_keys += ["C kv", "C kf", "C q", "C qf", "C g", "C corr", "C wf", "C vf", "C of", "C out", "C wo"]
        s_keys += [("D", u) for u in range(ND)] + [("D f1", e, i) for e in range(EXPERTS) for i in range(2)]
        t_keys += ["D n"] + [("D p", u, j) for u in range(ND) for j in range(2)] + ["D o", "D n2", "D g"]
        m_keys += ["D q", "D k", "D v"] + [("D o", t) for t in range(TILES)] + ["D wo", "D gate", "D b2"]
        m_keys += [("D f2", e) for e in range(EXPERTS)]
        S = Ring(sem, "scores", 2, s_keys)
        T = Ring(sem, "turned", 2, t_keys)
        M = Ring(sem, "products", 2, m_keys)
        turned_probs = {k: i % 4 for i, k in enumerate(k for k in t_keys if k[0] in ("A p", "B p", "D p"))}

        LNS = ["A", "B", ("F", 0), ("F", 1), "C", "D0", "D1", "D2"]
        UNITS = [("A", u) for u in range(NA)] + [("B", l, t) for l, t in LT] + [("D", u) for u in range(ND)]
        unit_index = {k: i for i, k in enumerate(UNITS)}
        turned_key = {("A", u): ("A p", u, 1) for u in range(NA)}
        turned_key.update({("B", l, t): ("B p", l, t, 1) for l, t in LT})
        turned_key.update({("D", u): ("D p", u, 1) for u in range(ND)})
        stats_ready = Marks(sem, "stats_ready", LNS)
        rstd_ready = Marks(sem, "rstd_ready", LNS)
        normed = Marks(sem, "normed", LNS)
        maxima = Marks(sem, "maxima", UNITS)
        centered = Marks(sem, "centered", [("A", u) for u in range(NA)])
        exps = Marks(sem, "exps", UNITS)
        squares = Marks(sem, "squares", LT)
        sums = Marks(sem, "sums", LT)
        norms = Marks(sem, "norms", LT)
        cos_part = Marks(sem, "cos_part", LT)
        rotated = Marks(sem, "rotated", LT)
        gelus = Marks(sem, "gelus", [(l, i) for l in range(LAYERS) for i in range(3)])
        biased = Marks(sem, "biased", ["A", ("B", 0), ("B", 1), "C", "D"])
        ffn_added = Marks(sem, "ffn_added", ["B"])
        spectra = Marks(sem, "spectra", ["C qk", "C vw"])
        peak = Marks(sem, "peak", ["C", "D"])
        selection_exps = Marks(sem, "selection_exps", ["C", "D"])
        selection = Marks(sem, "selection", ["C", "D"])
        finished = Marks(sem, "finished", ["D"])
        mask_scaled = Marks(sem, "mask_scaled", ["A"])
        dve_chain = sem("dve_chain")
        pool_chain = sem("pool_chain")
        x_in = sem("x_in")
        ctx_in = sem("ctx_in")
        mask_in = sem("mask_in")
        x_out = sem("x_out")
        batch_sems = list(sems)

        weights_in = [sem(f"weights_in{i}") for i in range(len(GROUPS))]
        consts_in = sem("consts_in")
        set_up = sem("set_up")

        with nc.Block() as block:
            @block.sync
            def _(sp):
                def load(i):
                    a, b = WCOL[GROUPS[i][0]][0], WCOL[GROUPS[i][1]][1]
                    sp.dma_start(wt[:, a:b], weights_dram[:, a:b]).then_inc(weights_in[i], 16)
                load(0)
                sp.dma_start(cs[:, :], consts_dram).then_inc(consts_in, 16)
                for i in range(1, len(GROUPS)):
                    load(i)

            @block.vector
            def _(dve):
                v = nc.vector
                v.memset(mhalf[:], -0.5)
                v.memset(vA[:, :, HD:HD + 1], 1.0)
                v.memset(vD[:, :, :, HD:HD + 1], 1.0)
                v.memset(vnat[:, :, :, LHD:LHD + 1], 1.0)
                v.memset(vmix[:, :, :, LHD:LHD + 1], 1.0)
                v.memset(vmix[0:WIN, 0, :, 0:LHD], 0.0)
                v.memset(hT[64:P, 0:1], 0.0)
                v.memset(kT[:, :, 0:WIN], 0.0)
                v.memset(corr[:, SEQ:SEQ + 2], SENTINEL)
                v.memset(top[:, 8 + TOPK:16], SENTINEL)
                v.memset(logit[:, :, 8:16], SENTINEL)
                v.memset(gtwo[:, :, 2:8], SENTINEL)

            @block.gpsimd
            def _(pool):
                g = nc.gpsimd
                pool.wait_ge(consts_in, 16)
                pool.wait_ge(weights_in[1], 16)
                pool.wait_ge(weights_in[2], 16)
                for l in range(LAYERS):
                    for j, name in enumerate(("qs", "ks")):
                        s = w(f"{name}{l}")
                        g.tensor_tensor(rot[l][:, :, j, 0, :], rot_base[:, :, j, 0, :],
                                        s[:, None, :].broadcast_to([P, TILES, LHD]), ALU.mult)
                        for o, i in ((0, 32), (32, 0)):
                            last = g.tensor_tensor(rot[l][:, :, j, 1, o:o + 32], rot_base[:, :, j, 1, o:o + 32],
                                                   s[:, None, i:i + 32].broadcast_to([P, TILES, 32]), ALU.mult)
                    last.then_inc(set_up, 1)
                    pool.wait_ge(set_up, l + 1)

        with nc.Fori(0, BATCH) as batch:
            with nc.Block() as block:
                @block.sync
                def _(sp):
                    sp.dma_start(x[:], x_dram[bass.ds(batch, 1), :, :].rearrange("o (t p) d -> p (o t) d", p=P)).then_inc(x_in, 16)
                    sp.dma_start(ctxT[:], ctxT_dram[bass.ds(batch, 1), :, :].rearrange("o p k -> p (o k)")).then_inc(ctx_in, 16)
                    sp.dma_start(maskb[:], mask_dram[bass.ds(batch, 1), :, :].rearrange("o (t p) k -> p (o t) k", p=P)).then_inc(mask_in, 16)
                    if last_stage == "D":
                        sp.wait_ge(*finished.done("D"))
                    elif last_stage == "A":
                        sp.wait_ge(*M.emptied("A wo"))
                    elif last_stage == "B":
                        sp.wait_ge(*ffn_added.done("B"))
                    else:
                        sp.wait_ge(*M.emptied("C wo"))
                    sp.dma_start(out_dram[bass.ds(batch, 1), :, :].rearrange("o (t p) d -> p (o t) d", p=P), x[:]).then_inc(x_out, 16)
                    sp.wait_ge(x_out, 16)

                @block.tensor
                def _(pe):
                    def reuse(ring, key):
                        before = ring.reused(key)
                        if before:
                            pe.wait_ge(*before)

                    def turn(key, source, rows=P, cols=P, n=TILES, at=P):
                        reuse(T, key)
                        for i in range(n):
                            last = nc.tensor.transpose(psT[0:cols, T.slot(key), i * at:i * at + rows], source(i),
                                                       ident[0:rows, 0:rows])
                        last.then_inc(T.fill(key), 1)

                    def product(key, terms, rows=P, cols=SEQ):
                        reuse(M, key)
                        for i, (lhsT, rhs) in enumerate(terms):
                            last = nc.tensor.matmul(psM[0:rows, M.slot(key), 0:cols], lhsT, rhs, start=(i == 0),
                                                    stop=(i == len(terms) - 1))
                        last.then_inc(M.fill(key), 1)

                    def tokens(key, terms, cols=P):
                        reuse(M, key)
                        for t in range(TILES):
                            pairs = terms(t)
                            for i, (lhsT, rhs) in enumerate(pairs):
                                last = nc.tensor.matmul(psM[:, M.slot(key), t * cols:(t + 1) * cols], lhsT, rhs,
                                                        start=(i == 0), stop=(i == len(pairs) - 1))
                        last.then_inc(M.fill(key), 1)

                    def tile(buf, t):
                        return buf[:, t * P:(t + 1) * P]

                    pe.wait_ge(consts_in, 16)
                    pe.wait_ge(weights_in[0], 16)
                    pe.wait_ge(ctx_in, 16)
                    nc.tensor.matmul(psM[:, M.slot("A kv"), 0:CTX], w("ak"), ctxT[:], start=True, stop=True)
                    nc.tensor.matmul(psM[0:CTX, M.slot("A kv"), P:2 * P], ctxT[:], w("av"), start=True,
                                     stop=True).then_inc(M.fill("A kv"), 1)
                    pe.wait_ge(*normed.done("A"))
                    turn("A n", lambda t: ntok[:, t])
                    pe.wait_ge(*T.emptied("A n"))
                    product("A q", [(w("aq"), nT[:])])
                    pe.wait_ge(*M.emptied("A q"))
                    for i in range(NA + 2):
                        if i < NA:
                            t, half = divmod(i, 2)
                            reuse(S, ("A", i))
                            for bank in range(2):
                                g = 32 * (2 * half + bank)
                                last = nc.tensor.matmul(
                                    psS[:, S.slot(("A", i)), bank, 0:4 * CTX], QT[g:g + 32, t * P:(t + 1) * P],
                                    kTmA[g:g + 32].rearrange("p j k -> p (j k)"), start=True, stop=True)
                            last.then_inc(S.fill(("A", i)), 1)
                        if 1 <= i <= NA:
                            u = i - 1
                            pe.wait_ge(*exps.done(("A", u)))
                            for j in range(2):
                                turn(("A p", u, j), lambda n: probs[:, unit_index[("A", u)] % 2,
                                                                    (4 * j + n) * CTX:(4 * j + n + 1) * CTX], cols=CTX)
                        if i >= 2:
                            u = i - 2
                            t, half = divmod(u, 2)
                            if half == 0:
                                reuse(M, ("A o", t))
                            for j in range(2):
                                pe.wait_ge(*T.emptied(("A p", u, j)))
                                for n in range(4):
                                    h = 8 * half + 4 * j + n
                                    last = nc.tensor.matmul(
                                        psM[:, M.slot(("A o", t)), h * (HD + 1):(h + 1) * (HD + 1)],
                                        probsT[0:CTX, turned_probs[("A p", u, j)], n * P:(n + 1) * P], vA[:, h, :],
                                        start=True, stop=True)
                            if half == 1:
                                last.then_inc(M.fill(("A o", t)), 1)
                    pe.wait_ge(*M.emptied(("A o", TILES - 1)))
                    turn("A o", lambda t: otok[:, t])
                    pe.wait_ge(*T.emptied("A o"))
                    tokens("A wo", lambda t: [(tile(nT, t), w("ao"))])
                    if last_stage == "A":
                        return

                    for l in range(LAYERS):
                        pe.wait_ge(weights_in[1 + l], 16)
                        if l == 0:
                            pe.wait_ge(*normed.done("B"))
                        else:
                            pe.wait_ge(*M.emptied(("B w2", l - 1)))
                        turn(("B y", l), lambda t: y[:, t])
                        pe.wait_ge(*T.emptied(("B y", l)))
                        wqkv = w(f"qkv{l}")
                        for i in range(TILES + 2):
                            if i < TILES:
                                reuse(S, ("B qk", l, i))
                                for j in range(2):
                                    last = nc.tensor.matmul(psS[:, S.slot(("B qk", l, i)), j, :], tile(hT, i),
                                                            wqkv[:, j * 512:(j + 1) * 512], start=True, stop=True)
                                last.then_inc(S.fill(("B qk", l, i)), 1)
                                product(("B v", l, i), [(tile(hT, i), wqkv[:, 1024:1536])])
                            if i >= 2:
                                t = i - 2
                                pe.wait_ge(*rotated.done((l, t)))
                                for j in range(2):
                                    turn(("B qk", l, t, j), lambda n: qr[:, t % 2, j, n * P:(n + 1) * P])
                        for i in range(TILES + 3):
                            if i < TILES:
                                key = ("B s", l, i)
                                reuse(S, key)
                                pe.wait_ge(*T.emptied(("B qk", l, i, 1)))
                                for pair in range(PAIRS):
                                    for win in range(2):
                                        for half in range(2):
                                            q0 = i * P + win * WIN
                                            last = nc.tensor.matmul(
                                                psS[win * WIN:(win + 1) * WIN, S.slot(key), half, pair * P:(pair + 1) * P],
                                                qT[half * LHD:(half + 1) * LHD, pair, q0:q0 + WIN],
                                                kT[half * LHD:(half + 1) * LHD, pair, q0:q0 + P], start=True, stop=True)
                                last.then_inc(S.fill(key), 1)
                            if 1 <= i <= TILES:
                                t = i - 1
                                pe.wait_ge(*exps.done(("B", l, t)))
                                for half in range(2):
                                    turn(("B p", l, t, half), lambda n: probs[:, unit_index[("B", l, t)] % 2,
                                                                              (4 * half + n) * P:(4 * half + n + 1) * P])
                            if 2 <= i <= TILES + 1:
                                t = i - 2
                                for half in range(2):
                                    key = ("B o", l, t, half)
                                    reuse(M, key)
                                    pe.wait_ge(*T.emptied(("B p", l, t, half)))
                                    for pair in range(PAIRS):
                                        for win, v in enumerate((vmix, vnat)):
                                            last = nc.tensor.matmul(
                                                psM[win * WIN:(win + 1) * WIN, M.slot(key), pair * (LHD + 1):(pair + 1) * (LHD + 1)],
                                                probsT[:, turned_probs[("B p", l, t, half)], pair * P + win * WIN:pair * P + (win + 1) * WIN],
                                                v[:, t, 2 * pair + half, :], start=True, stop=True)
                                    last.then_inc(M.fill(key), 1)
                            if i >= 3:
                                t = i - 3
                                pe.wait_ge(*M.emptied(("B o", l, t, 1)))
                                turn(("B o", l, t), lambda n: o8[:, t % 2, n * P:(n + 1) * P])
                        pe.wait_ge(*T.emptied(("B o", l, TILES - 1)))
                        wo = w(f"bwo{l}").rearrange("p (c d) -> p c d", c=PAIRS)
                        tokens(("B wo", l), lambda t: [(oT[:, n, t * P:(t + 1) * P], wo[:, n, :]) for n in range(PAIRS)])
                        pe.wait_ge(*M.emptied(("B wo", l)))
                        turn(("B y2", l), lambda t: y[:, t])
                        pe.wait_ge(*T.emptied(("B y2", l)))
                        turn(("B tok", l), lambda t: tile(hT, t))
                        pe.wait_ge(*normed.done(("F", l)))
                        turn(("B n", l), lambda t: ntok[:, t])
                        pe.wait_ge(*T.emptied(("B n", l)))
                        w1 = w(f"w1{l}")
                        for i, (h0, hn) in enumerate(CHUNKS):
                            key = ("B w1", l, i)
                            reuse(S, key)
                            for bank, base in enumerate((HID, 0)):
                                last = nc.tensor.matmul(psS[0:hn, S.slot(key), bank, :], w1[:, base + h0:base + h0 + hn],
                                                        nT[:], start=True, stop=True)
                            last.then_inc(S.fill(key), 1)
                        pe.wait_ge(*S.emptied(("B w1", l, 2)))
                        pe.wait_ge(*S.emptied(("B w1", l, 1)))
                        w2 = w(f"w2{l}").rearrange("p (c d) -> p c d", c=3)
                        tokens(("B w2", l), lambda t: [(hid[0:hn, l % 2, n, t * P:(t + 1) * P], w2[0:hn, n, :])
                                                       for n, (_, hn) in enumerate(CHUNKS)])
                    if last_stage == "B":
                        return

                    pe.wait_ge(weights_in[3], 16)
                    reuse(M, "C kv")
                    nc.tensor.matmul(psM[0:CTX, M.slot("C kv"), 0:P], ctxT[:], w("ck"), start=True, stop=True)
                    nc.tensor.matmul(psM[0:CTX, M.slot("C kv"), P:2 * P], ctxT[:], w("cv"), start=True,
                                     stop=True).then_inc(M.fill("C kv"), 1)
                    pe.wait_ge(*M.emptied("C kv"))
                    product("C kf", [(ktok, dft[0:CTX, 0, :])])
                    pe.wait_ge(*normed.done("C"))
                    turn("C n", lambda t: ntok[:, t])
                    pe.wait_ge(*T.emptied("C n"))
                    tokens("C q", lambda t: [(tile(nT, t), w("cq"))])
                    pe.wait_ge(*M.emptied("C q"))
                    product("C qf", [(otok[:, t, :], dft[:, t, :]) for t in range(TILES)])

                    def spectrum(key, plus, minus, cols):
                        reuse(M, key)
                        for i in range(4):
                            f = (i % 2) * P
                            p, second = (p1, plus) if i < 2 else (p2, minus)
                            for n, rhs in enumerate((plus, second)):
                                last = nc.tensor.matmul(psM[:, M.slot(key), i * cols:(i + 1) * cols],
                                                        p[:, n * HALF + f:n * HALF + f + P], rhs, start=(n == 0), stop=(n == 1))
                        last.then_inc(M.fill(key), 1)

                    pe.wait_ge(*spectra.done("C qk"))
                    spectrum("C g", c("ind"), c("nind"), HEADS)
                    pe.wait_ge(*M.emptied("C g"))
                    product("C corr", [(G[:, i, :], idft[:, i, :]) for i in range(4)], rows=HEADS)
                    pe.wait_ge(*selection.done("C"))
                    turn("C w", lambda t: ew[:, t * P:(t + 1) * P], rows=HEADS, at=HEADS)
                    pe.wait_ge(*T.emptied("C w"))
                    product("C wf", [(tile(wx, t), dft[:, t, :]) for t in range(TILES)])
                    product("C vf", [(vtok, dft[0:CTX, 0, :])])
                    pe.wait_ge(*spectra.done("C vw"))
                    spectrum("C of", ident, c("nident"), P)
                    pe.wait_ge(*M.emptied("C of"))
                    product("C out", [(tile(of, i), idft[:, i, :]) for i in range(4)])
                    pe.wait_ge(*M.emptied("C out"))
                    tokens("C wo", lambda t: [(tile(nT, t), w("co"))])
                    if last_stage == "C":
                        return

                    pe.wait_ge(weights_in[4], 16)
                    pe.wait_ge(*normed.done("D1"))
                    turn("D n", lambda t: ntok[:, t])
                    pe.wait_ge(*T.emptied("D n"))
                    product("D q", [(w("dqkv")[:, 0:P], nT[:])])
                    product("D k", [(w("dqkv")[:, P:2 * P], nT[:])])
                    tokens("D v", lambda t: [(tile(nT, t), w("dqkv")[:, 2 * P:3 * P])])
                    pe.wait_ge(*M.emptied("D q"))
                    pe.wait_ge(*M.emptied("D k"))
                    pe.wait_ge(*M.emptied("D v"))
                    for i in range(ND + 2):
                        if i < ND:
                            t, banks = CAUSAL_UNITS[i]
                            wide = (t + 1) * P
                            reuse(S, ("D", i))
                            for n in range(len(banks[0])):
                                for bank in range(2):
                                    h = banks[bank][n]
                                    g = 32 * (h // 4)
                                    last = nc.tensor.matmul(psS[:, S.slot(("D", i)), bank, n * wide:(n + 1) * wide],
                                                            QT[g:g + 32, t * P:(t + 1) * P],
                                                            kTmD[g:g + 32, h % 4, 0:wide], start=True, stop=True)
                            last.then_inc(S.fill(("D", i)), 1)
                        if 1 <= i <= ND:
                            u = i - 1
                            t, banks = CAUSAL_UNITS[u]
                            pe.wait_ge(*exps.done(("D", u)))
                            for j in range(2):
                                turn(("D p", u, j), lambda n: probs[:, unit_index[("D", u)] % 2, j * 512 + n * P:j * 512 + (n + 1) * P],
                                     n=len(banks[j]) * (t + 1))
                        if i >= 2:
                            u = i - 2
                            t, banks = CAUSAL_UNITS[u]
                            if u == 0 or CAUSAL_UNITS[u - 1][0] != t:
                                reuse(M, ("D o", t))
                            for j in range(2):
                                pe.wait_ge(*T.emptied(("D p", u, j)))
                                for n, h in enumerate(banks[j]):
                                    for k in range(t + 1):
                                        at = (n * (t + 1) + k) * P
                                        last = nc.tensor.matmul(
                                            psM[:, M.slot(("D o", t)), h * (HD + 1):(h + 1) * (HD + 1)],
                                            probsT[:, turned_probs[("D p", u, j)], at:at + P], vD[:, k, h, :],
                                            start=(k == 0), stop=(k == t))
                            if u + 1 == ND or CAUSAL_UNITS[u + 1][0] != t:
                                last.then_inc(M.fill(("D o", t)), 1)
                    pe.wait_ge(*M.emptied(("D o", TILES - 1)))
                    turn("D o", lambda t: otok[:, t])
                    pe.wait_ge(*T.emptied("D o"))
                    tokens("D wo", lambda t: [(tile(nT, t), w("dwo"))])
                    pe.wait_ge(*normed.done("D2"))
                    turn("D n2", lambda t: ntok[:, t])
                    pe.wait_ge(*T.emptied("D n2"))
                    tokens("D gate", lambda t: [(tile(nT, t), w("gate"))], cols=EXPERTS)
                    pe.wait_ge(*selection.done("D"))
                    turn("D g", lambda t: gates[:, t, :], cols=EXPERTS)
                    pe.wait_ge(*T.emptied("D g"))
                    tokens("D b2", lambda t: [(gT[:, t * P:(t + 1) * P], w("fc2b", EXPERTS))])
                    pe.wait_ge(weights_in[5], 16)
                    fc1 = w("fc1").rearrange("p (e f) -> p e f", e=EXPERTS)
                    fc2 = w("fc2").rearrange("p (e c d) -> p e c d", e=EXPERTS, c=FC)
                    for e in range(EXPERTS + 1):
                        if e < EXPERTS:
                            for i in range(2):
                                key = ("D f1", e, i)
                                reuse(S, key)
                                for bank in range(2):
                                    n = 2 * i + bank
                                    last = nc.tensor.matmul(psS[:, S.slot(key), bank, :], fc1[:, e, n * P:(n + 1) * P], nT[:],
                                                            start=True, stop=True)
                                last.then_inc(S.fill(key), 1)
                        if e:
                            pe.wait_ge(*S.emptied(("D f1", e - 1, 0)))
                            pe.wait_ge(*S.emptied(("D f1", e - 1, 1)))
                            tokens(("D f2", e - 1), lambda t: [(hid[:, (e - 1) % 2, n, t * P:(t + 1) * P], fc2[:, e - 1, n, :])
                                                               for n in range(FC)])

                @block.scalar
                def _(act):
                    def turned(key):
                        act.wait_ge(*T.filled(key))
                        return psT[:, T.slot(key), :]

                    def shift(key):
                        src = turned(key)
                        nc.scalar.activation(hT[0:64, :], src[0:64, :], ACT.Copy)
                        nc.scalar.activation(hT[64:P, 1:SEQ], src[64:P, 0:SEQ - 1], ACT.Copy).then_inc(T.empty(key), 1)

                    def turned_out(key, rows=P, n=512):
                        src = turned(key)
                        nc.scalar.activation(probsT[0:rows, turned_probs[key], 0:n], src[0:rows, 0:n], ACT.Copy
                                             ).then_inc(T.empty(key), 1)

                    nc.scalar.activation(nT[:], turned("A n"), ACT.Copy).then_inc(T.empty("A n"), 1)
                    for i in range(NA + 1):
                        if i < NA:
                            k = unit_index[("A", i)] % 2
                            act.wait_ge(*centered.done(("A", i)))
                            nc.scalar.activation(probs[:, k, 0:8 * CTX], probs[:, k, 0:8 * CTX], ACT.Exp
                                                 ).then_inc(exps.sem, 1)
                        if i:
                            for j in range(2):
                                turned_out(("A p", i - 1, j), rows=CTX)
                    nc.scalar.activation(nT[:], turned("A o"), ACT.Copy).then_inc(T.empty("A o"), 1)
                    if last_stage == "A":
                        return

                    for l in range(LAYERS):
                        shift(("B y", l))
                        for i in range(TILES + 2):
                            if i < TILES:
                                key = ("B qk", l, i)
                                if l or i:
                                    act.wait_ge(*sums.done(LT[LT.index((l, i)) - 1]))
                                act.wait_ge(*S.filled(key))
                                nc.scalar.activation(sq, psS[:, S.slot(key)], ACT.Square).then_inc(squares.sem, 1)
                                key = ("B v", l, i)
                                act.wait_ge(*M.filled(key))
                                v = psM[:, M.slot(key), :].rearrange("p (h d) -> p h d", h=LHEADS)
                                nc.scalar.activation(vmix[WIN:P, i, :, 0:LHD], v[0:WIN], ACT.Copy)
                                if i + 1 < TILES:
                                    nc.scalar.activation(vmix[0:WIN, i + 1, :, 0:LHD], v[WIN:P], ACT.Copy)
                                nc.scalar.activation(vnat[:, i, :, 0:LHD], v, ACT.Copy).then_inc(M.empty(key), 1)
                            if i >= 2:
                                t = i - 2
                                for j, dst in enumerate((qT[:, :, t * P:(t + 1) * P], kT[:, :, WIN + t * P:WIN + (t + 1) * P])):
                                    key = ("B qk", l, t, j)
                                    src = turned(key).rearrange("p (n k) -> p n k", n=PAIRS)
                                    nc.scalar.activation(dst, src, ACT.Copy).then_inc(T.empty(key), 1)
                        for i in range(TILES + 3):
                            if i < TILES:
                                k = unit_index[("B", l, i)] % 2
                                act.wait_ge(*maxima.done(("B", l, i)))
                                for h in range(LHEADS):
                                    row = probs[:, k, h * P:(h + 1) * P]
                                    last = nc.scalar.activation(row, row, ACT.Exp, bias=nm[:, k, h:h + 1], scale=QK_SCALE)
                                last.then_inc(exps.sem, 1)
                            if 1 <= i <= TILES:
                                for half in range(2):
                                    turned_out(("B p", l, i - 1, half))
                            if i >= 3:
                                t = i - 3
                                key = ("B o", l, t)
                                nc.scalar.activation(oT[:, :, t * P:(t + 1) * P], turned(key).rearrange("p (n k) -> p n k", n=PAIRS),
                                                     ACT.Copy).then_inc(T.empty(key), 1)
                        shift(("B y2", l))
                        key = ("B n", l)
                        nc.scalar.activation(nT[:], turned(key), ACT.Identity, bias=w(f"lnb{l}"), scale=w(f"lng{l}")
                                             ).then_inc(T.empty(key), 1)
                        for i, (_, hn) in enumerate(CHUNKS):
                            key = ("B w1", l, i)
                            if i == 2:
                                act.wait_ge(*S.emptied(("B w1", l, 0)))
                            act.wait_ge(*S.filled(key))
                            nc.scalar.activation(gl[0:hn, i % 2, :], psS[0:hn, S.slot(key), 0, :], ACT.Gelu,
                                                 bias=w(f"b1g{l}")[0:hn, i:i + 1]).then_inc(gelus.sem, 1)
                    if last_stage == "B":
                        return

                    def copied(key, dst, src=None):
                        act.wait_ge(*M.filled(key))
                        nc.scalar.activation(dst, psM[:, M.slot(key), :], ACT.Copy).then_inc(M.empty(key), 1)

                    copied("C kf", wf)
                    nc.scalar.activation(nT[:], turned("C n"), ACT.Copy).then_inc(T.empty("C n"), 1)
                    act.wait_ge(*peak.done("C"))
                    nc.scalar.activation(ew[:], corr[:, 0:SEQ], ACT.Exp, bias=top[:, 16:17]).then_inc(selection_exps.sem, 1)
                    weights_T = turned("C w")[:, 0:TILES * HEADS].rearrange("p (t h) -> p t h", t=TILES)
                    nc.scalar.activation(wx.rearrange("p (t h d) -> p t h d", t=TILES, h=HEADS),
                                         weights_T[:, :, :, None].broadcast_to([P, TILES, HEADS, HD]), ACT.Copy
                                         ).then_inc(T.empty("C w"), 1)
                    copied("C wf", wf)
                    copied("C of", of)
                    copied("C out", nT[:])
                    if last_stage == "C":
                        return

                    nc.scalar.activation(nT[:], turned("D n"), ACT.Identity, bias=w("ln1b"), scale=w("ln1w")
                                         ).then_inc(T.empty("D n"), 1)
                    act.wait_ge(*M.filled("D q"))
                    nc.scalar.activation(QT[:], psM[:, M.slot("D q"), :], ACT.Identity, bias=w("dbq")
                                         ).then_inc(M.empty("D q"), 1)
                    for i in range(ND + 1):
                        if i < ND:
                            t, banks = CAUSAL_UNITS[i]
                            wide = (t + 1) * P
                            k = unit_index[("D", i)] % 2
                            act.wait_ge(*maxima.done(("D", i)))
                            for bank in range(2):
                                for n in range(len(banks[bank])):
                                    row = probs[:, k, bank * 512 + n * wide:bank * 512 + (n + 1) * wide]
                                    col = bank * 4 + n
                                    last = nc.scalar.activation(row, row, ACT.Exp, bias=nm[:, k, col:col + 1], scale=SCALE)
                            last.then_inc(exps.sem, 1)
                        if i:
                            t, banks = CAUSAL_UNITS[i - 1]
                            for j in range(2):
                                turned_out(("D p", i - 1, j), n=len(banks[j]) * (t + 1) * P)
                    nc.scalar.activation(nT[:], turned("D o"), ACT.Copy).then_inc(T.empty("D o"), 1)
                    nc.scalar.activation(nT[:], turned("D n2"), ACT.Identity, bias=w("ln2b"), scale=w("ln2w")
                                         ).then_inc(T.empty("D n2"), 1)
                    act.wait_ge(*peak.done("D"))
                    nc.scalar.activation(gex[:], gex[:], ACT.Exp).then_inc(selection_exps.sem, 1)
                    nc.scalar.activation(gT[:], turned("D g")[0:EXPERTS, :], ACT.Copy).then_inc(T.empty("D g"), 1)
                    fc1b = w("fc1b").rearrange("p (e c) -> p e c", e=EXPERTS)
                    for e in range(EXPERTS):
                        if e >= 2:
                            act.wait_ge(*M.filled(("D f2", e - 2)))
                        for i in range(2):
                            key = ("D f1", e, i)
                            act.wait_ge(*S.filled(key))
                            for bank in range(2):
                                n = 2 * i + bank
                                last = nc.scalar.activation(hid[:, e % 2, n, :], psS[:, S.slot(key), bank, :], ACT.Gelu,
                                                            bias=fc1b[:, e, n:n + 1])
                            last.then_inc(S.empty(key), 1)

                @block.vector
                def _(dve):
                    v = nc.vector
                    chained = [0]

                    def link(instruction):
                        chained[0] += 1
                        instruction.then_inc(dve_chain, 1)
                        dve.wait_ge(dve_chain, chained[0])

                    def layer_norm(key, source, out):
                        for t in range(TILES):
                            last = v.bn_stats(stats[:, t], source(t))
                        link(last)
                        for t in range(TILES):
                            last = v.bn_aggr(mv[:, t], stats[:, t])
                        last.then_inc(stats_ready.sem, 1)
                        dve.wait_ge(*rstd_ready.done(key))
                        for t in range(TILES):
                            last = v.tensor_scalar(out[:, t], source(t), mv[:, t, 0:1], rstd[:, t:t + 1],
                                                   ALU.subtract, ALU.mult)
                        return last

                    def made(key):
                        dve.wait_ge(*M.filled(key))
                        return psM[:, M.slot(key), :]

                    def add_tokens(key, stream):
                        src = made(key).rearrange("p (t d) -> p t d", t=TILES)
                        v.tensor_tensor(stream[:], src, stream[:], ALU.add).then_inc(M.empty(key), 1)

                    def normalize(key, t):
                        src = made(key)[:, 0:HEADS * (HD + 1)].rearrange("p (h d) -> p h d", h=HEADS)
                        link(v.reciprocal(rden[:, t % 2, 0:HEADS], src[:, :, HD]))
                        v.tensor_tensor(otok[:, t, :].rearrange("p (h d) -> p h d", h=HEADS), src[:, :, 0:HD],
                                        rden[:, t % 2, 0:HEADS, None].broadcast_to([P, HEADS, HD]), ALU.mult
                                        ).then_inc(M.empty(key), 1)

                    def probs_free(unit):
                        i = unit_index[unit]
                        if i >= 2:
                            dve.wait_ge(*T.filled(turned_key[UNITS[i - 2]]))
                        return i % 2

                    dve.wait_ge(consts_in, 16)
                    dve.wait_ge(weights_in[0], 16)
                    dve.wait_ge(x_in, 16)
                    layer_norm("A", lambda t: x[:, t], ntok).then_inc(normed.sem, 1)
                    kv = made("A kv")
                    for j in range(4):
                        v.tensor_scalar(kTmA[:, j, :], kv[:, 0:CTX], w("abk"), c("headmask")[:, j:j + 1], ALU.add, ALU.mult)
                    v.tensor_tensor(vA[:, :, 0:HD], kv[0:CTX, P:2 * P].rearrange("p (h d) -> p h d", h=HEADS),
                                    w("abv", CTX).rearrange("p (h d) -> p h d", h=HEADS), ALU.add
                                    ).then_inc(M.empty("A kv"), 1)
                    v.tensor_scalar(QT[:], made("A q"), w("abq"), SCALE, ALU.add, ALU.mult).then_inc(M.empty("A q"), 1)
                    dve.wait_ge(*mask_scaled.done("A"))
                    for i in range(NA + 2):
                        if i < NA:
                            t, key = i // 2, ("A", i)
                            k = probs_free(key)
                            dve.wait_ge(*S.filled(key))
                            out = probs[:, k, 0:8 * CTX]
                            v.tensor_tensor(out.rearrange("p (b j k) -> p b j k", b=2, j=4),
                                            psS[:, S.slot(key), :, 0:4 * CTX].rearrange("p b (j k) -> p b j k", j=4),
                                            maskb[:, t, None, None, :].broadcast_to([P, 2, 4, CTX]), ALU.add
                                            ).then_inc(S.empty(key), 1)
                            dve.wait_ge(*S.emptied(key))
                            v.tensor_reduce(mx[:, k, :], out.rearrange("p (h k) -> p h k", h=8), X_AXIS, ALU.max
                                            ).then_inc(maxima.sem, 1)
                        if i >= 2 and (i - 2) % 2:
                            normalize(("A o", (i - 2) // 2), (i - 2) // 2)
                    dve.wait_ge(*biased.done("A"))
                    add_tokens("A wo", x)
                    if last_stage == "A":
                        return

                    dve.wait_ge(*M.emptied("A wo"))
                    layer_norm("B", lambda t: x[:, t], y).then_inc(normed.sem, 1)
                    for l in range(LAYERS):
                        def head_sums(t):
                            dve.wait_ge(*squares.done((l, t)))
                            v.tensor_reduce(ss[:, t % 2, :], sq.rearrange("p a (h d) -> p (a h) d", d=LHD), X_AXIS, ALU.add
                                            ).then_inc(sums.sem, 1)

                        head_sums(0)
                        for t in range(TILES):
                            if t + 1 < TILES:
                                head_sums(t + 1)
                            key = ("B qk", l, t)
                            dve.wait_ge(*norms.done((l, t)))
                            v.tensor_tensor(qn.rearrange("p a (h d) -> p (a h) d", d=LHD),
                                            psS[:, S.slot(key)].rearrange("p a (h d) -> p (a h) d", d=LHD),
                                            rn[:, t % 2, :, None].broadcast_to([P, 16, LHD]), ALU.mult
                                            ).then_inc(S.empty(key), 1)
                            dve.wait_ge(*S.emptied(key))
                            turned_half = qn.rearrange("p a (h d) -> p a h d", d=LHD)
                            out = t2.rearrange("p a (h d) -> p a h d", d=LHD)
                            for o, i in ((0, 32), (32, 0)):
                                last = v.tensor_tensor(out[:, :, :, o:o + 32], turned_half[:, :, :, i:i + 32],
                                                       rot[l][:, t, :, 1, None, o:o + 32].broadcast_to([P, 2, LHEADS, 32]),
                                                       ALU.mult)
                            link(last)
                            dve.wait_ge(*cos_part.done((l, t)))
                            if t >= 2:
                                dve.wait_ge(*T.filled(("B qk", l, t - 2, 1)))
                            elif l:
                                dve.wait_ge(*T.filled(("B qk", l - 1, t + 2, 1)))
                            v.tensor_tensor(qr[:, t % 2], t1, t2, ALU.add).then_inc(rotated.sem, 1)
                        for i in range(TILES + 2):
                            if i < TILES:
                                key = ("B s", l, i)
                                k = probs_free(("B", l, i))
                                dve.wait_ge(*S.filled(key))
                                mask = c("local")[:, (0 if i == 0 else P):(P if i == 0 else 2 * P)]
                                for half in range(2):
                                    for pair in range(PAIRS):
                                        h = 4 * half + pair
                                        last = v.tensor_tensor_reduce(
                                            probs[:, k, h * P:(h + 1) * P], psS[:, S.slot(key), half, pair * P:(pair + 1) * P], mask,
                                            1.0, SENTINEL, ALU.add, ALU.max, mx[:, k, h:h + 1])
                                last.then_inc(S.empty(key), 1)
                                dve.wait_ge(*S.emptied(key))
                                v.tensor_scalar(nm[:, k, :], mx[:, k, :], -QK_SCALE, None, ALU.mult).then_inc(maxima.sem, 1)
                            if i >= 2:
                                t = i - 2
                                if t >= 2:
                                    dve.wait_ge(*T.filled(("B o", l, t - 2)))
                                for half in range(2):
                                    key = ("B o", l, t, half)
                                    src = made(key)[:, 0:PAIRS * (LHD + 1)].rearrange("p (h d) -> p h d", h=PAIRS)
                                    link(v.reciprocal(rden[:, half, 0:PAIRS], src[:, :, LHD]))
                                    v.tensor_tensor(o8[:, t % 2, :].rearrange("p (n e d) -> p n e d", n=PAIRS, e=2)[:, :, half, :],
                                                    src[:, :, 0:LHD], rden[:, half, 0:PAIRS, None].broadcast_to([P, PAIRS, LHD]),
                                                    ALU.mult).then_inc(M.empty(key), 1)
                        add_tokens(("B wo", l), y)
                        key = ("B tok", l)
                        dve.wait_ge(*T.filled(key))
                        src = psT[:, T.slot(key), :].rearrange("p (t d) -> p t d", t=TILES)
                        last = layer_norm(("F", l), lambda t: src[:, t], ntok)
                        last.then_inc(normed.sem, 1)
                        dve.wait_ge(*normed.done(("F", l)))
                        v.tensor_copy(small[:, 4:5], rstd[:, 0:1]).then_inc(T.empty(key), 1)
                        for i, (_, hn) in enumerate(CHUNKS):
                            key = ("B w1", l, i)
                            dve.wait_ge(*gelus.done((l, i)))
                            v.scalar_tensor_tensor(out=hid[0:hn, l % 2, i, :], in0=psS[0:hn, S.slot(key), 1, :],
                                                   scalar=w(f"b1a{l}")[0:hn, i:i + 1], in1=gl[0:hn, i % 2, :],
                                                   op0=ALU.add, op1=ALU.mult).then_inc(S.empty(key), 1)
                        dve.wait_ge(*biased.done(("B", l)))
                        add_tokens(("B w2", l), y)
                    if last_stage == "B":
                        return

                    kv = made("C kv")
                    v.tensor_tensor(ktok, kv[0:CTX, 0:P], w("cbk", CTX), ALU.add)
                    v.tensor_tensor(vtok, kv[0:CTX, P:2 * P], w("cbv", CTX), ALU.add).then_inc(M.empty("C kv"), 1)
                    dve.wait_ge(*ffn_added.done("B"))
                    layer_norm("C", lambda t: x[:, t], ntok).then_inc(normed.sem, 1)
                    v.tensor_tensor(otok[:], made("C q").rearrange("p (t d) -> p t d", t=TILES),
                                    w("cbq")[:, None, :].broadcast_to([P, TILES, P]), ALU.add).then_inc(M.empty("C q"), 1)

                    def multiply_spectra(key, other):
                        dve.wait_ge(*M.emptied(other))
                        ab = made(key)
                        v.tensor_tensor(p1, ab, wf, ALU.mult)
                        v.tensor_tensor(p2[:, 0:HALF], ab[:, HALF:], wf[:, 0:HALF], ALU.mult)
                        v.tensor_tensor(p2[:, HALF:], ab[:, 0:HALF], wf[:, HALF:], ALU.mult).then_inc(M.empty(key), 1)
                        dve.wait_ge(*M.emptied(key))
                        v.memset(p2[:, HALF:HALF + 1], 0.0)
                        link(v.tensor_copy(p2[:, 0:1], p1[:, HALF:HALF + 1]))
                        v.memset(p1[:, HALF:HALF + 1], 0.0).then_inc(spectra.sem, 1)

                    multiply_spectra("C qf", "C kf")
                    v.tensor_copy(G[:], made("C g")[:, 0:4 * HEADS].rearrange("p (i h) -> p i h", i=4)
                                  ).then_inc(M.empty("C g"), 1)
                    v.tensor_copy(corr[:, 0:SEQ], made("C corr")[0:HEADS, :]).then_inc(M.empty("C corr"), 1)
                    dve.wait_ge(*M.emptied("C corr"))
                    link(v.max(top[:, 0:8], corr[:, 0:SEQ]))
                    v.tensor_scalar(top[:, 16:17], top[:, 0:1], -1.0, None, ALU.mult).then_inc(peak.sem, 1)
                    link(v.tensor_copy(top[:, 8:8 + TOPK], top[:, 0:TOPK]))
                    link(v.match_replace(rep[:], top[:, 8:16], corr[:], REPLACED))
                    link(v.tensor_tensor(rep[:, 0:SEQ], rep[:, 0:SEQ], corr[:, 0:SEQ], ALU.not_equal))
                    dve.wait_ge(*selection_exps.done("C"))
                    link(v.tensor_tensor(ew[:], ew[:], rep[:, 0:SEQ], ALU.mult))
                    link(v.tensor_reduce(top[:, 17:18], ew[:], X_AXIS, ALU.add))
                    link(v.reciprocal(top[:, 18:19], top[:, 17:18]))
                    v.tensor_scalar(ew[:], ew[:], top[:, 18:19], None, ALU.mult).then_inc(selection.sem, 1)
                    multiply_spectra("C vf", "C wf")
                    dve.wait_ge(*biased.done("C"))
                    add_tokens("C wo", x)
                    if last_stage == "C":
                        return

                    dve.wait_ge(*M.emptied("C wo"))
                    layer_norm("D0", lambda t: x[:, t], y).then_inc(normed.sem, 1)
                    dve.wait_ge(*normed.done("D0"))
                    layer_norm("D1", lambda t: y[:, t], ntok).then_inc(normed.sem, 1)
                    dk = made("D k")
                    for j in range(4):
                        last = v.tensor_scalar(kTmD[:, j, :], dk, w("dbk"), c("headmask")[:, j:j + 1], ALU.add, ALU.mult)
                    last.then_inc(M.empty("D k"), 1)
                    v.tensor_tensor(vD[:, :, :, 0:HD], made("D v").rearrange("p (t h d) -> p t h d", t=TILES, h=HEADS),
                                    w("dbv").rearrange("p (h d) -> p h d", h=HEADS)[:, None, :, :].broadcast_to([P, TILES, HEADS, HD]),
                                    ALU.add).then_inc(M.empty("D v"), 1)
                    for i in range(ND + 2):
                        if i < ND:
                            t, banks = CAUSAL_UNITS[i]
                            wide = (t + 1) * P
                            key = ("D", i)
                            k = probs_free(key)
                            dve.wait_ge(*S.filled(key))
                            mask = c("causal")[:, SEQ - wide:SEQ]
                            for bank in range(2):
                                for n in range(len(banks[bank])):
                                    col = bank * 4 + n
                                    last = v.tensor_tensor_reduce(
                                        probs[:, k, bank * 512 + n * wide:bank * 512 + (n + 1) * wide],
                                        psS[:, S.slot(key), bank, n * wide:(n + 1) * wide], mask, 1.0, SENTINEL,
                                        ALU.add, ALU.max, mx[:, k, col:col + 1])
                            last.then_inc(S.empty(key), 1)
                            dve.wait_ge(*S.emptied(key))
                            n = len(banks[0])
                            m = mx[:, k, :].rearrange("p (b n) -> p b n", b=2)[:, :, 0:n]
                            o = nm[:, k, :].rearrange("p (b n) -> p b n", b=2)[:, :, 0:n]
                            v.tensor_scalar(o, m, -SCALE, None, ALU.mult).then_inc(maxima.sem, 1)
                        if i >= 2:
                            t = CAUSAL_UNITS[i - 2][0]
                            if i - 2 + 1 == ND or CAUSAL_UNITS[i - 1][0] != t:
                                normalize(("D o", t), t)
                    dve.wait_ge(*biased.done("D"))
                    add_tokens("D wo", y)
                    dve.wait_ge(*M.emptied("D wo"))
                    layer_norm("D2", lambda t: y[:, t], ntok).then_inc(normed.sem, 1)
                    v.tensor_copy(logit[:, :, 0:8], made("D gate")[:, 0:TILES * EXPERTS].rearrange("p (t e) -> p t e", t=TILES)
                                  ).then_inc(M.empty("D gate"), 1)
                    dve.wait_ge(*M.emptied("D gate"))
                    for t in range(TILES):
                        last = v.max(gtop[:, t, :], logit[:, t, 0:8])
                    link(last)
                    v.tensor_tensor(gex[:], logit[:, :, 0:8], gtop[:, :, 0:1].broadcast_to([P, TILES, 8]), ALU.subtract
                                    ).then_inc(peak.sem, 1)
                    link(v.tensor_copy(gtwo[:, :, 0:2], gtop[:, :, 0:2]))
                    for t in range(TILES):
                        last = v.match_replace(lrep[:, t, :], gtwo[:, t, :], logit[:, t, :], REPLACED)
                    link(last)
                    link(v.tensor_tensor(lrep[:, :, 0:8], lrep[:, :, 0:8], logit[:, :, 0:8], ALU.not_equal))
                    dve.wait_ge(*selection_exps.done("D"))
                    link(v.tensor_tensor(gex[:], gex[:], lrep[:, :, 0:8], ALU.mult))
                    link(v.tensor_reduce(gsum[:], gex[:], X_AXIS, ALU.add))
                    link(v.reciprocal(gsum[:], gsum[:]))
                    v.tensor_tensor(gates[:], gex[:], gsum[:, :, None].broadcast_to([P, TILES, 8]), ALU.mult
                                    ).then_inc(selection.sem, 1)
                    add_tokens("D b2", y)
                    dve.wait_ge(*M.emptied("D b2"))
                    dve.wait_ge(*selection.done("D"))
                    for e in range(EXPERTS):
                        key = ("D f2", e)
                        if e:
                            dve.wait_ge(*M.emptied(("D f2", e - 1)))
                        src = made(key)
                        for t in range(TILES):
                            last = v.scalar_tensor_tensor(out=y[:, t], in0=src[:, t * P:(t + 1) * P], scalar=gates[:, t, e:e + 1],
                                                          in1=y[:, t], op0=ALU.mult, op1=ALU.add)
                        last.then_inc(M.empty(key), 1)
                    dve.wait_ge(*M.emptied(("D f2", EXPERTS - 1)))
                    v.tensor_tensor(x[:], x[:], y[:], ALU.add).then_inc(finished.sem, 1)

                @block.gpsimd
                def _(pool):
                    g = nc.gpsimd
                    chained = [0]

                    def link(instruction):
                        chained[0] += 1
                        instruction.then_inc(pool_chain, 1)
                        pool.wait_ge(pool_chain, chained[0])

                    def rsqrt(key):
                        pool.wait_ge(*stats_ready.done(key))
                        link(g.tensor_scalar(small[:, 0:TILES], mv[:, :, 1], EPS, None, ALU.add))
                        g.tensor_tensor(rstd[:], small[:, 0:TILES], mhalf[:, 0:TILES], ALU.pow).then_inc(rstd_ready.sem, 1)

                    def add_bias(stream, name):
                        g.tensor_tensor(stream[:], stream[:], w(name)[:, None, :].broadcast_to([P, TILES, P]), ALU.add
                                        ).then_inc(biased.sem, 1)

                    pool.wait_ge(set_up, LAYERS)
                    pool.wait_ge(mask_in, 16)
                    g.tensor_scalar(maskb[:], maskb[:], NEG, None, ALU.mult).then_inc(mask_scaled.sem, 1)
                    rsqrt("A")
                    pool.wait_ge(*normed.done("A"))
                    add_bias(x, "abo")
                    for i in range(NA):
                        k = unit_index[("A", i)] % 2
                        pool.wait_ge(*maxima.done(("A", i)))
                        s = probs[:, k, 0:8 * CTX].rearrange("p (h k) -> p h k", h=8)
                        g.tensor_tensor(s, s, mx[:, k, :, None].broadcast_to([P, 8, CTX]), ALU.subtract
                                        ).then_inc(centered.sem, 1)
                    if last_stage == "A":
                        return

                    rsqrt("B")
                    for l in range(LAYERS):
                        def unit_norms(t):
                            pool.wait_ge(*sums.done((l, t)))
                            link(g.tensor_scalar(rn[:, t % 2, :], ss[:, t % 2, :], 1e-24, None, ALU.max))
                            g.tensor_tensor(rn[:, t % 2, :], rn[:, t % 2, :], mhalf[:], ALU.pow).then_inc(norms.sem, 1)

                        unit_norms(0)
                        for t in range(TILES):
                            if t + 1 < TILES:
                                unit_norms(t + 1)
                            pool.wait_ge(*S.emptied(("B qk", l, t)))
                            if l or t:
                                pool.wait_ge(*rotated.done(LT[LT.index((l, t)) - 1]))
                            for j in range(2):
                                last = g.tensor_tensor(t1[:, j, :].rearrange("p (h d) -> p h d", h=LHEADS),
                                                       qn[:, j, :].rearrange("p (h d) -> p h d", h=LHEADS),
                                                       rot[l][:, t, j, 0, None, :].broadcast_to([P, LHEADS, LHD]), ALU.mult)
                            last.then_inc(cos_part.sem, 1)
                        rsqrt(("F", l))
                        pool.wait_ge(*T.filled(("B y2", l)))
                        add_bias(y, f"b2{l}")
                    pool.wait_ge(*M.emptied(("B w2", LAYERS - 1)))
                    g.tensor_tensor(x[:], x[:], y[:], ALU.add).then_inc(ffn_added.sem, 1)
                    if last_stage == "B":
                        return

                    rsqrt("C")
                    pool.wait_ge(*normed.done("C"))
                    add_bias(x, "cbo")
                    if last_stage == "C":
                        return

                    rsqrt("D0")
                    rsqrt("D1")
                    pool.wait_ge(*normed.done("D1"))
                    add_bias(y, "dbo")
                    rsqrt("D2")
            nc.all_engine_barrier()
            first, n = batch_sems[0].num, len(batch_sems)
            assert [s.num for s in batch_sems] == list(range(first, first + n))
            nc.gpsimd.sem_clear(range(first, first + n))
            nc.all_engine_barrier()


def constants():
    import numpy as np
    out = np.zeros((P, CTOTAL), np.float32)

    def put(name, value):
        a, b = CCOL[name]
        out[:, a:b] = np.asarray(value).reshape(P, b - a)

    part = np.arange(P)
    put("ident", np.eye(P))
    put("nident", -np.eye(P))
    put("headmask", (part % 32)[:, None] // HD == np.arange(4)[None, :])
    ind = (part[:, None] // HD == np.arange(HEADS)[None, :]) / HD
    put("ind", ind)
    put("nind", -ind)
    i, j = (part % WIN)[:, None], np.arange(P)[None, :]
    allowed = (i <= j) & (j <= i + WIN)
    first = allowed & ((part >= WIN)[:, None] | (j >= WIN))
    put("local", np.where(np.concatenate([first, allowed], 1), 0.0, -1e37))
    q, k = part[:, None], np.arange(SEQ)[None, :]
    put("causal", np.where(k - (SEQ - P) <= q, 0.0, -1e37))
    half = np.arange(0, LHD, 2, dtype=np.float32)
    inv = (1.0 / np.float32(10000.0) ** (half / LHD)).astype(np.float32)
    pos = np.arange(SEQ, dtype=np.float32)
    freqs = np.tile(pos[:, None] * inv[None, :], (1, 2)).astype(np.float32)
    base = (half + 0.4 * LHD) / (1.4 * LHD)
    scale = np.tile(base[None, :] ** ((pos - SEQ // 2) / (WIN // 2))[:, None], (1, 2)).astype(np.float64)
    cos, sin = np.cos(freqs.astype(np.float64)), np.sin(freqs.astype(np.float64))
    sin[:, :LHD // 2] *= -1
    rot = np.stack([np.stack([cos * scale, sin * scale], 1), np.stack([cos / scale, sin / scale], 1)], 1)
    put("rot", rot.reshape(TILES, P, 2, 2, LHD).transpose(1, 0, 2, 3, 4))
    n = np.arange(SEQ)[:, None]
    f = np.arange(HALF)[None, :]
    angle = 2 * np.pi * ((n * f) % SEQ) / SEQ
    cosines, sines = np.cos(angle), np.sin(angle)
    sines[:, 0] = (-1.0) ** n[:, 0]
    table = np.concatenate([cosines, sines], 1)
    put("dft", table.reshape(TILES, P, SEQ).transpose(1, 0, 2))
    weight = np.full((SEQ, 1), 2.0 / SEQ)
    weight[0] = weight[HALF] = 1.0 / SEQ
    put("idft", (table.T * weight).reshape(TILES, P, SEQ).transpose(1, 0, 2))
    return out


def pack_weights(a):
    import numpy as np
    out = np.zeros((P, WTOTAL), np.float32)

    def put(name, value, rows=P):
        lo, hi = WCOL[name]
        out[:rows, lo:hi] = np.asarray(value).reshape(rows, hi - lo)

    def row(v):
        return np.broadcast_to(np.asarray(v)[None, :], (P, len(v)))

    for s, k in (("a", "L0_xattn_"), ("c", "L1_xattn_")):
        for n in "qkvo":
            put(s + n, a[f"{k}W{n}"])
    put("abq", a["L0_xattn_bq"])
    put("abk", a["L0_xattn_bk"])
    put("abv", row(a["L0_xattn_bv"]))
    put("abo", row(a["L0_xattn_bo"]))
    for n in "qkvo":
        put("cb" + n, row(a[f"L1_xattn_b{n}"]))
    f = {k[len("L0_ffn_"):]: np.asarray(v) for k, v in a.items() if k.startswith("L0_ffn_")}
    for l in range(LAYERS):
        put(f"qkv{l}", f["wqkv"][l])
        put(f"qs{l}", row(f["q_scale"][l]))
        put(f"ks{l}", row(f["k_scale"][l]))
        put(f"bwo{l}", f["wo"][l].reshape(PAIRS, P, P).transpose(1, 0, 2))
        put(f"lng{l}", f["ln_g"][l])
        put(f"lnb{l}", f["ln_b"][l])
        put(f"w1{l}", f["w1"][l])
        for i, (h0, hn) in enumerate(CHUNKS):
            out[:hn, WCOL[f"b1a{l}"][0] + i] = f["b1"][l][h0:h0 + hn]
            out[:hn, WCOL[f"b1g{l}"][0] + i] = f["b1"][l][HID + h0:HID + h0 + hn]
            lo = WCOL[f"w2{l}"][0] + i * P
            out[:hn, lo:lo + P] = f["w2"][l][h0:h0 + hn]
        put(f"b2{l}", row(f["b2"][l]))
    d = {k[len("L1_ffn_"):]: np.asarray(v) for k, v in a.items() if k.startswith("L1_ffn_")}
    put("ln1w", d["ln1_w"])
    put("ln1b", d["ln1_b"])
    put("ln2w", d["ln2_w"])
    put("ln2b", d["ln2_b"])
    put("dqkv", d["Wqkv"])
    put("dbq", d["bqkv"][0:P])
    put("dbk", d["bqkv"][P:2 * P])
    put("dbv", row(d["bqkv"][2 * P:]))
    put("dwo", d["Wo"])
    put("dbo", row(d["bo"]))
    put("gate", d["gate_W"])
    put("fc2b", d["fc2_b"], EXPERTS)
    put("fc1b", d["fc1_b"].reshape(EXPERTS, FC, P).transpose(2, 0, 1))
    put("fc1", d["fc1_w"].transpose(2, 0, 1))
    put("fc2", d["fc2_w"].reshape(EXPERTS, P, FC, P).transpose(3, 0, 2, 1))
    return out


def kernel(**inputs):
    import numpy as np
    import concourse.bacc as bacc
    from concourse.bass_utils import run_bass_kernel_spmd

    nc = bacc.Bacc("TRN2", target_bir_lowering=False, num_devices=1)
    arrays = {
        "x_in": np.ascontiguousarray(inputs["x"]),
        "ctxT_in": np.ascontiguousarray(np.asarray(inputs["ctx_1024"]).transpose(0, 2, 1)),
        "mask_in": np.ascontiguousarray(np.asarray(inputs["mask_Bx1xSxS2_fk0"])[:, 0]),
        "weights": pack_weights(inputs),
        "constants": constants(),
    }
    args = [nc.dram_tensor(n, v.shape, F32, kind="ExternalInput").ap() for n, v in arrays.items()]
    args.append(nc.dram_tensor("x_result", (BATCH, SEQ, P), F32, kind="ExternalOutput").ap())
    program(nc, *args)
    r = run_bass_kernel_spmd(nc, [arrays], core_ids=[0])
    return r.results[0]["x_result"]
```

```python
from contextlib import ExitStack

import concourse.bass as bass
from concourse import mybir
from concourse.alu_op_type import AluOpType as ALU

F32 = mybir.dt.float32
ACT = mybir.ActivationFunctionType
X_AXIS = mybir.AxisListType.X

P = 128
BATCH, SEQ, CTX = 4, 512, 77
STREAMS = 2
LAG = 0
TILES = SEQ // P
HEADS, HD = 16, 8
LAYERS, LHEADS, LHD, WIN = 2, 8, 64, 64
PAIRS = LHEADS // 2
VN = 96
VW = (LHEADS - 1) * (LHD + 1) + VN + 1
HID = 341
EXPERTS, FFN = 8, 512
FC = FFN // P
EXPERT_SLOTS = 4
TOPK = 6
HALF = SEQ // 2
SCALE = float(HD) ** -0.5
QK_SCALE = 8.0
EPS = 1e-5
NEG = -1e15
SENTINEL = -3.0e38
REPLACED = -3.3e38

WEIGHTS = (
    [("aq", P), ("ak", P), ("av", P), ("ao", 4 * P), ("abq", 1), ("abk", 1), ("abv", P), ("abo", P)]
    + [(f"{n}{l}", LHD) for l in range(LAYERS) for n in ("qs", "ks")]
    + [("cq", P), ("ck", P), ("cv", P), ("co", P), ("cbq", P), ("cbk", P), ("cbv", P), ("cbo", P)]
    + [(f"{n}{l}", c) for l in range(LAYERS) for n, c in (
        ("qkv", 3 * 512), ("bwo", PAIRS * P), ("lng", 1), ("lnb", 1),
        ("w1", 2 * 3 * P), ("b1a", 3), ("b1g", 3), ("w2", 3 * P), ("b2", P))]
    + [("ln1w", 1), ("ln1b", 1), ("ln2w", 1), ("ln2b", 1), ("dqkv", 3 * P), ("dbq", 1), ("dbk", 1), ("dbv", P),
       ("dwo", 4 * P), ("dbo", P), ("gate", EXPERTS), ("fc2b", P), ("fc1b", EXPERTS * FC)])
CONSTS = [("ident", P), ("nident", P), ("headmask", HEADS), ("ind", HEADS), ("nind", HEADS), ("local", 2 * P),
          ("causal", SEQ), ("rot", TILES * 2 * 2 * LHD), ("dft", TILES * SEQ), ("idft", TILES * SEQ)]


def columns(parts):
    at, out = 0, {}
    for name, n in parts:
        out[name] = (at, at + n)
        at += n
    return out, at


WCOL, WTOTAL = columns(WEIGHTS)
CCOL, CTOTAL = columns(CONSTS)
STAY = WCOL["qkv0"][0]
LAYER_COLS = WCOL["qkv1"][0] - STAY
PLACES = [max(LAYER_COLS, 2 * TILES * SEQ, EXPERT_SLOTS * 2 * FFN), max(LAYER_COLS, WTOTAL - WCOL["ln1w"][0])]

CAUSAL_UNITS = [(t, list(range(h, h + n))) for t, n in enumerate((4, 2, 1, 1)) for h in range(0, HEADS, n)]
LAST_UNIT = [max(u for u, (t, _) in enumerate(CAUSAL_UNITS) if t == tile) for tile in range(TILES)]


class Ring:

    def __init__(self, sem, name, banks):
        self.banks = banks
        self.full = [sem(f"{name}_full{i}") for i in range(len(banks))]
        self.free = [sem(f"{name}_free{i}") for i in range(len(banks))]
        self.at = {}

    def reused(self):
        s, n = len(self.at) % len(self.banks), len(self.at) // len(self.banks)
        return (self.free[s], n) if n else None

    def take(self, key):
        assert key not in self.at, key
        i = len(self.at)
        self.at[key] = (i % len(self.banks), i // len(self.banks))
        return self.bank(key)

    def bank(self, key):
        return self.banks[self.at[key][0]]

    def filled(self, key):
        s, n = self.at[key]
        return self.full[s], n + 1

    def emptied(self, key):
        s, n = self.at[key]
        return self.free[s], n + 1

    def fill(self, key):
        return self.full[self.at[key][0]]

    def empty(self, key):
        return self.free[self.at[key][0]]


class Marks:

    def __init__(self, sem, name, keys):
        self.sem = sem(name)
        self.n = {k: i + 1 for i, k in enumerate(keys)}

    def done(self, key):
        return self.sem, self.n[key]


NA, ND = 4 * TILES, len(CAUSAL_UNITS)


class Stream:

    def __init__(self, index, sem, sb, psum):
        self.index = index
        s = f"_{index}"
        self.x = sb("x" + s, [P, TILES, P])
        self.y = sb("y" + s, [P, TILES, P])
        self.ctxT = sb("ctxT" + s, [P, CTX])
        self.maskb = sb("maskb" + s, [P, TILES, CTX])
        normal = sb("normal" + s, [P, 2, 512])
        self.ntok = normal[:, 0, :].rearrange("p (t d) -> p t d", t=TILES)
        self.nT = normal[:, 1, :]
        self.hT = sb("hT" + s, [P, SEQ])
        self.QT = sb("QT" + s, [P, SEQ])
        self.probs = sb("probs" + s, [P, 2, 512])
        self.probsT = sb("probsT" + s, [P, 2, 512])
        region = sb("region" + s, [P, REGION])

        def part(at, *shape, rows=P):
            n = 1
            for d in shape:
                n *= d
            assert at + n <= REGION
            flat = region[0:rows, at:at + n]
            if len(shape) == 1:
                return flat
            if len(shape) == 2:
                return flat.rearrange("p (a b) -> p a b", a=shape[0])
            return flat.rearrange("p (a b c) -> p a b c", a=shape[0], b=shape[1])

        self.kTmA = part(0, HEADS, CTX)
        self.kA = part(1280, CTX)
        self.vA = part(1408, HEADS, 32)
        self.kTmD = part(0, HEADS, SEQ)
        self.vD = part(HEADS * SEQ, TILES, HEADS, 32)
        self.kD = self.nT_free = normal[:, 0, :]
        self.recip = normal[:, 0, :]
        self.oP = self.hT[:].rearrange("p (j q) -> p j q", j=4)
        kz, qz, vz = LHEADS * (WIN + SEQ), PAIRS * SEQ, TILES * VW
        self.kTz = part(0, LHEADS, WIN + SEQ)
        self.qT = part(kz, PAIRS, SEQ)
        self.oT = self.qT
        self.hidB = part(kz, 3, SEQ)
        self.vnat = part(kz + qz, TILES, VW)
        self.vmix = part(kz + qz + vz, TILES, VW)
        n = LHEADS * (LHD + 1)
        self.vnat_heads = self.vnat[:, :, 0:n].rearrange("p t (h d) -> p t h d", h=LHEADS)
        self.vmix_heads = self.vmix[:, :, 0:n].rearrange("p t (h d) -> p t h d", h=LHEADS)
        self.sq = self.probsT[:]
        self.t1 = self.probs[:]
        self.qn = sb("qn" + s, [P, 2, 512])[:]
        self.t2 = normal[:]
        self.o8 = normal[:, 0, :]
        self.gl = self.probs[:]
        self.p1, self.p2, self.wf, self.wx, self.of = (part(512 * i, 512) for i in range(5))
        self.kvtok = part(2560, 2 * P)
        self.ktok, self.vtok = part(2560, P), part(2560 + P, P)
        self.corr = sb("corr" + s, [HEADS, SEQ + 2])
        self.rep = sb("rep" + s, [HEADS, SEQ + 2])
        self.ew = sb("ew" + s, [HEADS, SEQ])
        self.G = sb("G" + s, [P, 4, HEADS])
        self.top = sb("top" + s, [HEADS, 24])
        self.hid = region[:, 0:2 * FC * SEQ].rearrange("p (a c n) -> p a c n", a=2, c=FC)
        self.logit = sb("logit" + s, [P, TILES, 16])
        self.lrep = sb("lrep" + s, [P, TILES, 16])
        self.gtop = sb("gtop" + s, [P, TILES, 8])
        self.gtwo = sb("gtwo" + s, [P, TILES, 8])
        self.gex = sb("gex" + s, [P, TILES, 8])
        self.gsum = sb("gsum" + s, [P, TILES])
        self.gates = sb("gates" + s, [P, TILES, 8])
        self.gT = self.QT[0:EXPERTS, :]
        self.stats = sb("stats" + s, [P, TILES, 6])
        self.mv = sb("mv" + s, [P, TILES, 2])
        self.small = sb("small" + s, [P, 8])
        self.rstd = sb("rstd" + s, [P, TILES])
        self.ss = sb("ss" + s, [P, 2, 16])
        self.rn = sb("rn" + s, [P, 2, 16])
        self.mx = sb("mx" + s, [P, 2, 4])
        self.nm = sb("nm" + s, [P, 2, 4])
        self.rden = sb("rden" + s, [P, 2, 4])

        self.S = Ring(sem, "scores" + s, [psum(f"psS{s}_{i}")[:] for i in range(2)])
        self.T = Ring(sem, "turned" + s, [psum("psT" + s)[:]])
        self.M = Ring(sem, "products" + s, [psum("psM" + s)[:]])

        LT = [(l, t) for l in range(LAYERS) for t in range(TILES)]
        LNS = ["A", "B", ("F", 0), ("F", 1), "C", "D0", "D1", "D2"]
        UNITS = [("A", u) for u in range(NA)] + [("B", l, u) for l in range(LAYERS) for u in range(2 * TILES)] \
            + [("D", u) for u in range(ND)]

        def marks(name, keys):
            return Marks(sem, name + s, keys)

        self.stats_ready = marks("stats_ready", LNS)
        self.rstd_ready = marks("rstd_ready", LNS)
        self.normed = marks("normed", LNS)
        self.maxima = marks("maxima", UNITS)
        self.centered = marks("centered", [("A", u) for u in range(NA)])
        self.exps = marks("exps", UNITS)
        self.attended = marks("attended", [(k, t) for k in "AD" for t in range(TILES)])
        self.prepared = marks("prepared", ["A kv", "D k"])
        self.masked_keys = marks("masked_keys", ["D"])
        self.cleared = marks("cleared", ["B", "D"])
        self.ones = marks("ones", ["B"])
        self.squares = marks("squares", [(l, t, j) for l, t in LT for j in range(2)])
        self.sums = marks("sums", LT)
        self.norms = marks("norms", LT)
        self.cos_part = marks("cos_part", LT)
        self.rotated = marks("rotated", LT)
        self.biased = marks("biased", ["A", ("B", 0), ("B", 1), "C", "D"])
        self.ffn_added = marks("ffn_added", ["B"])
        self.spectra = marks("spectra", ["C qk", "C vw"])
        self.peak = marks("peak", ["C", "D"])
        self.selection_exps = marks("selection_exps", ["C", "D"])
        self.selection = marks("selection", ["C", "D"])
        self.finished = marks("finished", ["D"])
        self.mask_scaled = marks("mask_scaled", ["A"])
        self.x_in = sem("x_in" + s)
        self.ctx_in = sem("ctx_in" + s)
        self.mask_in = sem("mask_in" + s)
        self.x_out = sem("x_out" + s)


REGION = LHEADS * (WIN + SEQ) + PAIRS * SEQ + 2 * TILES * VW
steps_seen = {}


def program(nc, x_dram, ctxT_dram, mask_dram, weights_dram, experts_dram, consts_dram, out_dram, last_stage="D"):
    with ExitStack() as stack:
        sems = []

        def sem(name):
            s = stack.enter_context(nc.semaphore(name))
            sems.append(s)
            return s

        def sb(name, shape):
            return stack.enter_context(nc.sbuf_tensor(name, shape, F32))

        def psum(name):
            return stack.enter_context(nc.psum_tensor(name, [P, 512], F32))

        wt = sb("wt", [P, STAY])
        cs = sb("cs", [P, CCOL["dft"][0]])
        place = [sb(f"place{i}", [P, n]) for i, n in enumerate(PLACES)]
        mhalf = sb("mhalf", [P, 16])

        def w(name, rows=P):
            a, b = WCOL[name]
            for first, buffer in ((WCOL["ln1w"][0], place[1]), (WCOL["qkv1"][0], place[1]), (STAY, place[0]), (0, wt)):
                if a >= first:
                    return buffer[0:rows, a - first:b - first]

        def c(name, rows=P):
            a, b = CCOL[name]
            return cs[0:rows, a:b]

        ident = c("ident")
        dft, idft = (place[0][:, i * TILES * SEQ:(i + 1) * TILES * SEQ].rearrange("p (t f) -> p t f", t=TILES) for i in range(2))
        experts = place[0][:, 0:EXPERT_SLOTS * 2 * FFN].rearrange("p (s n) -> p s n", s=EXPERT_SLOTS)
        rot_base = c("rot").rearrange("p (t q a d) -> p t q a d", t=TILES, q=2, a=2)
        rot = [sb("rot", [P, TILES, 2, 2, LHD])[:], rot_base]
        streams = [Stream(i, sem, sb, psum) for i in range(STREAMS)]
        dve_chain = sem("dve_chain")
        pool_chain = sem("pool_chain")
        expert_in = [sem(f"expert_in{i}") for i in range(EXPERT_SLOTS)]
        layer_in = [sem(f"layer_in{l}") for l in range(LAYERS)]
        fourier_in = sem("fourier_in")
        causal_in = sem("causal_in")
        batch_sems = list(sems)

        weights_in = sem("weights_in")
        consts_in = sem("consts_in")
        set_up = sem("set_up")

        def alternate(engine, stream_program):
            lanes = [stream_program(st) for st in streams]
            names = [[] for _ in streams]
            at = 0
            while any(lane is not None for lane in lanes):
                for i in range(STREAMS):
                    if lanes[i] is None or at < i * LAG:
                        continue
                    try:
                        names[i].append(next(lanes[i]))
                    except StopIteration:
                        lanes[i] = None
                at += 1
            assert steps_seen.setdefault("steps", names[0]) == names[0] == names[1], engine

        with nc.Block() as block:
            @block.sync
            def _(sp):
                sp.dma_start(cs[:], consts_dram[:, 0:CCOL["dft"][0]]).then_inc(consts_in, 16)
                sp.dma_start(wt[:], weights_dram[:, 0:STAY]).then_inc(weights_in, 16)

            @block.vector
            def _(dve):
                v = nc.vector
                v.memset(mhalf[:], -0.5)
                for st in streams:
                    v.memset(st.kTz.rearrange("p a b -> p (a b)")[:, 0:1], 0.0)
                    v.memset(st.vnat.rearrange("p a b -> p (a b)"), 0.0)
                    v.memset(st.vmix.rearrange("p a b -> p (a b)"), 0.0)
                    v.memset(st.probsT[:], 0.0)
                    v.memset(st.small[:], 0.0)
                    v.memset(st.corr[:, SEQ:SEQ + 2], SENTINEL)
                    v.memset(st.top[:, 8 + TOPK:16], SENTINEL)
                    v.memset(st.logit[:, :, 8:16], SENTINEL)
                    v.memset(st.gtwo[:, :, 2:8], SENTINEL)

            @block.gpsimd
            def _(pool):
                g = nc.gpsimd
                pool.wait_ge(consts_in, 16)
                pool.wait_ge(weights_in, 16)
                for l in range(LAYERS):
                    for j, name in enumerate(("qs", "ks")):
                        s = w(f"{name}{l}")
                        g.tensor_tensor(rot[l][:, :, j, 0, :], rot_base[:, :, j, 0, :],
                                        s[:, None, :].broadcast_to([P, TILES, LHD]), ALU.mult)
                        for o, i in ((0, 32), (32, 0)):
                            last = g.tensor_tensor(rot[l][:, :, j, 1, o:o + 32], rot_base[:, :, j, 1, o:o + 32],
                                                   s[:, None, i:i + 32].broadcast_to([P, TILES, 32]), ALU.mult)
                    last.then_inc(set_up, 1)
                    pool.wait_ge(set_up, l + 1)

        with nc.Fori(0, BATCH // STREAMS) as round_no:
            with nc.Block() as block:
                @block.tensor
                def _(pe):
                    def reuse(ring):
                        before = ring.reused()
                        if before:
                            pe.wait_ge(*before)

                    def turn(st, key, source, rows=P, cols=P, n=TILES, at=P):
                        reuse(st.T)
                        bank = st.T.take(key)
                        for i in range(n):
                            last = nc.tensor.transpose(bank[0:cols, i * at:i * at + rows], source(i), ident[0:rows, 0:rows])
                        last.then_inc(st.T.fill(key), 1)

                    def product(st, key, terms, rows=P, cols=SEQ, ring=None):
                        ring = ring or st.M
                        reuse(ring)
                        bank = ring.take(key)
                        for i, (lhsT, rhs) in enumerate(terms):
                            last = nc.tensor.matmul(bank[0:rows, 0:cols], lhsT, rhs, start=(i == 0), stop=(i == len(terms) - 1))
                        last.then_inc(ring.fill(key), 1)

                    def tokens(st, key, terms, cols=P):
                        reuse(st.M)
                        bank = st.M.take(key)
                        for t in range(TILES):
                            pairs = terms(t)
                            for i, (lhsT, rhs) in enumerate(pairs):
                                last = nc.tensor.matmul(bank[:, t * cols:(t + 1) * cols], lhsT, rhs,
                                                        start=(i == 0), stop=(i == len(pairs) - 1))
                        last.then_inc(st.M.fill(key), 1)

                    def tile(buf, t):
                        return buf[:, t * P:(t + 1) * P]

                    def stream_program(st):
                        S, T, M, x, y, ntok, nT, hT = st.S, st.T, st.M, st.x, st.y, st.ntok, st.nT, st.hT
                        pe.wait_ge(consts_in, 16)
                        pe.wait_ge(weights_in, 16)
                        pe.wait_ge(st.ctx_in, 16)
                        bank = M.take("A kv")
                        nc.tensor.matmul(bank[:, 0:CTX], w("ak"), st.ctxT[:], start=True, stop=True)
                        nc.tensor.matmul(bank[0:CTX, P:2 * P], st.ctxT[:], w("av"), start=True,
                                         stop=True).then_inc(M.fill("A kv"), 1)
                        pe.wait_ge(*st.normed.done("A"))
                        turn(st, "A n", lambda t: ntok[:, t])
                        yield "A n"
                        pe.wait_ge(*T.emptied("A n"))
                        product(st, "A q", [(w("aq"), nT[:])])
                        yield "A q"
                        pe.wait_ge(*M.emptied("A q"))
                        pe.wait_ge(*st.prepared.done("A kv"))
                        wo = w("ao").rearrange("p (j d) -> p j d", j=4)
                        for i in range(NA + 4):
                            if i < NA:
                                t, g = divmod(i, 4)
                                product(st, ("A s", i), [(tile(st.QT, t), st.kTmA[:, 4 * g:4 * g + 4, :].rearrange("p h k -> p (h k)"))],
                                        cols=4 * CTX, ring=S)
                            if 1 <= i <= NA:
                                u = i - 1
                                pe.wait_ge(*st.exps.done(("A", u)))
                                turn(st, ("A p", u), lambda n: st.probs[:, u % 2, n * CTX:(n + 1) * CTX], cols=CTX)
                            if 2 <= i <= NA + 1:
                                t, g = divmod(i - 2, 4)
                                if g == 0:
                                    reuse(M)
                                    bank = M.take(("A o", t))
                                pe.wait_ge(*T.emptied(("A p", i - 2)))
                                for n in range(4):
                                    last = nc.tensor.matmul(bank[32 * n:32 * n + 32, g * P:(g + 1) * P], st.vA[:, 4 * g + n, :],
                                                            st.probsT[:, i % 2, n * P:(n + 1) * P], start=True, stop=True)
                                if g == 3:
                                    last.then_inc(M.fill(("A o", t)), 1)
                            if i >= 4 and i % 4 == 3:
                                t = (i - 4) // 4
                                pe.wait_ge(*st.attended.done(("A", t)))
                                product(st, ("A wo", t), [(st.oP[:, j, :], wo[:, j, :]) for j in range(4)], cols=P, ring=T)
                            yield ("A", i)
                        if last_stage == "A":
                            return

                        for l in range(LAYERS):
                            pe.wait_ge(layer_in[l], 16)
                            if l == 0:
                                pe.wait_ge(*st.normed.done("B"))
                            else:
                                pe.wait_ge(*M.emptied(("B w2", l - 1)))
                            turn(st, ("B y", l), lambda t: y[:, t])
                            yield ("B y", l)
                            pe.wait_ge(*T.emptied(("B y", l)))
                            wqkv = w(f"qkv{l}")
                            for i in range(TILES + 2):
                                if i < TILES:
                                    product(st, ("B q", l, i), [(tile(hT, i), wqkv[:, 0:512])], ring=S)
                                    product(st, ("B k", l, i), [(tile(hT, i), wqkv[:, 512:1024])], ring=S)
                                    product(st, ("B v", l, i), [(tile(hT, i), wqkv[:, 1024:1536])])
                                if i >= 1 and i <= TILES:
                                    t = i - 1
                                    pe.wait_ge(*st.rotated.done((l, t)))
                                    for j in range(2):
                                        turn(st, ("B qk", l, t, j), lambda n: st.t1[:, j, n * P:(n + 1) * P])
                                yield ("B qk", l, i)
                            for i in range(2 * TILES + 3):
                                if i < 2 * TILES:
                                    t, half = divmod(i, 2)
                                    key = ("B s", l, i)
                                    reuse(S)
                                    bank = S.take(key)
                                    pe.wait_ge(*T.emptied(("B qk", l, t, 1)))
                                    for n in range(4):
                                        h = 4 * half + n
                                        for win in range(2):
                                            q0 = t * P + win * WIN
                                            last = nc.tensor.matmul(
                                                bank[win * WIN:(win + 1) * WIN, n * P:(n + 1) * P],
                                                st.qT[:, h // 2, q0:q0 + WIN], st.kTz[:, h, q0:q0 + P], start=True, stop=True)
                                    last.then_inc(S.fill(key), 1)
                                if 1 <= i <= 2 * TILES:
                                    u = i - 1
                                    pe.wait_ge(*st.exps.done(("B", l, u)))
                                    turn(st, ("B p", l, u), lambda n: st.probs[:, u % 2, n * P:(n + 1) * P])
                                if 2 <= i <= 2 * TILES + 1:
                                    u = i - 2
                                    t, half = divmod(u, 2)
                                    key = ("B o", l, u)
                                    reuse(M)
                                    bank = M.take(key)
                                    pe.wait_ge(*T.emptied(("B p", l, u)))
                                    for n in range(4):
                                        h = 4 * half + n
                                        for win, v in enumerate((st.vmix, st.vnat)):
                                            last = nc.tensor.matmul(
                                                bank[win * WIN:(win + 1) * WIN, n * VN:(n + 1) * VN],
                                                st.probsT[:, u % 2, n * P + win * WIN:n * P + (win + 1) * WIN],
                                                v[:, t, h * (LHD + 1):h * (LHD + 1) + VN], start=True, stop=True)
                                    last.then_inc(M.fill(key), 1)
                                if i >= 4 and i % 2 == 0:
                                    t = (i - 4) // 2
                                    pe.wait_ge(*M.emptied(("B o", l, 2 * t + 1)))
                                    turn(st, ("B o", l, t), lambda n: st.o8[:, n * P:(n + 1) * P])
                                yield ("B s", l, i)
                            pe.wait_ge(*T.emptied(("B o", l, TILES - 1)))
                            wo_l = w(f"bwo{l}").rearrange("p (c d) -> p c d", c=PAIRS)
                            tokens(st, ("B wo", l), lambda t: [(st.oT[:, n, t * P:(t + 1) * P], wo_l[:, n, :]) for n in range(PAIRS)])
                            yield ("B wo", l)
                            pe.wait_ge(*M.emptied(("B wo", l)))
                            turn(st, ("B y2", l), lambda t: y[:, t])
                            yield ("B y2", l)
                            pe.wait_ge(*T.emptied(("B y2", l)))
                            turn(st, ("B tok", l), lambda t: tile(hT, t))
                            yield ("B tok", l)
                            pe.wait_ge(*st.normed.done(("F", l)))
                            turn(st, ("B n", l), lambda t: ntok[:, t])
                            yield ("B n", l)
                            pe.wait_ge(*T.emptied(("B n", l)))
                            w1 = w(f"w1{l}").rearrange("p (a c) -> p a c", a=2)
                            for i in range(3):
                                for a in (1, 0):
                                    product(st, ("B w1", l, i, a), [(w1[:, a, i * P:(i + 1) * P], nT[:])], ring=S)
                                yield ("B w1", l, i)
                            for i in range(3):
                                pe.wait_ge(*S.emptied(("B w1", l, i, 0)))
                            w2 = w(f"w2{l}").rearrange("p (c d) -> p c d", c=3)
                            tokens(st, ("B w2", l), lambda t: [(st.hidB[:, n, t * P:(t + 1) * P], w2[:, n, :]) for n in range(3)])
                            yield ("B w2", l)
                        if last_stage == "B":
                            return

                        pe.wait_ge(fourier_in, 16)
                        reuse(M)
                        bank = M.take("C kv")
                        nc.tensor.matmul(bank[0:CTX, 0:P], st.ctxT[:], w("ck"), start=True, stop=True)
                        nc.tensor.matmul(bank[0:CTX, P:2 * P], st.ctxT[:], w("cv"), start=True, stop=True).then_inc(M.fill("C kv"), 1)
                        yield "C kv"
                        pe.wait_ge(*M.emptied("C kv"))
                        product(st, "C kf", [(st.ktok, dft[:, 0, :])])
                        yield "C kf"
                        pe.wait_ge(*st.normed.done("C"))
                        turn(st, "C n", lambda t: ntok[:, t])
                        yield "C n"
                        pe.wait_ge(*T.emptied("C n"))
                        tokens(st, "C q", lambda t: [(tile(nT, t), w("cq"))])
                        yield "C q"
                        pe.wait_ge(*M.emptied("C q"))
                        product(st, "C qf", [(tile(hT, t), dft[:, t, :]) for t in range(TILES)])
                        yield "C qf"

                        def spectrum(key, plus, minus, cols):
                            reuse(M)
                            bank = M.take(key)
                            for i in range(4):
                                f = (i % 2) * P
                                p, second = (st.p1, plus) if i < 2 else (st.p2, minus)
                                for n, rhs in enumerate((plus, second)):
                                    last = nc.tensor.matmul(bank[:, i * cols:(i + 1) * cols], p[:, n * HALF + f:n * HALF + f + P],
                                                            rhs, start=(n == 0), stop=(n == 1))
                            last.then_inc(M.fill(key), 1)

                        pe.wait_ge(*st.spectra.done("C qk"))
                        spectrum("C g", c("ind"), c("nind"), HEADS)
                        yield "C g"
                        pe.wait_ge(*M.emptied("C g"))
                        product(st, "C corr", [(st.G[:, i, :], idft[:, i, :]) for i in range(4)], rows=HEADS)
                        yield "C corr"
                        product(st, "C vf", [(st.vtok, dft[:, 0, :])])
                        yield "C vf"
                        pe.wait_ge(*st.selection.done("C"))
                        turn(st, "C w", lambda t: st.ew[:, t * P:(t + 1) * P], rows=HEADS, at=HEADS)
                        yield "C w"
                        pe.wait_ge(*T.emptied("C w"))
                        product(st, "C wf", [(tile(st.wx, t), dft[:, t, :]) for t in range(TILES)])
                        yield "C wf"
                        pe.wait_ge(*st.spectra.done("C vw"))
                        spectrum("C of", ident, c("nident"), P)
                        yield "C of"
                        pe.wait_ge(*M.emptied("C of"))
                        product(st, "C out", [(tile(st.of, i), idft[:, i, :]) for i in range(4)])
                        yield "C out"
                        pe.wait_ge(*M.emptied("C out"))
                        tokens(st, "C wo", lambda t: [(tile(nT, t), w("co"))])
                        yield "C wo"
                        if last_stage == "C":
                            return

                        pe.wait_ge(causal_in, 16)
                        pe.wait_ge(*st.normed.done("D1"))
                        turn(st, "D n", lambda t: ntok[:, t])
                        yield "D n"
                        pe.wait_ge(*T.emptied("D n"))
                        product(st, "D k", [(w("dqkv")[:, P:2 * P], nT[:])])
                        yield "D k"
                        product(st, "D q", [(w("dqkv")[:, 0:P], nT[:])])
                        yield "D q"
                        tokens(st, "D v", lambda t: [(tile(nT, t), w("dqkv")[:, 2 * P:3 * P])])
                        yield "D v"
                        pe.wait_ge(*M.emptied("D q"))
                        pe.wait_ge(*M.emptied("D v"))
                        pe.wait_ge(*st.prepared.done("D k"))
                        pe.wait_ge(*st.masked_keys.done("D"))
                        wo = w("dwo").rearrange("p (j d) -> p j d", j=4)
                        for i in range(ND + 4):
                            if i < ND:
                                t, heads = CAUSAL_UNITS[i]
                                wide = (t + 1) * P
                                reuse(S)
                                bank = S.take(("D s", i))
                                for n, h in enumerate(heads):
                                    last = nc.tensor.matmul(bank[:, n * wide:(n + 1) * wide], tile(st.QT, t), st.kTmD[:, h, 0:wide],
                                                            start=True, stop=True)
                                last.then_inc(S.fill(("D s", i)), 1)
                            if 1 <= i <= ND:
                                u = i - 1
                                t, heads = CAUSAL_UNITS[u]
                                pe.wait_ge(*st.exps.done(("D", u)))
                                turn(st, ("D p", u), lambda n: st.probs[:, u % 2, n * P:(n + 1) * P], n=len(heads) * (t + 1))
                            if 2 <= i <= ND + 1:
                                u = i - 2
                                t, heads = CAUSAL_UNITS[u]
                                if u == 0 or CAUSAL_UNITS[u - 1][0] != t:
                                    reuse(M)
                                    bank_o = M.take(("D o", t))
                                pe.wait_ge(*T.emptied(("D p", u)))
                                for k in range(t + 1):
                                    for n, h in enumerate(heads):
                                        at = (n * (t + 1) + k) * P
                                        r, j = 32 * (h % 4), h // 4
                                        last = nc.tensor.matmul(bank_o[r:r + 32, j * P:(j + 1) * P], st.vD[:, k, h, :],
                                                                st.probsT[:, u % 2, at:at + P], start=(k == 0), stop=(k == t),
                                                                skip_group_check=True)
                                if LAST_UNIT[t] == u:
                                    last.then_inc(M.fill(("D o", t)), 1)
                            if i - 3 in LAST_UNIT:
                                t = LAST_UNIT.index(i - 3)
                                pe.wait_ge(*st.attended.done(("D", t)))
                                product(st, ("D wo", t), [(st.oP[:, j, :], wo[:, j, :]) for j in range(4)], cols=P, ring=T)
                            yield ("D", i)
                        pe.wait_ge(*st.normed.done("D2"))
                        turn(st, "D n2", lambda t: ntok[:, t])
                        yield "D n2"
                        pe.wait_ge(*T.emptied("D n2"))
                        tokens(st, "D gate", lambda t: [(tile(nT, t), w("gate"))], cols=EXPERTS)
                        yield "D gate"

                        def up(e):
                            pe.wait_ge(expert_in[e % EXPERT_SLOTS], 16 * (e // EXPERT_SLOTS + 1))
                            for n in range(FC):
                                product(st, ("D f1", e, n), [(experts[:, e % EXPERT_SLOTS, n * P:(n + 1) * P], nT[:])], ring=S)

                        up(0)
                        yield "D up"
                        pe.wait_ge(*st.selection.done("D"))
                        turn(st, "D g", lambda t: st.gates[:, t, :], cols=EXPERTS)
                        yield "D g"
                        pe.wait_ge(*T.emptied("D g"))
                        tokens(st, "D b2", lambda t: [(st.gT[:, t * P:(t + 1) * P], w("fc2b", EXPERTS))])
                        yield "D b2"
                        for e in range(EXPERTS):
                            if e + 1 < EXPERTS:
                                up(e + 1)
                            for n in range(FC):
                                pe.wait_ge(*S.emptied(("D f1", e, n)))
                            fc2 = experts[:, e % EXPERT_SLOTS, FFN:].rearrange("p (c d) -> p c d", c=FC)
                            tokens(st, ("D f2", e), lambda t: [(st.hid[:, e % 2, n, t * P:(t + 1) * P], fc2[:, n, :])
                                                               for n in range(FC)])
                            yield ("D e", e)

                    alternate("pe", stream_program)

                @block.scalar
                def _(act):
                    def stream_program(st):
                        S, T, M, x, y, ntok, nT, hT = st.S, st.T, st.M, st.x, st.y, st.ntok, st.nT, st.hT

                        def turned(key):
                            act.wait_ge(*T.filled(key))
                            return T.bank(key)

                        def shift(key):
                            src = turned(key)
                            nc.scalar.activation(hT[0:64, :], src[0:64, :], ACT.Copy)
                            nc.scalar.activation(hT[64:P, 1:SEQ], src[64:P, 0:SEQ - 1], ACT.Copy).then_inc(T.empty(key), 1)

                        def turned_out(key, u, rows=P, n=512):
                            src = turned(key)
                            nc.scalar.activation(st.probsT[0:rows, u % 2, 0:n], src[0:rows, 0:n], ACT.Copy
                                                 ).then_inc(T.empty(key), 1)

                        yield "A n"
                        nc.scalar.activation(nT[:], turned("A n"), ACT.Copy).then_inc(T.empty("A n"), 1)
                        yield "A q"
                        for i in range(NA + 4):
                            if i < NA:
                                act.wait_ge(*st.centered.done(("A", i)))
                                row = st.probs[:, i % 2, 0:4 * CTX]
                                nc.scalar.activation(row, row, ACT.Exp).then_inc(st.exps.sem, 1)
                            if 1 <= i <= NA:
                                turned_out(("A p", i - 1), i - 1, rows=CTX)
                            yield ("A", i)
                        if last_stage == "A":
                            return

                        for l in range(LAYERS):
                            yield ("B y", l)
                            act.wait_ge(*st.cleared.done("B"))
                            shift(("B y", l))
                            for i in range(TILES + 2):
                                if i < TILES:
                                    for j, name in enumerate(("B q", "B k")):
                                        key = (name, l, i)
                                        act.wait_ge(*S.filled(key))
                                        if i and j == 0:
                                            act.wait_ge(*st.sums.done((l, i - 1)))
                                        nc.scalar.activation(st.sq[:, j, :], S.bank(key), ACT.Square).then_inc(st.squares.sem, 1)
                                    key = ("B v", l, i)
                                    act.wait_ge(*M.filled(key))
                                    v = M.bank(key).rearrange("p (h d) -> p h d", h=LHEADS)
                                    nc.scalar.activation(st.vmix_heads[WIN:P, i, :, 0:LHD], v[0:WIN], ACT.Copy)
                                    if i + 1 < TILES:
                                        nc.scalar.activation(st.vmix_heads[0:WIN, i + 1, :, 0:LHD], v[WIN:P], ACT.Copy)
                                    nc.scalar.activation(st.vnat_heads[:, i, :, 0:LHD], v, ACT.Copy).then_inc(M.empty(key), 1)
                                if 1 <= i <= TILES:
                                    t = i - 1
                                    key = ("B qk", l, t, 0)
                                    nc.scalar.activation(st.qT[:, :, t * P:(t + 1) * P], turned(key).rearrange("p (n k) -> p n k", n=PAIRS),
                                                         ACT.Copy).then_inc(T.empty(key), 1)
                                    key = ("B qk", l, t, 1)
                                    src = turned(key).rearrange("p (n k) -> p n k", n=PAIRS)
                                    z = st.kTz[:].rearrange("p (n e) k -> p n e k", e=2)
                                    nc.scalar.activation(z[0:64, :, 0, WIN + t * P:WIN + (t + 1) * P], src[0:64], ACT.Copy)
                                    nc.scalar.activation(z[64:P, :, 1, WIN + t * P:WIN + (t + 1) * P], src[64:P], ACT.Copy
                                                         ).then_inc(T.empty(key), 1)
                                yield ("B qk", l, i)
                            for i in range(2 * TILES + 3):
                                if i < 2 * TILES:
                                    act.wait_ge(*st.maxima.done(("B", l, i)))
                                    for n in range(4):
                                        row = st.probs[:, i % 2, n * P:(n + 1) * P]
                                        last = nc.scalar.activation(row, row, ACT.Exp, bias=st.nm[:, i % 2, n:n + 1], scale=QK_SCALE)
                                    last.then_inc(st.exps.sem, 1)
                                if 1 <= i <= 2 * TILES:
                                    turned_out(("B p", l, i - 1), i - 1)
                                if i >= 4 and i % 2 == 0:
                                    t = (i - 4) // 2
                                    key = ("B o", l, t)
                                    nc.scalar.activation(st.oT[:, :, t * P:(t + 1) * P], turned(key).rearrange("p (n k) -> p n k", n=PAIRS),
                                                         ACT.Copy).then_inc(T.empty(key), 1)
                                yield ("B s", l, i)
                            yield ("B wo", l)
                            yield ("B y2", l)
                            shift(("B y2", l))
                            yield ("B tok", l)
                            yield ("B n", l)
                            key = ("B n", l)
                            nc.scalar.activation(nT[:], turned(key), ACT.Identity, bias=w(f"lnb{l}"), scale=w(f"lng{l}")
                                                 ).then_inc(T.empty(key), 1)
                            for i in range(3):
                                key = ("B w1", l, i, 1)
                                if i == 2:
                                    act.wait_ge(*S.emptied(("B w1", l, 0, 0)))
                                act.wait_ge(*S.filled(key))
                                nc.scalar.activation(st.gl[:, i % 2, :], S.bank(key), ACT.Gelu, bias=w(f"b1g{l}")[:, i:i + 1]
                                                     ).then_inc(S.empty(key), 1)
                                yield ("B w1", l, i)
                            yield ("B w2", l)
                        if last_stage == "B":
                            return

                        def copied(key, dst):
                            act.wait_ge(*M.filled(key))
                            nc.scalar.activation(dst, M.bank(key), ACT.Copy).then_inc(M.empty(key), 1)

                        yield "C kv"
                        yield "C kf"
                        copied("C kf", st.wf)
                        yield "C n"
                        nc.scalar.activation(nT[:], turned("C n"), ACT.Copy).then_inc(T.empty("C n"), 1)
                        yield "C q"
                        yield "C qf"
                        yield "C g"
                        yield "C corr"
                        act.wait_ge(*st.peak.done("C"))
                        nc.scalar.activation(st.ew[:], st.corr[:, 0:SEQ], ACT.Exp, bias=st.top[:, 16:17]).then_inc(st.selection_exps.sem, 1)
                        yield "C vf"
                        copied("C vf", st.wf)
                        yield "C w"
                        weights_T = turned("C w")[:, 0:TILES * HEADS].rearrange("p (t h) -> p t h", t=TILES)
                        nc.scalar.activation(st.wx.rearrange("p (t h d) -> p t h d", t=TILES, h=HEADS),
                                             weights_T[:, :, :, None].broadcast_to([P, TILES, HEADS, HD]), ACT.Copy
                                             ).then_inc(T.empty("C w"), 1)
                        yield "C wf"
                        yield "C of"
                        copied("C of", st.of)
                        yield "C out"
                        copied("C out", nT[:])
                        yield "C wo"
                        if last_stage == "C":
                            return

                        yield "D n"
                        nc.scalar.activation(nT[:], turned("D n"), ACT.Identity, bias=w("ln1b"), scale=w("ln1w")
                                             ).then_inc(T.empty("D n"), 1)
                        yield "D k"
                        act.wait_ge(*M.filled("D k"))
                        nc.scalar.activation(st.kD, M.bank("D k"), ACT.Identity, bias=w("dbk")).then_inc(M.empty("D k"), 1)
                        yield "D q"
                        act.wait_ge(*M.filled("D q"))
                        nc.scalar.activation(st.QT[:], M.bank("D q"), ACT.Identity, bias=w("dbq")).then_inc(M.empty("D q"), 1)
                        yield "D v"
                        for i in range(ND + 4):
                            if i < ND:
                                t, heads = CAUSAL_UNITS[i]
                                wide = (t + 1) * P
                                act.wait_ge(*st.maxima.done(("D", i)))
                                for n in range(len(heads)):
                                    row = st.probs[:, i % 2, n * wide:(n + 1) * wide]
                                    last = nc.scalar.activation(row, row, ACT.Exp, bias=st.nm[:, i % 2, n:n + 1], scale=SCALE)
                                last.then_inc(st.exps.sem, 1)
                            if 1 <= i <= ND:
                                t, heads = CAUSAL_UNITS[i - 1]
                                turned_out(("D p", i - 1), i - 1, n=len(heads) * (t + 1) * P)
                            yield ("D", i)
                        yield "D n2"
                        nc.scalar.activation(nT[:], turned("D n2"), ACT.Identity, bias=w("ln2b"), scale=w("ln2w")
                                             ).then_inc(T.empty("D n2"), 1)
                        yield "D gate"
                        act.wait_ge(*st.peak.done("D"))
                        nc.scalar.activation(st.gex[:], st.gex[:], ACT.Exp).then_inc(st.selection_exps.sem, 1)
                        fc1b = w("fc1b").rearrange("p (e c) -> p e c", e=EXPERTS)

                        def hidden(e):
                            for n in range(FC):
                                key = ("D f1", e, n)
                                act.wait_ge(*S.filled(key))
                                nc.scalar.activation(st.hid[:, e % 2, n, :], S.bank(key), ACT.Gelu, bias=fc1b[:, e, n:n + 1]
                                                     ).then_inc(S.empty(key), 1)

                        hidden(0)
                        yield "D up"
                        yield "D g"
                        nc.scalar.activation(st.gT[:], turned("D g")[0:EXPERTS, :], ACT.Copy).then_inc(T.empty("D g"), 1)
                        yield "D b2"
                        for e in range(EXPERTS):
                            if e + 1 < EXPERTS:
                                if e:
                                    act.wait_ge(*M.filled(("D f2", e - 1)))
                                hidden(e + 1)
                            yield ("D e", e)

                    alternate("act", stream_program)

                @block.vector
                def _(dve):
                    v = nc.vector
                    chained = [0]

                    def link(instruction):
                        chained[0] += 1
                        instruction.then_inc(dve_chain, 1)
                        dve.wait_ge(dve_chain, chained[0])

                    def stream_program(st):
                        S, T, M, x, y, ntok, nT, hT = st.S, st.T, st.M, st.x, st.y, st.ntok, st.nT, st.hT
                        probs, mx, nm = st.probs, st.mx, st.nm

                        def layer_norm(key, source, out):
                            for t in range(TILES):
                                last = v.bn_stats(st.stats[:, t], source(t))
                            link(last)
                            for t in range(TILES):
                                last = v.bn_aggr(st.mv[:, t], st.stats[:, t])
                            last.then_inc(st.stats_ready.sem, 1)
                            dve.wait_ge(*st.rstd_ready.done(key))
                            for t in range(TILES):
                                last = v.tensor_scalar(out[:, t], source(t), st.mv[:, t, 0:1], st.rstd[:, t:t + 1],
                                                       ALU.subtract, ALU.mult)
                            last.then_inc(st.normed.sem, 1)

                        def made(key, ring=None):
                            ring = ring or M
                            dve.wait_ge(*ring.filled(key))
                            return ring.bank(key)

                        def add_tokens(key, stream):
                            src = made(key).rearrange("p (t d) -> p t d", t=TILES)
                            v.tensor_tensor(stream[:], src, stream[:], ALU.add).then_inc(M.empty(key), 1)

                        def normalize(stage, t):
                            src = made((stage + " o", t))
                            if t:
                                dve.wait_ge(*T.filled((stage + " wo", t - 1)))
                            link(v.stream_shuffle(st.recip, src, [HD] * 32))
                            link(v.reciprocal(st.recip, st.recip))
                            v.tensor_tensor(st.oP.rearrange("p j q -> p (j q)"), src, st.recip, ALU.mult
                                            ).then_inc(M.empty((stage + " o", t)), 1)
                            dve.wait_ge(*M.emptied((stage + " o", t)))
                            v.tensor_copy(st.small[:, 5:6], st.small[:, 4:5]).then_inc(st.attended.sem, 1)

                        def add_tile(key, stream, t):
                            src = made(key, T)
                            v.tensor_tensor(stream[:, t], src[:, 0:P], stream[:, t], ALU.add).then_inc(T.empty(key), 1)

                        dve.wait_ge(consts_in, 16)
                        dve.wait_ge(weights_in, 16)
                        dve.wait_ge(st.x_in, 16)
                        layer_norm("A", lambda t: x[:, t], ntok)
                        yield "A n"
                        kv = made("A kv")
                        link(v.memset(st.vA[:], 0.0))
                        v.tensor_scalar(st.kA, kv[:, 0:CTX], w("abk"), None, ALU.add)
                        link(v.memset(st.vA[0:CTX, :, HD:HD + 1], 1.0))
                        v.tensor_tensor(st.kTmA[:], st.kA[:, None, :].broadcast_to([P, HEADS, CTX]),
                                        c("headmask")[:, :, None].broadcast_to([P, HEADS, CTX]), ALU.mult)
                        v.tensor_tensor(st.vA[0:CTX, :, 0:HD], kv[0:CTX, P:2 * P].rearrange("p (h d) -> p h d", h=HEADS),
                                        w("abv", CTX).rearrange("p (h d) -> p h d", h=HEADS), ALU.add
                                        ).then_inc(M.empty("A kv"), 1)
                        dve.wait_ge(*M.emptied("A kv"))
                        v.tensor_copy(st.small[:, 5:6], st.small[:, 4:5]).then_inc(st.prepared.sem, 1)
                        yield "A q"
                        v.tensor_scalar(st.QT[:], made("A q"), w("abq"), SCALE, ALU.add, ALU.mult).then_inc(M.empty("A q"), 1)
                        dve.wait_ge(*st.mask_scaled.done("A"))
                        for i in range(NA + 4):
                            if i < NA:
                                t, key = i // 4, ("A s", i)
                                k = i % 2
                                if i >= 2:
                                    dve.wait_ge(*T.filled(("A p", i - 2)))
                                dve.wait_ge(*S.filled(key))
                                out = probs[:, k, 0:4 * CTX].rearrange("p (h k) -> p h k", h=4)
                                v.tensor_tensor(out, S.bank(key)[:, 0:4 * CTX].rearrange("p (h k) -> p h k", h=4),
                                                st.maskb[:, t, None, :].broadcast_to([P, 4, CTX]), ALU.add
                                                ).then_inc(S.empty(key), 1)
                                dve.wait_ge(*S.emptied(key))
                                v.tensor_reduce(mx[:, k, :], out, X_AXIS, ALU.max).then_inc(st.maxima.sem, 1)
                            if 2 <= i <= NA + 1 and i % 4 == 1:
                                normalize("A", (i - 2) // 4)
                            if i >= 4 and i % 4 == 3:
                                t = (i - 4) // 4
                                if t == 0:
                                    dve.wait_ge(*st.biased.done("A"))
                                add_tile(("A wo", t), x, t)
                            yield ("A", i)
                        if last_stage == "A":
                            return

                        dve.wait_ge(*T.emptied(("A wo", TILES - 1)))
                        layer_norm("B", lambda t: x[:, t], y)
                        v.memset(hT[64:P, 0:1], 0.0)
                        link(v.memset(st.vmix[0:WIN, 0, :], 0.0))
                        v.memset(st.vnat_heads[:, :, :, LHD:LHD + 1], 1.0)
                        v.memset(st.vmix_heads[:, :, :, LHD:LHD + 1], 1.0).then_inc(st.ones.sem, 1)
                        for l in range(LAYERS):
                            yield ("B y", l)

                            def rotate(t):
                                dve.wait_ge(*st.norms.done((l, t)))
                                if t:
                                    dve.wait_ge(*T.filled(("B qk", l, t - 1, 1)))
                                for j, name in enumerate(("B q", "B k")):
                                    v.tensor_tensor(st.qn[:, j, :].rearrange("p (h d) -> p h d", d=LHD),
                                                    S.bank((name, l, t)).rearrange("p (h d) -> p h d", d=LHD),
                                                    st.rn[:, t % 2, 8 * j:8 * j + 8, None].broadcast_to([P, LHEADS, LHD]), ALU.mult
                                                    ).then_inc(S.empty((name, l, t)), 1)
                                dve.wait_ge(*S.emptied(("B q", l, t)))
                                dve.wait_ge(*S.emptied(("B k", l, t)))
                                src = st.qn.rearrange("p a (h d) -> p a h d", d=LHD)
                                out = st.t2.rearrange("p a (h d) -> p a h d", d=LHD)
                                for o, i in ((0, 32), (32, 0)):
                                    last = v.tensor_tensor(out[:, :, :, o:o + 32], src[:, :, :, i:i + 32],
                                                           rot[l][:, t, :, 1, None, o:o + 32].broadcast_to([P, 2, LHEADS, 32]),
                                                           ALU.mult)
                                link(last)
                                dve.wait_ge(*st.cos_part.done((l, t)))
                                v.tensor_tensor(st.t1, st.t1, st.t2, ALU.add).then_inc(st.rotated.sem, 1)

                            for i in range(TILES + 2):
                                if i < TILES:
                                    dve.wait_ge(*st.squares.done((l, i, 1)))
                                    v.tensor_reduce(st.ss[:, i % 2, :], st.sq.rearrange("p a (h d) -> p (a h) d", d=LHD), X_AXIS,
                                                    ALU.add).then_inc(st.sums.sem, 1)
                                    rotate(i)
                                yield ("B qk", l, i)
                            for i in range(2 * TILES + 3):
                                if i < 2 * TILES:
                                    key = ("B s", l, i)
                                    k = i % 2
                                    if i >= 2:
                                        dve.wait_ge(*T.filled(("B p", l, i - 2)))
                                    dve.wait_ge(*S.filled(key))
                                    mask = c("local")[:, (0 if i < 2 else P):(P if i < 2 else 2 * P)]
                                    for n in range(4):
                                        last = v.tensor_tensor_reduce(
                                            probs[:, k, n * P:(n + 1) * P], S.bank(key)[:, n * P:(n + 1) * P], mask,
                                            1.0, SENTINEL, ALU.add, ALU.max, mx[:, k, n:n + 1])
                                    last.then_inc(S.empty(key), 1)
                                    dve.wait_ge(*S.emptied(key))
                                    v.tensor_scalar(nm[:, k, :], mx[:, k, :], -QK_SCALE, None, ALU.mult).then_inc(st.maxima.sem, 1)
                                if 2 <= i <= 2 * TILES + 1:
                                    u = i - 2
                                    t, half = divmod(u, 2)
                                    if half == 0 and t:
                                        dve.wait_ge(*T.filled(("B o", l, t - 1)))
                                    key = ("B o", l, u)
                                    src = made(key)[:, 0:4 * VN].rearrange("p (h d) -> p h d", h=4)
                                    link(v.reciprocal(st.rden[:, half, 0:4], src[:, :, LHD]))
                                    v.tensor_tensor(st.o8.rearrange("p (a h d) -> p a h d", a=2, h=4)[:, half],
                                                    src[:, :, 0:LHD], st.rden[:, half, 0:4, None].broadcast_to([P, 4, LHD]),
                                                    ALU.mult).then_inc(M.empty(key), 1)
                                yield ("B s", l, i)
                            yield ("B wo", l)
                            add_tokens(("B wo", l), y)
                            yield ("B y2", l)
                            yield ("B tok", l)
                            key = ("B tok", l)
                            src = made(key, T).rearrange("p (t d) -> p t d", t=TILES)
                            layer_norm(("F", l), lambda t: src[:, t], ntok)
                            dve.wait_ge(*st.normed.done(("F", l)))
                            v.tensor_copy(st.small[:, 5:6], st.small[:, 4:5]).then_inc(T.empty(key), 1)
                            yield ("B n", l)
                            for i in range(3):
                                key = ("B w1", l, i, 0)
                                dve.wait_ge(*S.emptied(("B w1", l, i, 1)))
                                dve.wait_ge(*S.filled(key))
                                v.scalar_tensor_tensor(out=st.hidB[:, i, :], in0=S.bank(key), scalar=w(f"b1a{l}")[:, i:i + 1],
                                                       in1=st.gl[:, i % 2, :], op0=ALU.add, op1=ALU.mult).then_inc(S.empty(key), 1)
                                yield ("B w1", l, i)
                            dve.wait_ge(*st.biased.done(("B", l)))
                            yield ("B w2", l)
                            add_tokens(("B w2", l), y)
                        if last_stage == "B":
                            return

                        yield "C kv"
                        kv = made("C kv")
                        link(v.memset(st.kvtok[:], 0.0))
                        v.tensor_tensor(st.ktok[0:CTX], kv[0:CTX, 0:P], w("cbk", CTX), ALU.add)
                        v.tensor_tensor(st.vtok[0:CTX], kv[0:CTX, P:2 * P], w("cbv", CTX), ALU.add).then_inc(M.empty("C kv"), 1)
                        dve.wait_ge(*st.ffn_added.done("B"))
                        layer_norm("C", lambda t: x[:, t], ntok)
                        yield "C kf"
                        yield "C n"
                        yield "C q"
                        v.tensor_tensor(hT[:].rearrange("p (t d) -> p t d", t=TILES), made("C q").rearrange("p (t d) -> p t d", t=TILES),
                                        w("cbq")[:, None, :].broadcast_to([P, TILES, P]), ALU.add).then_inc(M.empty("C q"), 1)
                        yield "C qf"

                        def multiply_spectra(first, second, cd_first):
                            dve.wait_ge(*M.emptied(second))
                            psum, sbuf = made(first), st.wf
                            v.tensor_tensor(st.p1, psum, sbuf, ALU.mult)
                            ab, cd = (sbuf, psum) if cd_first else (psum, sbuf)
                            v.tensor_tensor(st.p2[:, 0:HALF], ab[:, HALF:], cd[:, 0:HALF], ALU.mult)
                            v.tensor_tensor(st.p2[:, HALF:], ab[:, 0:HALF], cd[:, HALF:], ALU.mult).then_inc(M.empty(first), 1)
                            dve.wait_ge(*M.emptied(first))
                            v.memset(st.p2[:, HALF:HALF + 1], 0.0)
                            link(v.tensor_copy(st.p2[:, 0:1], st.p1[:, HALF:HALF + 1]))
                            v.memset(st.p1[:, HALF:HALF + 1], 0.0).then_inc(st.spectra.sem, 1)

                        multiply_spectra("C qf", "C kf", False)
                        yield "C g"
                        v.tensor_copy(st.G[:], made("C g")[:, 0:4 * HEADS].rearrange("p (i h) -> p i h", i=4)
                                      ).then_inc(M.empty("C g"), 1)
                        yield "C corr"
                        top, rep, ew, corr = st.top, st.rep, st.ew, st.corr
                        v.tensor_copy(corr[:, 0:SEQ], made("C corr")[0:HEADS, :]).then_inc(M.empty("C corr"), 1)
                        dve.wait_ge(*M.emptied("C corr"))
                        link(v.max(top[:, 0:8], corr[:, 0:SEQ]))
                        v.tensor_scalar(top[:, 16:17], top[:, 0:1], -1.0, None, ALU.mult).then_inc(st.peak.sem, 1)
                        link(v.tensor_copy(top[:, 8:8 + TOPK], top[:, 0:TOPK]))
                        link(v.match_replace(rep[:], top[:, 8:16], corr[:], REPLACED))
                        link(v.tensor_tensor(rep[:, 0:SEQ], rep[:, 0:SEQ], corr[:, 0:SEQ], ALU.not_equal))
                        dve.wait_ge(*st.selection_exps.done("C"))
                        link(v.tensor_tensor(ew[:], ew[:], rep[:, 0:SEQ], ALU.mult))
                        link(v.tensor_reduce(top[:, 17:18], ew[:], X_AXIS, ALU.add))
                        link(v.reciprocal(top[:, 18:19], top[:, 17:18]))
                        v.tensor_scalar(ew[:], ew[:], top[:, 18:19], None, ALU.mult).then_inc(st.selection.sem, 1)
                        yield "C vf"
                        yield "C w"
                        yield "C wf"
                        multiply_spectra("C wf", "C vf", True)
                        yield "C of"
                        yield "C out"
                        yield "C wo"
                        dve.wait_ge(*st.biased.done("C"))
                        add_tokens("C wo", x)
                        if last_stage == "C":
                            return

                        dve.wait_ge(*M.emptied("C wo"))
                        layer_norm("D0", lambda t: x[:, t], y)
                        dve.wait_ge(*st.normed.done("D0"))
                        layer_norm("D1", lambda t: y[:, t], ntok)
                        yield "D n"
                        yield "D k"
                        dve.wait_ge(*M.emptied("D k"))
                        for h in range(HEADS // 2):
                            last = v.tensor_scalar(st.kTmD[:, h, :], st.kD, c("headmask")[:, h:h + 1], None, ALU.mult)
                        last.then_inc(st.prepared.sem, 1)
                        yield "D q"
                        yield "D v"
                        dve.wait_ge(*st.cleared.done("D"))
                        v.memset(st.vD[:, :, :, HD:HD + 1], 1.0)
                        v.tensor_tensor(st.vD[:, :, :, 0:HD], made("D v").rearrange("p (t h d) -> p t h d", t=TILES, h=HEADS),
                                        w("dbv").rearrange("p (h d) -> p h d", h=HEADS)[:, None, :, :].broadcast_to([P, TILES, HEADS, HD]),
                                        ALU.add).then_inc(M.empty("D v"), 1)
                        for i in range(ND + 4):
                            if i < ND:
                                t, heads = CAUSAL_UNITS[i]
                                wide = (t + 1) * P
                                key = ("D s", i)
                                k = i % 2
                                if i >= 2:
                                    dve.wait_ge(*T.filled(("D p", i - 2)))
                                dve.wait_ge(*S.filled(key))
                                mask = c("causal")[:, SEQ - wide:SEQ]
                                for n in range(len(heads)):
                                    last = v.tensor_tensor_reduce(
                                        probs[:, k, n * wide:(n + 1) * wide], S.bank(key)[:, n * wide:(n + 1) * wide], mask,
                                        1.0, SENTINEL, ALU.add, ALU.max, mx[:, k, n:n + 1])
                                last.then_inc(S.empty(key), 1)
                                dve.wait_ge(*S.emptied(key))
                                n = len(heads)
                                v.tensor_scalar(nm[:, k, 0:n], mx[:, k, 0:n], -SCALE, None, ALU.mult).then_inc(st.maxima.sem, 1)
                            if i - 2 in LAST_UNIT:
                                normalize("D", LAST_UNIT.index(i - 2))
                            if i - 3 in LAST_UNIT:
                                t = LAST_UNIT.index(i - 3)
                                if t == 0:
                                    dve.wait_ge(*st.biased.done("D"))
                                add_tile(("D wo", t), y, t)
                            yield ("D", i)
                        dve.wait_ge(*T.emptied(("D wo", TILES - 1)))
                        layer_norm("D2", lambda t: y[:, t], ntok)
                        yield "D n2"
                        yield "D gate"
                        logit, gtop, gtwo, gex, lrep = st.logit, st.gtop, st.gtwo, st.gex, st.lrep
                        v.tensor_copy(logit[:, :, 0:8], made("D gate")[:, 0:TILES * EXPERTS].rearrange("p (t e) -> p t e", t=TILES)
                                      ).then_inc(M.empty("D gate"), 1)
                        dve.wait_ge(*M.emptied("D gate"))
                        for t in range(TILES):
                            last = v.max(gtop[:, t, :], logit[:, t, 0:8])
                        link(last)
                        v.tensor_tensor(gex[:], logit[:, :, 0:8], gtop[:, :, 0:1].broadcast_to([P, TILES, 8]), ALU.subtract
                                        ).then_inc(st.peak.sem, 1)
                        link(v.tensor_copy(gtwo[:, :, 0:2], gtop[:, :, 0:2]))
                        for t in range(TILES):
                            last = v.match_replace(lrep[:, t, :], gtwo[:, t, :], logit[:, t, :], REPLACED)
                        link(last)
                        link(v.tensor_tensor(lrep[:, :, 0:8], lrep[:, :, 0:8], logit[:, :, 0:8], ALU.not_equal))
                        dve.wait_ge(*st.selection_exps.done("D"))
                        link(v.tensor_tensor(gex[:], gex[:], lrep[:, :, 0:8], ALU.mult))
                        link(v.tensor_reduce(st.gsum[:], gex[:], X_AXIS, ALU.add))
                        link(v.reciprocal(st.gsum[:], st.gsum[:]))
                        v.tensor_tensor(st.gates[:], gex[:], st.gsum[:, :, None].broadcast_to([P, TILES, 8]), ALU.mult
                                        ).then_inc(st.selection.sem, 1)
                        yield "D up"
                        yield "D g"
                        yield "D b2"
                        add_tokens("D b2", y)
                        dve.wait_ge(*M.emptied("D b2"))
                        dve.wait_ge(*st.selection.done("D"))
                        for e in range(EXPERTS):
                            key = ("D f2", e)
                            if e:
                                dve.wait_ge(*M.emptied(("D f2", e - 1)))
                            src = made(key)
                            for t in range(TILES):
                                last = v.scalar_tensor_tensor(out=y[:, t], in0=src[:, t * P:(t + 1) * P], scalar=st.gates[:, t, e:e + 1],
                                                              in1=y[:, t], op0=ALU.mult, op1=ALU.add)
                            last.then_inc(M.empty(key), 1)
                            yield ("D e", e)
                        dve.wait_ge(*M.emptied(("D f2", EXPERTS - 1)))
                        v.tensor_tensor(x[:], x[:], y[:], ALU.add).then_inc(st.finished.sem, 1)

                    alternate("dve", stream_program)

                @block.gpsimd
                def _(pool):
                    g = nc.gpsimd
                    chained = [0]

                    def link(instruction):
                        chained[0] += 1
                        instruction.then_inc(pool_chain, 1)
                        pool.wait_ge(pool_chain, chained[0])

                    def stream_program(st):
                        S, T, M, x, y = st.S, st.T, st.M, st.x, st.y

                        def rsqrt(key):
                            pool.wait_ge(*st.stats_ready.done(key))
                            link(g.tensor_scalar(st.small[:, 0:TILES], st.mv[:, :, 1], EPS, None, ALU.add))
                            g.tensor_tensor(st.rstd[:], st.small[:, 0:TILES], mhalf[:, 0:TILES], ALU.pow).then_inc(st.rstd_ready.sem, 1)

                        def add_bias(stream, name):
                            g.tensor_tensor(stream[:], stream[:], w(name)[:, None, :].broadcast_to([P, TILES, P]), ALU.add
                                            ).then_inc(st.biased.sem, 1)

                        pool.wait_ge(set_up, LAYERS)
                        pool.wait_ge(st.mask_in, 16)
                        rsqrt("A")
                        yield "A n"
                        g.tensor_scalar(st.maskb[:], st.maskb[:], NEG, None, ALU.mult).then_inc(st.mask_scaled.sem, 1)
                        pool.wait_ge(*st.normed.done("A"))
                        add_bias(x, "abo")
                        yield "A q"
                        for i in range(NA + 4):
                            if i < NA:
                                k = i % 2
                                pool.wait_ge(*st.maxima.done(("A", i)))
                                s = st.probs[:, k, 0:4 * CTX].rearrange("p (h k) -> p h k", h=4)
                                g.tensor_tensor(s, s, st.mx[:, k, :, None].broadcast_to([P, 4, CTX]), ALU.subtract
                                                ).then_inc(st.centered.sem, 1)
                            yield ("A", i)
                        if last_stage == "A":
                            return

                        rsqrt("B")
                        pool.wait_ge(*st.ones.done("B"))
                        g.memset(st.kTz[:], 0.0).then_inc(st.cleared.sem, 1)
                        for l in range(LAYERS):
                            yield ("B y", l)
                            for i in range(TILES + 2):
                                if i < TILES:
                                    pool.wait_ge(*st.sums.done((l, i)))
                                    link(g.tensor_scalar(st.rn[:, i % 2, :], st.ss[:, i % 2, :], 1e-24, None, ALU.max))
                                    g.tensor_tensor(st.rn[:, i % 2, :], st.rn[:, i % 2, :], mhalf[:], ALU.pow).then_inc(st.norms.sem, 1)
                                    for j, name in enumerate(("B q", "B k")):
                                        pool.wait_ge(*S.emptied((name, l, i)))
                                        last = g.tensor_tensor(st.t1[:, j, :].rearrange("p (h d) -> p h d", h=LHEADS),
                                                               st.qn[:, j, :].rearrange("p (h d) -> p h d", h=LHEADS),
                                                               rot[l][:, i, j, 0, None, :].broadcast_to([P, LHEADS, LHD]), ALU.mult)
                                    last.then_inc(st.cos_part.sem, 1)
                                yield ("B qk", l, i)
                            for i in range(2 * TILES + 3):
                                yield ("B s", l, i)
                            yield ("B wo", l)
                            yield ("B y2", l)
                            yield ("B tok", l)
                            rsqrt(("F", l))
                            pool.wait_ge(*T.filled(("B y2", l)))
                            add_bias(y, f"b2{l}")
                            yield ("B n", l)
                            for i in range(3):
                                yield ("B w1", l, i)
                            yield ("B w2", l)
                        pool.wait_ge(*M.emptied(("B w2", LAYERS - 1)))
                        g.tensor_tensor(x[:], x[:], y[:], ALU.add).then_inc(st.ffn_added.sem, 1)
                        if last_stage == "B":
                            return

                        yield "C kv"
                        rsqrt("C")
                        pool.wait_ge(*st.normed.done("C"))
                        add_bias(x, "cbo")
                        g.memset(st.vD[:], 0.0).then_inc(st.cleared.sem, 1)
                        for name in ("kf", "n", "q", "qf", "g", "corr", "vf", "w", "wf", "of", "out", "wo"):
                            yield "C " + name
                        if last_stage == "C":
                            return

                        rsqrt("D0")
                        rsqrt("D1")
                        pool.wait_ge(*st.normed.done("D1"))
                        pool.wait_ge(causal_in, 16)
                        add_bias(y, "dbo")
                        yield "D n"
                        yield "D k"
                        pool.wait_ge(*M.emptied("D k"))
                        for h in range(HEADS // 2, HEADS):
                            last = g.tensor_scalar(st.kTmD[:, h, :], st.kD, c("headmask")[:, h:h + 1], None, ALU.mult)
                        last.then_inc(st.masked_keys.sem, 1)
                        yield "D q"
                        yield "D v"
                        for i in range(ND + 4):
                            yield ("D", i)
                        rsqrt("D2")
                        for name in ("n2", "gate", "up", "g", "b2"):
                            yield "D " + name
                        for e in range(EXPERTS):
                            yield ("D e", e)

                    alternate("pool", stream_program)

                @block.sync
                def _(sp):
                    def batches(dram, st):
                        return dram.rearrange("(r s) n d -> s r n d", s=STREAMS)[st.index]

                    for st in streams:
                        here = bass.ds(round_no, 1)
                        sp.dma_start(st.x[:], batches(x_dram, st)[here, :, :].rearrange("o (t p) d -> p (o t) d", p=P)).then_inc(st.x_in, 16)
                        sp.dma_start(st.ctxT[:], batches(ctxT_dram, st)[here, :, :].rearrange("o p k -> p (o k)")).then_inc(st.ctx_in, 16)
                        sp.dma_start(st.maskb[:], batches(mask_dram, st)[here, :, :].rearrange("o (t p) k -> p (o t) k", p=P)).then_inc(st.mask_in, 16)
                    for l in range(LAYERS):
                        a = STAY + l * LAYER_COLS
                        sp.dma_start(place[l][:, 0:LAYER_COLS], weights_dram[:, a:a + LAYER_COLS]).then_inc(layer_in[l], 16)
                    if last_stage in "CD":
                        for st in streams:
                            sp.wait_ge(*st.M.filled(("B w2", 0)))
                            sp.wait_ge(*st.biased.done(("B", 0)))
                        sp.dma_start(place[0][:, 0:2 * TILES * SEQ], consts_dram[:, CCOL["dft"][0]:]).then_inc(fourier_in, 16)
                    if last_stage == "D":
                        for st in streams:
                            sp.wait_ge(*st.M.filled(("B w2", 1)))
                            sp.wait_ge(*st.biased.done(("B", 1)))
                        a = WCOL["ln1w"][0]
                        sp.dma_start(place[1][:, 0:WTOTAL - a], weights_dram[:, a:]).then_inc(causal_in, 16)
                        for st in streams:
                            sp.wait_ge(*st.M.filled("C out"))
                        for e in range(EXPERTS):
                            if e >= EXPERT_SLOTS:
                                for st in streams:
                                    sp.wait_ge(*st.M.filled(("D f2", e - EXPERT_SLOTS)))
                            sp.dma_start(experts[:, e % EXPERT_SLOTS, :], experts_dram[e]).then_inc(expert_in[e % EXPERT_SLOTS], 16)
                    for st in streams:
                        if last_stage == "D":
                            sp.wait_ge(*st.finished.done("D"))
                        elif last_stage == "A":
                            sp.wait_ge(*st.T.emptied(("A wo", TILES - 1)))
                        elif last_stage == "B":
                            sp.wait_ge(*st.ffn_added.done("B"))
                        else:
                            sp.wait_ge(*st.M.emptied("C wo"))
                        sp.dma_start(batches(out_dram, st)[bass.ds(round_no, 1), :, :].rearrange("o (t p) d -> p (o t) d", p=P),
                                     st.x[:]).then_inc(st.x_out, 16)
                    for st in streams:
                        sp.wait_ge(st.x_out, 16)
            nc.all_engine_barrier()
            first, n = batch_sems[0].num, len(batch_sems)
            assert [s.num for s in batch_sems] == list(range(first, first + n))
            nc.gpsimd.sem_clear(range(first, first + n))
            nc.all_engine_barrier()


def constants():
    import numpy as np
    out = np.zeros((P, CTOTAL), np.float32)

    def put(name, value):
        a, b = CCOL[name]
        out[:, a:b] = np.asarray(value).reshape(P, b - a)

    part = np.arange(P)
    put("ident", np.eye(P))
    put("nident", -np.eye(P))
    put("headmask", part[:, None] // HD == np.arange(HEADS)[None, :])
    ind = (part[:, None] // HD == np.arange(HEADS)[None, :]) / HD
    put("ind", ind)
    put("nind", -ind)
    i, j = (part % WIN)[:, None], np.arange(P)[None, :]
    allowed = (i <= j) & (j <= i + WIN)
    first = allowed & ((part >= WIN)[:, None] | (j >= WIN))
    put("local", np.where(np.concatenate([first, allowed], 1), 0.0, -1e37))
    q, k = part[:, None], np.arange(SEQ)[None, :]
    put("causal", np.where(k - (SEQ - P) <= q, 0.0, -1e37))
    half = np.arange(0, LHD, 2, dtype=np.float32)
    inv = (1.0 / np.float32(10000.0) ** (half / LHD)).astype(np.float32)
    pos = np.arange(SEQ, dtype=np.float32)
    freqs = np.tile(pos[:, None] * inv[None, :], (1, 2)).astype(np.float32)
    base = (half + 0.4 * LHD) / (1.4 * LHD)
    scale = np.tile(base[None, :] ** ((pos - SEQ // 2) / (WIN // 2))[:, None], (1, 2)).astype(np.float64)
    cos, sin = np.cos(freqs.astype(np.float64)), np.sin(freqs.astype(np.float64))
    sin[:, :LHD // 2] *= -1
    rot = np.stack([np.stack([cos * scale, sin * scale], 1), np.stack([cos / scale, sin / scale], 1)], 1)
    put("rot", rot.reshape(TILES, P, 2, 2, LHD).transpose(1, 0, 2, 3, 4))
    n = np.arange(SEQ)[:, None]
    f = np.arange(HALF)[None, :]
    angle = 2 * np.pi * ((n * f) % SEQ) / SEQ
    cosines, sines = np.cos(angle), np.sin(angle)
    sines[:, 0] = (-1.0) ** n[:, 0]
    table = np.concatenate([cosines, sines], 1)
    put("dft", table.reshape(TILES, P, SEQ).transpose(1, 0, 2))
    weight = np.full((SEQ, 1), 2.0 / SEQ)
    weight[0] = weight[HALF] = 1.0 / SEQ
    put("idft", (table.T * weight).reshape(TILES, P, SEQ).transpose(1, 0, 2))
    return out


def pack_weights(a):
    import numpy as np
    out = np.zeros((P, WTOTAL), np.float32)

    def put(name, value, rows=P):
        lo, hi = WCOL[name]
        out[:rows, lo:hi] = np.asarray(value).reshape(rows, hi - lo)

    def row(v):
        return np.broadcast_to(np.asarray(v)[None, :], (P, len(v)))

    def spread(v):
        wide = np.zeros((4, 32, 4, P), np.float32)
        wide[:, :HD] = np.asarray(v).reshape(4, 4, HD, P).transpose(1, 2, 0, 3)
        return wide

    for s, k in (("a", "L0_xattn_"), ("c", "L1_xattn_")):
        for n in "qkvo":
            put(s + n, spread(a[f"{k}W{n}"]) if s + n == "ao" else a[f"{k}W{n}"])
    put("abq", a["L0_xattn_bq"])
    put("abk", a["L0_xattn_bk"])
    put("abv", row(a["L0_xattn_bv"]))
    put("abo", row(a["L0_xattn_bo"]))
    for n in "qkvo":
        put("cb" + n, row(a[f"L1_xattn_b{n}"]))
    f = {k[len("L0_ffn_"):]: np.asarray(v) for k, v in a.items() if k.startswith("L0_ffn_")}
    for l in range(LAYERS):
        put(f"qkv{l}", f["wqkv"][l])
        put(f"qs{l}", row(f["q_scale"][l]))
        put(f"ks{l}", row(f["k_scale"][l]))
        put(f"bwo{l}", f["wo"][l].reshape(PAIRS, P, P).transpose(1, 0, 2))
        put(f"lng{l}", f["ln_g"][l])
        put(f"lnb{l}", f["ln_b"][l])
        w1 = np.zeros((P, 2, 3 * P), np.float32)
        w1[:, :, :HID] = f["w1"][l].reshape(P, 2, HID)
        put(f"w1{l}", w1)
        b1 = np.zeros((2, 3 * P), np.float32)
        b1[:, :HID] = f["b1"][l].reshape(2, HID)
        put(f"b1a{l}", b1[0].reshape(3, P).T)
        put(f"b1g{l}", b1[1].reshape(3, P).T)
        w2 = np.zeros((3 * P, P), np.float32)
        w2[:HID] = f["w2"][l]
        put(f"w2{l}", w2.reshape(3, P, P).transpose(1, 0, 2))
        put(f"b2{l}", row(f["b2"][l]))
    d = {k[len("L1_ffn_"):]: np.asarray(v) for k, v in a.items() if k.startswith("L1_ffn_")}
    put("ln1w", d["ln1_w"])
    put("ln1b", d["ln1_b"])
    put("ln2w", d["ln2_w"])
    put("ln2b", d["ln2_b"])
    put("dqkv", d["Wqkv"])
    put("dbq", d["bqkv"][0:P])
    put("dbk", d["bqkv"][P:2 * P])
    put("dbv", row(d["bqkv"][2 * P:]))
    put("dwo", spread(d["Wo"]))
    put("dbo", row(d["bo"]))
    put("gate", d["gate_W"])
    put("fc2b", d["fc2_b"], EXPERTS)
    put("fc1b", d["fc1_b"].reshape(EXPERTS, FC, P).transpose(2, 0, 1))
    return out


def pack_experts(fc1_w, fc2_w):
    import numpy as np
    fc1 = np.asarray(fc1_w).transpose(0, 2, 1)
    fc2 = np.asarray(fc2_w).reshape(EXPERTS, P, FC, P).transpose(0, 3, 2, 1).reshape(EXPERTS, P, FFN)
    return np.ascontiguousarray(np.concatenate([fc1, fc2], 2))


def kernel(**inputs):
    import numpy as np
    import concourse.bacc as bacc
    from concourse.bass_utils import run_bass_kernel_spmd

    nc = bacc.Bacc("TRN2", target_bir_lowering=False, num_devices=1)
    arrays = {
        "x_in": np.ascontiguousarray(inputs["x"]),
        "ctxT_in": np.ascontiguousarray(np.asarray(inputs["ctx_1024"]).transpose(0, 2, 1)),
        "mask_in": np.ascontiguousarray(np.asarray(inputs["mask_Bx1xSxS2_fk0"])[:, 0]),
        "weights": pack_weights(inputs),
        "experts_in": pack_experts(inputs["L1_ffn_fc1_w"], inputs["L1_ffn_fc2_w"]),
        "constants": constants(),
    }
    args = [nc.dram_tensor(n, v.shape, F32, kind="ExternalInput").ap() for n, v in arrays.items()]
    args.append(nc.dram_tensor("x_result", (BATCH, SEQ, P), F32, kind="ExternalOutput").ap())
    program(nc, *args)
    r = run_bass_kernel_spmd(nc, [arrays], core_ids=[0])
    return r.results[0]["x_result"]
```

```python
from contextlib import ExitStack

import concourse.bass as bass
from concourse import mybir
from concourse.alu_op_type import AluOpType as ALU

F32 = mybir.dt.float32
ACT = mybir.ActivationFunctionType
X_AXIS = mybir.AxisListType.X

P = 128
BATCH, SEQ, CTX = 4, 512, 77
STREAMS = 2
TURN, USE = 2, 3
TILES = SEQ // P
HEADS, HD = 16, 8
LAYERS, LHEADS, LHD, WIN = 2, 8, 64, 64
PAIRS = LHEADS // 2
VN = 96
VW = (LHEADS - 1) * (LHD + 1) + VN + 1
HID = 341
EXPERTS, FFN = 8, 512
FC = FFN // P
EXPERT_SLOTS = 4
TOPK = 6
HALF = SEQ // 2
SCALE = float(HD) ** -0.5
QK_SCALE = 8.0
EPS = 1e-5
NEG = -1e15
SENTINEL = -3.0e38
REPLACED = -3.3e38

WEIGHTS = (
    [("aq", P), ("ak", P), ("av", P), ("ao", 4 * P), ("abq", 1), ("abk", 1), ("abv", P), ("abo", P)]
    + [(f"{n}{l}", LHD) for l in range(LAYERS) for n in ("qs", "ks")]
    + [("cq", P), ("ck", P), ("cv", P), ("co", P), ("cbq", P), ("cbk", P), ("cbv", P), ("cbo", P)]
    + [(f"{n}{l}", c) for l in range(LAYERS) for n, c in (
        ("qkv", 3 * 512), ("bwo", PAIRS * P), ("lng", 1), ("lnb", 1),
        ("w1", 2 * 3 * P), ("b1a", 3), ("b1g", 3), ("w2", 3 * P), ("b2", P))]
    + [("ln1w", 1), ("ln1b", 1), ("ln2w", 1), ("ln2b", 1), ("dqkv", 3 * P), ("dbq", 1), ("dbk", 1), ("dbv", P),
       ("dwo", 4 * P), ("dbo", P), ("gate", EXPERTS), ("fc2b", P), ("fc1b", EXPERTS * FC)])
CONSTS = [("ident", P), ("nident", P), ("headmask", HEADS), ("ind", HEADS), ("nind", HEADS), ("local", 2 * P),
          ("causal", SEQ), ("rot", TILES * 2 * 2 * LHD), ("dft", TILES * SEQ), ("idft", TILES * SEQ)]


def columns(parts):
    at, out = 0, {}
    for name, n in parts:
        out[name] = (at, at + n)
        at += n
    return out, at


WCOL, WTOTAL = columns(WEIGHTS)
CCOL, CTOTAL = columns(CONSTS)
STAY = WCOL["qkv0"][0]
LAYER_COLS = WCOL["qkv1"][0] - STAY
PLACES = [max(LAYER_COLS, 2 * TILES * SEQ, EXPERT_SLOTS * 2 * FFN), max(LAYER_COLS, WTOTAL - WCOL["ln1w"][0])]

CAUSAL_UNITS = [(t, list(range(h, h + n))) for t, n in enumerate((4, 2, 1, 1)) for h in range(0, HEADS, n)]
LAST_UNIT = [max(u for u, (t, _) in enumerate(CAUSAL_UNITS) if t == tile) for tile in range(TILES)]


class Ring:

    def __init__(self, sem, name, banks):
        self.banks = banks
        self.full = [sem(f"{name}_full{i}") for i in range(len(banks))]
        self.free = [sem(f"{name}_free{i}") for i in range(len(banks))]
        self.at = {}

    def reused(self):
        s, n = len(self.at) % len(self.banks), len(self.at) // len(self.banks)
        return (self.free[s], n) if n else None

    def take(self, key):
        assert key not in self.at, key
        i = len(self.at)
        self.at[key] = (i % len(self.banks), i // len(self.banks))
        return self.bank(key)

    def bank(self, key):
        return self.banks[self.at[key][0]]

    def filled(self, key):
        s, n = self.at[key]
        return self.full[s], n + 1

    def emptied(self, key):
        s, n = self.at[key]
        return self.free[s], n + 1

    def fill(self, key):
        return self.full[self.at[key][0]]

    def empty(self, key):
        return self.free[self.at[key][0]]


class Marks:

    def __init__(self, sem, name, keys):
        self.sem = sem(name)
        self.n = {k: i + 1 for i, k in enumerate(keys)}

    def done(self, key):
        return self.sem, self.n[key]


NA, ND = 4 * TILES, len(CAUSAL_UNITS)


class Stream:

    def __init__(self, index, sem, sb, psum):
        self.index = index
        s = f"_{index}"
        self.x = sb("x" + s, [P, TILES, P])
        self.y = sb("y" + s, [P, TILES, P])
        self.ctxT = sb("ctxT" + s, [P, CTX])
        self.maskb = sb("maskb" + s, [P, TILES, CTX])
        normal = sb("normal" + s, [P, 2, 512])
        self.ntok = normal[:, 0, :].rearrange("p (t d) -> p t d", t=TILES)
        self.nT = normal[:, 1, :]
        self.hT = sb("hT" + s, [P, SEQ])
        self.QT = sb("QT" + s, [P, SEQ])
        self.probs = sb("probs" + s, [P, 2, 512])
        self.probsT = sb("probsT" + s, [P, 2, 512])
        region = sb("region" + s, [P, REGION])

        def part(at, *shape, rows=P):
            n = 1
            for d in shape:
                n *= d
            assert at + n <= REGION
            flat = region[0:rows, at:at + n]
            if len(shape) == 1:
                return flat
            if len(shape) == 2:
                return flat.rearrange("p (a b) -> p a b", a=shape[0])
            return flat.rearrange("p (a b c) -> p a b c", a=shape[0], b=shape[1])

        self.kTmA = part(0, HEADS, CTX)
        self.kA = part(1280, CTX)
        self.vA = part(1408, HEADS, 32)
        self.kTmD = part(0, HEADS, SEQ)
        self.vD = part(HEADS * SEQ, TILES, HEADS, 32)
        self.kD = normal[:, 0, :]
        turned_qk = sb("turned_qk" + s, [P, 2, 512])
        self.recip, self.rwide = turned_qk[:, 0, :], turned_qk[:, 1, :]
        self.oP = self.hT[:].rearrange("p (j q) -> p j q", j=4)
        kz, qz, vz = LHEADS * (WIN + SEQ), PAIRS * SEQ, TILES * VW
        self.kTz = part(0, LHEADS, WIN + SEQ)
        self.qT = part(kz, PAIRS, SEQ)
        self.oT = self.qT
        self.hidB = part(kz, 3, SEQ)
        self.vnat = part(kz + qz, TILES, VW)
        self.vmix = part(kz + qz + vz, TILES, VW)
        n = LHEADS * (LHD + 1)
        self.vnat_heads = self.vnat[:, :, 0:n].rearrange("p t (h d) -> p t h d", h=LHEADS)
        self.vmix_heads = self.vmix[:, :, 0:n].rearrange("p t (h d) -> p t h d", h=LHEADS)
        self.sq = self.probsT[:]
        self.t1 = [self.probs[:], turned_qk[:]]
        self.t2 = normal[:]
        self.o8 = normal[:, 0, :]
        self.gl = self.probs[:]
        self.p1, self.p2, self.wf, self.wx, self.of = (part(512 * i, 512) for i in range(5))
        self.kvtok = part(2560, 2 * P)
        self.ktok, self.vtok = part(2560, P), part(2560 + P, P)
        self.corr = sb("corr" + s, [HEADS, SEQ + 2])
        self.rep = sb("rep" + s, [HEADS, SEQ + 2])
        self.ew = sb("ew" + s, [HEADS, SEQ])
        self.G = sb("G" + s, [P, 4, HEADS])
        self.top = sb("top" + s, [HEADS, 24])
        self.hid = region[:, 0:2 * FC * SEQ].rearrange("p (a c n) -> p a c n", a=2, c=FC)
        self.logit = sb("logit" + s, [P, TILES, 16])
        self.lrep = sb("lrep" + s, [P, TILES, 16])
        self.gtop = sb("gtop" + s, [P, TILES, 8])
        self.gtwo = sb("gtwo" + s, [P, TILES, 8])
        self.gex = sb("gex" + s, [P, TILES, 8])
        self.gsum = sb("gsum" + s, [P, TILES])
        self.gates = sb("gates" + s, [P, TILES, 8])
        self.gT = self.QT[0:EXPERTS, :]
        self.stats = sb("stats" + s, [P, TILES, 6])
        self.mv = sb("mv" + s, [P, TILES, 2])
        self.small = sb("small" + s, [P, 8])
        self.rstd = sb("rstd" + s, [P, TILES])
        self.ss = sb("ss" + s, [P, 2, 16])
        self.rn = sb("rn" + s, [P, 2, 16])
        self.mx = sb("mx" + s, [P, 2, 4])
        self.nm = sb("nm" + s, [P, 2, 4])
        self.sums_of = sb("sums_of" + s, [P, 2, HEADS])
        self.rsum = sb("rsum" + s, [P, HEADS])
        self.rden = sb("rden" + s, [P, 2, 4])

        self.S = Ring(sem, "scores" + s, [psum(f"psS{s}_{i}")[:] for i in range(2)])
        self.T = Ring(sem, "turned" + s, [psum("psT" + s)[:]])
        self.M = Ring(sem, "products" + s, [psum("psM" + s)[:]])

        LT = [(l, t) for l in range(LAYERS) for t in range(TILES)]
        LNS = ["A", "B", ("F", 0), ("F", 1), "C", "D0", "D1", "D2"]
        UNITS = [("A", u) for u in range(NA)] + [("B", l, u) for l in range(LAYERS) for u in range(2 * TILES)] \
            + [("D", u) for u in range(ND)]

        def marks(name, keys):
            return Marks(sem, name + s, keys)

        self.stats_ready = marks("stats_ready", LNS)
        self.rstd_ready = marks("rstd_ready", LNS)
        self.normed = marks("normed", LNS)
        self.maxima = marks("maxima", UNITS)
        self.exps = marks("exps", UNITS)
        AD = [(k, t) for k in "AD" for t in range(TILES)]
        self.reciprocals = marks("reciprocals", AD)
        self.widened = marks("widened", AD)
        self.prepared = marks("prepared", ["A kv", "D k"])
        self.masked_keys = marks("masked_keys", range(1, TILES))
        self.cleared = marks("cleared", ["B", "D"])
        self.ones = marks("ones", ["B"])
        self.squares = marks("squares", [(l, t, j) for l, t in LT for j in range(2)])
        self.sums = marks("sums", LT)
        self.norms = marks("norms", LT)
        self.turns_added = marks("turns_added", LT)
        self.rotated = marks("rotated", LT)
        self.biased = marks("biased", ["A", ("B", 0), ("B", 1), "C", "D"])
        self.ffn_added = marks("ffn_added", ["B"])
        self.spectra = marks("spectra", ["C qk", "C vw"])
        self.peak = marks("peak", ["C", "D"])
        self.selection_exps = marks("selection_exps", ["C", "D"])
        self.selection = marks("selection", ["C", "D"])
        self.finished = marks("finished", ["D"])
        self.mask_scaled = marks("mask_scaled", ["A"])
        self.x_in = sem("x_in" + s)
        self.ctx_in = sem("ctx_in" + s)
        self.mask_in = sem("mask_in" + s)
        self.x_out = sem("x_out" + s)


REGION = LHEADS * (WIN + SEQ) + PAIRS * SEQ + 2 * TILES * VW
steps_seen = {}


def program(nc, x_dram, ctxT_dram, mask_dram, weights_dram, experts_dram, consts_dram, out_dram, last_stage="D"):
    with ExitStack() as stack:
        sems = []

        def sem(name):
            s = stack.enter_context(nc.semaphore(name))
            sems.append(s)
            return s

        def sb(name, shape):
            return stack.enter_context(nc.sbuf_tensor(name, shape, F32))

        def psum(name):
            return stack.enter_context(nc.psum_tensor(name, [P, 512], F32))

        wt = sb("wt", [P, STAY])
        cs = sb("cs", [P, CCOL["dft"][0]])
        place = [sb(f"place{i}", [P, n]) for i, n in enumerate(PLACES)]
        mhalf = sb("mhalf", [P, 16])

        def w(name, rows=P):
            a, b = WCOL[name]
            for first, buffer in ((WCOL["ln1w"][0], place[1]), (WCOL["qkv1"][0], place[1]), (STAY, place[0]), (0, wt)):
                if a >= first:
                    return buffer[0:rows, a - first:b - first]

        def c(name, rows=P):
            a, b = CCOL[name]
            return cs[0:rows, a:b]

        ident = c("ident")
        dft, idft = (place[0][:, i * TILES * SEQ:(i + 1) * TILES * SEQ].rearrange("p (t f) -> p t f", t=TILES) for i in range(2))
        experts = place[0][:, 0:EXPERT_SLOTS * 2 * FFN].rearrange("p (s n) -> p s n", s=EXPERT_SLOTS)
        rot_base = c("rot").rearrange("p (t q a d) -> p t q a d", t=TILES, q=2, a=2)
        rot = [sb("rot", [P, TILES, 2, 2, LHD])[:], rot_base]
        streams = [Stream(i, sem, sb, psum) for i in range(STREAMS)]
        dve_chain = sem("dve_chain")
        pool_chain = sem("pool_chain")
        expert_in = [sem(f"expert_in{i}") for i in range(EXPERT_SLOTS)]
        layer_in = [sem(f"layer_in{l}") for l in range(LAYERS)]
        fourier_in = sem("fourier_in")
        causal_in = sem("causal_in")
        rotary_in = sem("rotary_in")
        autocorrelation_in = sem("autocorrelation_in")
        rotary_made = sem("rotary_made")
        batch_sems = list(sems)

        weights_in = sem("weights_in")
        consts_in = sem("consts_in")

        def mask_keys(engine, st, t):
            return engine.tensor_tensor(st.kTmD[:, :, t * P:(t + 1) * P], st.kD[:, None, t * P:(t + 1) * P].broadcast_to([P, HEADS, P]),
                                        c("headmask")[:, :, None].broadcast_to([P, HEADS, P]), ALU.mult)

        def alternate(engine, stream_program):
            lanes = [stream_program(st) for st in streams]
            names = [[] for _ in streams]
            while any(lane is not None for lane in lanes):
                for i in range(STREAMS):
                    if lanes[i] is None:
                        continue
                    try:
                        names[i].append(next(lanes[i]))
                    except StopIteration:
                        lanes[i] = None
            assert steps_seen.setdefault("steps", names[0]) == names[0] == names[1], engine

        with nc.Block() as block:
            @block.sync
            def _(sp):
                a, b = CCOL["rot"][0], WCOL["qs0"][0]
                sp.dma_start(wt[:, 0:b], weights_dram[:, 0:b]).then_inc(weights_in, 16)
                sp.dma_start(cs[:, 0:a], consts_dram[:, 0:a]).then_inc(consts_in, 16)

            @block.vector
            def _(dve):
                v = nc.vector
                v.memset(mhalf[:], -0.5)
                for st in streams:
                    for values in (st.vnat, st.vmix):
                        v.memset(values[:, :, LHEADS * (LHD + 1):], 0.0)
                    v.memset(st.probsT[:], 0.0)
                    v.memset(st.small[:], 0.0)
                    v.memset(st.corr[:, SEQ:SEQ + 2], SENTINEL)
                    v.memset(st.top[:, 8 + TOPK:16], SENTINEL)
                    v.memset(st.logit[:, :, 8:16], SENTINEL)
                    v.memset(st.gtwo[:, :, 2:8], SENTINEL)

        with nc.Fori(0, BATCH // STREAMS) as round_no:
            with nc.Block() as block:
                @block.tensor
                def _(pe):
                    def reuse(ring):
                        before = ring.reused()
                        if before:
                            pe.wait_ge(*before)

                    def turn(st, key, source, rows=P, cols=P, n=TILES, at=P):
                        reuse(st.T)
                        bank = st.T.take(key)
                        for i in range(n):
                            last = nc.tensor.transpose(bank[0:cols, i * at:i * at + rows], source(i), ident[0:rows, 0:rows])
                        last.then_inc(st.T.fill(key), 1)

                    def product(st, key, terms, rows=P, cols=SEQ, ring=None):
                        ring = ring or st.M
                        reuse(ring)
                        bank = ring.take(key)
                        for i, (lhsT, rhs) in enumerate(terms):
                            last = nc.tensor.matmul(bank[0:rows, 0:cols], lhsT, rhs, start=(i == 0), stop=(i == len(terms) - 1))
                        last.then_inc(ring.fill(key), 1)

                    def tokens(st, key, terms, cols=P):
                        reuse(st.M)
                        bank = st.M.take(key)
                        for t in range(TILES):
                            pairs = terms(t)
                            for i, (lhsT, rhs) in enumerate(pairs):
                                last = nc.tensor.matmul(bank[:, t * cols:(t + 1) * cols], lhsT, rhs,
                                                        start=(i == 0), stop=(i == len(pairs) - 1))
                        last.then_inc(st.M.fill(key), 1)

                    def tile(buf, t):
                        return buf[:, t * P:(t + 1) * P]

                    def spread_reciprocals(st, stage, t):
                        pe.wait_ge(*st.widened.done((stage, t)))
                        reuse(st.T)
                        key = (stage + " r", t)
                        bank = st.T.take(key)
                        for j in range(4):
                            last = nc.tensor.matmul(bank[:, j * P:(j + 1) * P],
                                                    st.rwide[:, j * P:(j + 1) * P], ident, start=True, stop=True)
                        last.then_inc(st.T.fill(key), 1)

                    def stream_program(st):
                        S, T, M, x, y, ntok, nT, hT = st.S, st.T, st.M, st.x, st.y, st.ntok, st.nT, st.hT
                        pe.wait_ge(consts_in, 16)
                        pe.wait_ge(weights_in, 16)
                        pe.wait_ge(st.ctx_in, 16)
                        bank = M.take("A kv")
                        nc.tensor.matmul(bank[:, 0:CTX], w("ak"), st.ctxT[:], start=True, stop=True)
                        nc.tensor.matmul(bank[0:CTX, P:2 * P], st.ctxT[:], w("av"), start=True,
                                         stop=True).then_inc(M.fill("A kv"), 1)
                        yield "statistics", "A"
                        pe.wait_ge(*st.normed.done("A"))
                        turn(st, "A n", lambda t: ntok[:, t])
                        yield "A n"
                        pe.wait_ge(*T.emptied("A n"))
                        product(st, "A q", [(w("aq"), nT[:])])
                        yield "A q"
                        pe.wait_ge(*M.emptied("A q"))
                        pe.wait_ge(*st.prepared.done("A kv"))
                        wo = w("ao").rearrange("p (j d) -> p j d", j=4)
                        for i in range(NA + 5):
                            if i >= USE and (i - USE) % 4 == 3:
                                spread_reciprocals(st, "A", (i - USE) // 4)
                            if i < NA:
                                t, g = divmod(i, 4)
                                product(st, ("A s", i), [(tile(st.QT, t), st.kTmA[:, 4 * g:4 * g + 4, :].rearrange("p h k -> p (h k)"))],
                                        cols=4 * CTX, ring=S)
                            if TURN <= i < NA + TURN:
                                u = i - TURN
                                pe.wait_ge(*st.exps.done(("A", u)))
                                turn(st, ("A p", u), lambda n: st.probs[:, u % 2, n * CTX:(n + 1) * CTX], cols=CTX)
                            if USE <= i < NA + USE:
                                u = i - USE
                                t, g = divmod(u, 4)
                                if g == 0:
                                    reuse(M)
                                    bank = M.take(("A o", t))
                                pe.wait_ge(*T.emptied(("A p", u)))
                                for n in range(4):
                                    last = nc.tensor.matmul(bank[32 * n:32 * n + 32, g * P:(g + 1) * P], st.vA[:, 4 * g + n, :],
                                                            st.probsT[:, u % 2, n * P:(n + 1) * P], start=True, stop=True)
                                if g == 3:
                                    last.then_inc(M.fill(("A o", t)), 1)
                            if 4 + USE <= i < NA + 4 and i % 4 == USE % 4:
                                t = (i - 4 - USE) // 4
                                pe.wait_ge(*M.emptied(("A o", t)))
                                product(st, ("A wo", t), [(st.oP[:, j, :], wo[:, j, :]) for j in range(4)], cols=P, ring=T)
                            yield ("A", i)
                        if last_stage == "A":
                            return

                        yield "statistics", "B"
                        for l in range(LAYERS):
                            pe.wait_ge(layer_in[l], 16)
                            if l == 0:
                                pe.wait_ge(*st.normed.done("B"))
                            else:
                                pe.wait_ge(*M.emptied(("B w2", l - 1)))
                            turn(st, ("B y", l), lambda t: y[:, t])
                            yield ("B y", l)
                            yield ("B shift", l)
                            pe.wait_ge(*T.emptied(("B y", l)))
                            wqkv = w(f"qkv{l}")
                            for i in range(TILES + 1):
                                if i < TILES:
                                    product(st, ("B q", l, i), [(tile(hT, i), wqkv[:, 0:512])], ring=S)
                                    product(st, ("B k", l, i), [(tile(hT, i), wqkv[:, 512:1024])], ring=S)
                                for j in range(2):
                                    if i >= 1:
                                        t = i - 1
                                        pe.wait_ge(*st.rotated.done((l, t)))
                                        turn(st, ("B qk", l, t, j), lambda n: st.t1[t % 2][:, j, n * P:(n + 1) * P])
                                    if i < TILES and j == 0:
                                        product(st, ("B v", l, i), [(tile(hT, i), wqkv[:, 1024:1536])])
                                yield ("B qk", l, i)
                            for i in range(2 * TILES + 4):
                                if TURN <= i < 2 * TILES + TURN:
                                    u = i - TURN
                                    pe.wait_ge(*st.exps.done(("B", l, u)))
                                    turn(st, ("B p", l, u), lambda n: st.probs[:, u % 2, n * P:(n + 1) * P])
                                if i < 2 * TILES:
                                    t, half = divmod(i, 2)
                                    key = ("B s", l, i)
                                    reuse(S)
                                    bank = S.take(key)
                                    pe.wait_ge(*T.emptied(("B qk", l, t, 1)))
                                    for n in range(4):
                                        h = 4 * half + n
                                        for win in range(2):
                                            q0 = t * P + win * WIN
                                            last = nc.tensor.matmul(
                                                bank[win * WIN:(win + 1) * WIN, n * P:(n + 1) * P],
                                                st.qT[:, h // 2, q0:q0 + WIN], st.kTz[:, h, q0:q0 + P], start=True, stop=True)
                                    last.then_inc(S.fill(key), 1)
                                if i >= 5 and i % 2:
                                    t = (i - 5) // 2
                                    pe.wait_ge(*M.emptied(("B o", l, 2 * t + 1)))
                                    turn(st, ("B o", l, t), lambda n: st.o8[:, n * P:(n + 1) * P])
                                if USE <= i < 2 * TILES + USE:
                                    u = i - USE
                                    t, half = divmod(u, 2)
                                    key = ("B o", l, u)
                                    reuse(M)
                                    bank = M.take(key)
                                    pe.wait_ge(*T.emptied(("B p", l, u)))
                                    for n in range(4):
                                        h = 4 * half + n
                                        for win, v in enumerate((st.vmix, st.vnat)):
                                            last = nc.tensor.matmul(
                                                bank[win * WIN:(win + 1) * WIN, n * VN:(n + 1) * VN],
                                                st.probsT[:, u % 2, n * P + win * WIN:n * P + (win + 1) * WIN],
                                                v[:, t, h * (LHD + 1):h * (LHD + 1) + VN], start=True, stop=True)
                                    last.then_inc(M.fill(key), 1)
                                yield ("B s", l, i)
                            pe.wait_ge(*T.emptied(("B o", l, TILES - 1)))
                            wo_l = w(f"bwo{l}").rearrange("p (c d) -> p c d", c=PAIRS)
                            tokens(st, ("B wo", l), lambda t: [(st.oT[:, n, t * P:(t + 1) * P], wo_l[:, n, :]) for n in range(PAIRS)])
                            yield ("B wo", l)
                            pe.wait_ge(*M.emptied(("B wo", l)))
                            turn(st, ("B y2", l), lambda t: y[:, t])
                            yield ("B y2", l)
                            pe.wait_ge(*T.emptied(("B y2", l)))
                            turn(st, ("B tok", l), lambda t: tile(hT, t))
                            yield ("B tok", l)
                            yield "statistics", ("F", l)
                            pe.wait_ge(*st.normed.done(("F", l)))
                            turn(st, ("B n", l), lambda t: ntok[:, t])
                            yield ("B n", l)
                            yield ("B nT", l)
                            pe.wait_ge(*T.emptied(("B n", l)))
                            w1 = w(f"w1{l}").rearrange("p (a c) -> p a c", a=2)
                            for i in range(3):
                                for a in (1, 0):
                                    product(st, ("B w1", l, i, a), [(w1[:, a, i * P:(i + 1) * P], nT[:])], ring=S)
                                yield ("B w1", l, i)
                            for i in range(3):
                                pe.wait_ge(*S.emptied(("B w1", l, i, 0)))
                            w2 = w(f"w2{l}").rearrange("p (c d) -> p c d", c=3)
                            tokens(st, ("B w2", l), lambda t: [(st.hidB[:, n, t * P:(t + 1) * P], w2[:, n, :]) for n in range(3)])
                            yield ("B w2", l)
                        if last_stage == "B":
                            return

                        pe.wait_ge(fourier_in, 16)
                        pe.wait_ge(autocorrelation_in, 16)
                        reuse(M)
                        bank = M.take("C kv")
                        nc.tensor.matmul(bank[0:CTX, 0:P], st.ctxT[:], w("ck"), start=True, stop=True)
                        nc.tensor.matmul(bank[0:CTX, P:2 * P], st.ctxT[:], w("cv"), start=True, stop=True).then_inc(M.fill("C kv"), 1)
                        yield "C kv"
                        yield "statistics", "C"
                        pe.wait_ge(*M.emptied("C kv"))
                        product(st, "C kf", [(st.ktok, dft[:, 0, :])])
                        yield "C kf"
                        pe.wait_ge(*st.normed.done("C"))
                        turn(st, "C n", lambda t: ntok[:, t])
                        yield "C n"
                        pe.wait_ge(*T.emptied("C n"))
                        tokens(st, "C q", lambda t: [(tile(nT, t), w("cq"))])
                        yield "C q"
                        pe.wait_ge(*M.emptied("C q"))
                        product(st, "C qf", [(tile(hT, t), dft[:, t, :]) for t in range(TILES)])
                        yield "C qf"

                        def spectrum(key, plus, minus, cols):
                            reuse(M)
                            bank = M.take(key)
                            for i in range(4):
                                f = (i % 2) * P
                                p, second = (st.p1, plus) if i < 2 else (st.p2, minus)
                                for n, rhs in enumerate((plus, second)):
                                    last = nc.tensor.matmul(bank[:, i * cols:(i + 1) * cols], p[:, n * HALF + f:n * HALF + f + P],
                                                            rhs, start=(n == 0), stop=(n == 1))
                            last.then_inc(M.fill(key), 1)

                        pe.wait_ge(*st.spectra.done("C qk"))
                        spectrum("C g", c("ind"), c("nind"), HEADS)
                        yield "C g"
                        pe.wait_ge(*M.emptied("C g"))
                        product(st, "C corr", [(st.G[:, i, :], idft[:, i, :]) for i in range(4)], rows=HEADS)
                        yield "C corr"
                        product(st, "C vf", [(st.vtok, dft[:, 0, :])])
                        yield "C vf"
                        pe.wait_ge(*st.selection.done("C"))
                        turn(st, "C w", lambda t: st.ew[:, t * P:(t + 1) * P], rows=HEADS, at=HEADS)
                        yield "C w"
                        pe.wait_ge(*T.emptied("C w"))
                        product(st, "C wf", [(tile(st.wx, t), dft[:, t, :]) for t in range(TILES)])
                        yield "C wf"
                        pe.wait_ge(*st.spectra.done("C vw"))
                        spectrum("C of", ident, c("nident"), P)
                        yield "C of"
                        pe.wait_ge(*M.emptied("C of"))
                        product(st, "C out", [(tile(st.of, i), idft[:, i, :]) for i in range(4)])
                        yield "C out"
                        pe.wait_ge(*M.emptied("C out"))
                        tokens(st, "C wo", lambda t: [(tile(nT, t), w("co"))])
                        yield "C wo"
                        if last_stage == "C":
                            return

                        yield "statistics", "D0"
                        yield "statistics", "D1"
                        pe.wait_ge(causal_in, 16)
                        pe.wait_ge(*st.normed.done("D1"))
                        turn(st, "D n", lambda t: ntok[:, t])
                        yield "D n"
                        pe.wait_ge(*T.emptied("D n"))
                        product(st, "D k", [(w("dqkv")[:, P:2 * P], nT[:])])
                        yield "D k"
                        product(st, "D q", [(w("dqkv")[:, 0:P], nT[:])])
                        yield "D q"
                        tokens(st, "D v", lambda t: [(tile(nT, t), w("dqkv")[:, 2 * P:3 * P])])
                        yield "D v"
                        pe.wait_ge(*M.emptied("D q"))
                        pe.wait_ge(*M.emptied("D v"))
                        pe.wait_ge(*st.prepared.done("D k"))
                        wo = w("dwo").rearrange("p (j d) -> p j d", j=4)
                        for i in range(ND + 5):
                            if i - USE in LAST_UNIT:
                                spread_reciprocals(st, "D", LAST_UNIT.index(i - USE))
                            if i < ND:
                                t, heads = CAUSAL_UNITS[i]
                                wide = (t + 1) * P
                                if t and i - 1 in LAST_UNIT:
                                    pe.wait_ge(*st.masked_keys.done(t))
                                reuse(S)
                                bank = S.take(("D s", i))
                                for n, h in enumerate(heads):
                                    last = nc.tensor.matmul(bank[:, n * wide:(n + 1) * wide], tile(st.QT, t), st.kTmD[:, h, 0:wide],
                                                            start=True, stop=True)
                                last.then_inc(S.fill(("D s", i)), 1)
                            if TURN <= i < ND + TURN:
                                u = i - TURN
                                t, heads = CAUSAL_UNITS[u]
                                pe.wait_ge(*st.exps.done(("D", u)))
                                turn(st, ("D p", u), lambda n: st.probs[:, u % 2, n * P:(n + 1) * P], n=len(heads) * (t + 1))
                            if USE <= i < ND + USE:
                                u = i - USE
                                t, heads = CAUSAL_UNITS[u]
                                if u == 0 or CAUSAL_UNITS[u - 1][0] != t:
                                    reuse(M)
                                    bank_o = M.take(("D o", t))
                                pe.wait_ge(*T.emptied(("D p", u)))
                                for k in range(t + 1):
                                    for n, h in enumerate(heads):
                                        at = (n * (t + 1) + k) * P
                                        r, j = 32 * (h % 4), h // 4
                                        last = nc.tensor.matmul(bank_o[r:r + 32, j * P:(j + 1) * P], st.vD[:, k, h, :],
                                                                st.probsT[:, u % 2, at:at + P], start=(k == 0), stop=(k == t),
                                                                skip_group_check=True)
                                if LAST_UNIT[t] == u:
                                    last.then_inc(M.fill(("D o", t)), 1)
                            if i - USE - 1 in LAST_UNIT:
                                t = LAST_UNIT.index(i - USE - 1)
                                pe.wait_ge(*M.emptied(("D o", t)))
                                product(st, ("D wo", t), [(st.oP[:, j, :], wo[:, j, :]) for j in range(4)], cols=P, ring=T)
                            yield ("D", i)
                        yield "statistics", "D2"
                        pe.wait_ge(*st.normed.done("D2"))
                        turn(st, "D n2", lambda t: ntok[:, t])
                        yield "D n2"
                        pe.wait_ge(*T.emptied("D n2"))
                        tokens(st, "D gate", lambda t: [(tile(nT, t), w("gate"))], cols=EXPERTS)
                        yield "D gate"
                        yield "D peak"

                        def up(e):
                            pe.wait_ge(expert_in[e % EXPERT_SLOTS], 16 * (e // EXPERT_SLOTS + 1))
                            for n in range(FC):
                                product(st, ("D f1", e, n), [(experts[:, e % EXPERT_SLOTS, n * P:(n + 1) * P], nT[:])], ring=S)

                        up(0)
                        yield "D up"
                        pe.wait_ge(*st.selection.done("D"))
                        turn(st, "D g", lambda t: st.gates[:, t, :], cols=EXPERTS)
                        yield "D g"
                        pe.wait_ge(*T.emptied("D g"))
                        tokens(st, "D b2", lambda t: [(st.gT[:, t * P:(t + 1) * P], w("fc2b", EXPERTS))])
                        yield "D b2"
                        for e in range(EXPERTS):
                            if e + 1 < EXPERTS:
                                up(e + 1)
                            for n in range(FC):
                                pe.wait_ge(*S.emptied(("D f1", e, n)))
                            fc2 = experts[:, e % EXPERT_SLOTS, FFN:].rearrange("p (c d) -> p c d", c=FC)
                            tokens(st, ("D f2", e), lambda t: [(st.hid[:, e % 2, n, t * P:(t + 1) * P], fc2[:, n, :])
                                                               for n in range(FC)])
                            yield ("D e", e)

                    alternate("pe", stream_program)

                @block.scalar
                def _(act):
                    def stream_program(st):
                        S, T, M, x, y, ntok, nT, hT = st.S, st.T, st.M, st.x, st.y, st.ntok, st.nT, st.hT

                        def turned(key):
                            act.wait_ge(*T.filled(key))
                            return T.bank(key)

                        def shift(key):
                            src = turned(key)
                            nc.scalar.activation(hT[0:64, :], src[0:64, :], ACT.Copy)
                            nc.scalar.activation(hT[64:P, 1:SEQ], src[64:P, 0:SEQ - 1], ACT.Copy).then_inc(T.empty(key), 1)

                        def turned_out(key, u, rows=P, n=512):
                            src = turned(key)
                            nc.scalar.activation(st.probsT[0:rows, u % 2, 0:n], src[0:rows, 0:n], ACT.Copy
                                                 ).then_inc(T.empty(key), 1)

                        yield "statistics", "A"
                        yield "A n"
                        nc.scalar.activation(nT[:], turned("A n"), ACT.Copy).then_inc(T.empty("A n"), 1)
                        yield "A q"
                        for i in range(NA + 5):
                            if i < NA:
                                t, g = divmod(i, 4)
                                act.wait_ge(*st.maxima.done(("A", i)))
                                for n in range(4):
                                    row = st.probs[:, i % 2, n * CTX:(n + 1) * CTX]
                                    last = nc.scalar.activation(row, row, ACT.Exp, bias=st.nm[:, i % 2, n:n + 1],
                                                                accum_out=st.sums_of[:, t % 2, 4 * g + n:4 * g + n + 1])
                                last.then_inc(st.exps.sem, 1)
                            yield ("A", i)
                        if last_stage == "A":
                            return

                        yield "statistics", "B"
                        for l in range(LAYERS):
                            yield ("B y", l)
                            act.wait_ge(*st.ones.done("B"))
                            shift(("B y", l))
                            yield ("B shift", l)
                            for i in range(TILES + 1):
                                if i < TILES:
                                    for j, name in enumerate(("B q", "B k")):
                                        key = (name, l, i)
                                        act.wait_ge(*S.filled(key))
                                        if i and j == 0:
                                            act.wait_ge(*st.sums.done((l, i - 1)))
                                        nc.scalar.activation(st.sq[:, j, :], S.bank(key), ACT.Square).then_inc(st.squares.sem, 1)
                                if 1 <= i <= TILES:
                                    t = i - 1
                                    act.wait_ge(*st.cleared.done("B"))
                                    key = ("B qk", l, t, 0)
                                    nc.scalar.activation(st.qT[:, :, t * P:(t + 1) * P], turned(key).rearrange("p (n k) -> p n k", n=PAIRS),
                                                         ACT.Copy).then_inc(T.empty(key), 1)
                                    key = ("B qk", l, t, 1)
                                    src = turned(key).rearrange("p (n k) -> p n k", n=PAIRS)
                                    z = st.kTz[:].rearrange("p (n e) k -> p n e k", e=2)
                                    nc.scalar.activation(z[0:64, :, 0, WIN + t * P:WIN + (t + 1) * P], src[0:64], ACT.Copy)
                                    nc.scalar.activation(z[64:P, :, 1, WIN + t * P:WIN + (t + 1) * P], src[64:P], ACT.Copy
                                                         ).then_inc(T.empty(key), 1)
                                if i < TILES:
                                    key = ("B v", l, i)
                                    act.wait_ge(*M.filled(key))
                                    v = M.bank(key).rearrange("p (h d) -> p h d", h=LHEADS)
                                    nc.scalar.activation(st.vmix_heads[WIN:P, i, :, 0:LHD], v[0:WIN], ACT.Copy)
                                    if i + 1 < TILES:
                                        nc.scalar.activation(st.vmix_heads[0:WIN, i + 1, :, 0:LHD], v[WIN:P], ACT.Copy)
                                    nc.scalar.activation(st.vnat_heads[:, i, :, 0:LHD], v, ACT.Copy).then_inc(M.empty(key), 1)
                                yield ("B qk", l, i)
                            for i in range(2 * TILES + 4):
                                if TURN <= i < 2 * TILES + TURN:
                                    turned_out(("B p", l, i - TURN), i - TURN)
                                if i < 2 * TILES:
                                    act.wait_ge(*st.maxima.done(("B", l, i)))
                                    for n in range(4):
                                        row = st.probs[:, i % 2, n * P:(n + 1) * P]
                                        last = nc.scalar.activation(row, row, ACT.Exp, bias=st.nm[:, i % 2, n:n + 1], scale=QK_SCALE)
                                    last.then_inc(st.exps.sem, 1)
                                if i >= 5 and i % 2:
                                    t = (i - 5) // 2
                                    key = ("B o", l, t)
                                    nc.scalar.activation(st.oT[:, :, t * P:(t + 1) * P], turned(key).rearrange("p (n k) -> p n k", n=PAIRS),
                                                         ACT.Copy).then_inc(T.empty(key), 1)
                                yield ("B s", l, i)
                            yield ("B wo", l)
                            yield ("B y2", l)
                            shift(("B y2", l))
                            yield ("B tok", l)
                            yield "statistics", ("F", l)
                            yield ("B n", l)
                            key = ("B n", l)
                            nc.scalar.activation(nT[:], turned(key), ACT.Identity, bias=w(f"lnb{l}"), scale=w(f"lng{l}")
                                                 ).then_inc(T.empty(key), 1)
                            yield ("B nT", l)
                            for i in range(3):
                                key = ("B w1", l, i, 1)
                                if i == 2:
                                    act.wait_ge(*S.emptied(("B w1", l, 0, 0)))
                                act.wait_ge(*S.filled(key))
                                nc.scalar.activation(st.gl[:, i % 2, :], S.bank(key), ACT.Gelu, bias=w(f"b1g{l}")[:, i:i + 1]
                                                     ).then_inc(S.empty(key), 1)
                                yield ("B w1", l, i)
                            yield ("B w2", l)
                        if last_stage == "B":
                            return

                        def copied(key, dst):
                            act.wait_ge(*M.filled(key))
                            nc.scalar.activation(dst, M.bank(key), ACT.Copy).then_inc(M.empty(key), 1)

                        yield "C kv"
                        yield "statistics", "C"
                        yield "C kf"
                        copied("C kf", st.wf)
                        yield "C n"
                        nc.scalar.activation(nT[:], turned("C n"), ACT.Copy).then_inc(T.empty("C n"), 1)
                        yield "C q"
                        yield "C qf"
                        yield "C g"
                        yield "C corr"
                        act.wait_ge(*st.peak.done("C"))
                        nc.scalar.activation(st.ew[:], st.corr[:, 0:SEQ], ACT.Exp, bias=st.top[:, 16:17]).then_inc(st.selection_exps.sem, 1)
                        yield "C vf"
                        copied("C vf", st.wf)
                        yield "C w"
                        weights_T = turned("C w")[:, 0:TILES * HEADS].rearrange("p (t h) -> p t h", t=TILES)
                        nc.scalar.activation(st.wx.rearrange("p (t h d) -> p t h d", t=TILES, h=HEADS),
                                             weights_T[:, :, :, None].broadcast_to([P, TILES, HEADS, HD]), ACT.Copy
                                             ).then_inc(T.empty("C w"), 1)
                        yield "C wf"
                        yield "C of"
                        copied("C of", st.of)
                        yield "C out"
                        copied("C out", nT[:])
                        yield "C wo"
                        if last_stage == "C":
                            return

                        yield "statistics", "D0"
                        yield "statistics", "D1"
                        yield "D n"
                        nc.scalar.activation(nT[:], turned("D n"), ACT.Identity, bias=w("ln1b"), scale=w("ln1w")
                                             ).then_inc(T.empty("D n"), 1)
                        yield "D k"
                        act.wait_ge(*M.filled("D k"))
                        nc.scalar.activation(st.kD, M.bank("D k"), ACT.Identity, bias=w("dbk")).then_inc(M.empty("D k"), 1)
                        yield "D q"
                        act.wait_ge(*M.filled("D q"))
                        nc.scalar.activation(st.QT[:], M.bank("D q"), ACT.Identity, bias=w("dbq")).then_inc(M.empty("D q"), 1)
                        yield "D v"
                        for i in range(ND + 5):
                            if TURN <= i < ND + TURN:
                                t, heads = CAUSAL_UNITS[i - TURN]
                                turned_out(("D p", i - TURN), i - TURN, n=len(heads) * (t + 1) * P)
                            if i < ND:
                                t, heads = CAUSAL_UNITS[i]
                                wide = (t + 1) * P
                                act.wait_ge(*st.maxima.done(("D", i)))
                                for n, h in enumerate(heads):
                                    row = st.probs[:, i % 2, n * wide:(n + 1) * wide]
                                    last = nc.scalar.activation(row, row, ACT.Exp, bias=st.nm[:, i % 2, n:n + 1], scale=SCALE,
                                                                accum_out=st.sums_of[:, t % 2, h:h + 1])
                                last.then_inc(st.exps.sem, 1)
                            yield ("D", i)
                        yield "statistics", "D2"
                        yield "D n2"
                        nc.scalar.activation(nT[:], turned("D n2"), ACT.Identity, bias=w("ln2b"), scale=w("ln2w")
                                             ).then_inc(T.empty("D n2"), 1)
                        yield "D gate"
                        act.wait_ge(*st.peak.done("D"))
                        nc.scalar.activation(st.gex[:], st.gex[:], ACT.Exp).then_inc(st.selection_exps.sem, 1)
                        yield "D peak"
                        fc1b = w("fc1b").rearrange("p (e c) -> p e c", e=EXPERTS)

                        def hidden(e):
                            for n in range(FC):
                                key = ("D f1", e, n)
                                act.wait_ge(*S.filled(key))
                                nc.scalar.activation(st.hid[:, e % 2, n, :], S.bank(key), ACT.Gelu, bias=fc1b[:, e, n:n + 1]
                                                     ).then_inc(S.empty(key), 1)

                        hidden(0)
                        yield "D up"
                        yield "D g"
                        nc.scalar.activation(st.gT[:], turned("D g")[0:EXPERTS, :], ACT.Copy).then_inc(T.empty("D g"), 1)
                        yield "D b2"
                        for e in range(EXPERTS):
                            if e + 1 < EXPERTS:
                                if e:
                                    act.wait_ge(*M.filled(("D f2", e - 1)))
                                hidden(e + 1)
                            yield ("D e", e)

                    alternate("act", stream_program)

                @block.vector
                def _(dve):
                    v = nc.vector
                    chained = [0]

                    def link(instruction):
                        chained[0] += 1
                        instruction.then_inc(dve_chain, 1)
                        dve.wait_ge(dve_chain, chained[0])

                    def stream_program(st):
                        S, T, M, x, y, ntok, nT, hT = st.S, st.T, st.M, st.x, st.y, st.ntok, st.nT, st.hT
                        probs, mx, nm = st.probs, st.mx, st.nm

                        def layer_norm(key, source, out, first=0):
                            for t in range(first, TILES):
                                last = v.bn_stats(st.stats[:, t], source(t))
                            link(last)
                            for t in range(TILES):
                                last = v.bn_aggr(st.mv[:, t], st.stats[:, t])
                            last.then_inc(st.stats_ready.sem, 1)
                            yield "statistics", key
                            dve.wait_ge(*st.rstd_ready.done(key))
                            for t in range(TILES):
                                last = v.tensor_scalar(out[:, t], source(t), st.mv[:, t, 0:1], st.rstd[:, t:t + 1],
                                                       ALU.subtract, ALU.mult)
                            last.then_inc(st.normed.sem, 1)

                        def made(key, ring=None):
                            ring = ring or M
                            dve.wait_ge(*ring.filled(key))
                            return ring.bank(key)

                        def add_tokens(key, stream):
                            src = made(key).rearrange("p (t d) -> p t d", t=TILES)
                            v.tensor_tensor(stream[:], src, stream[:], ALU.add).then_inc(M.empty(key), 1)

                        def reciprocals(stage, t, u):
                            dve.wait_ge(*st.exps.done((stage, u)))
                            if t:
                                dve.wait_ge(*st.widened.done((stage, t - 1)))
                            v.reciprocal(st.rsum[:], st.sums_of[:, t % 2, :]).then_inc(st.reciprocals.sem, 1)

                        def spread_out(stage, t):
                            if t:
                                dve.wait_ge(*M.emptied((stage + " o", t - 1)))
                            v.tensor_copy(st.recip, made((stage + " r", t), T)).then_inc(T.empty((stage + " r", t)), 1)

                        def normalize(stage, t):
                            dve.wait_ge(*T.emptied((stage + " r", t)))
                            dve.wait_ge(*M.filled((stage + " o", t)))
                            if t:
                                dve.wait_ge(*T.filled((stage + " wo", t - 1)))
                            v.tensor_tensor(st.oP.rearrange("p j q -> p (j q)"), M.bank((stage + " o", t)), st.recip, ALU.mult
                                            ).then_inc(M.empty((stage + " o", t)), 1)

                        def add_tile(key, stream, t):
                            src = made(key, T)
                            v.tensor_tensor(stream[:, t], src[:, 0:P], stream[:, t], ALU.add).then_inc(T.empty(key), 1)

                        dve.wait_ge(st.x_in, 16)
                        yield from layer_norm("A", lambda t: x[:, t], ntok)
                        dve.wait_ge(consts_in, 16)
                        dve.wait_ge(weights_in, 16)
                        yield "A n"
                        kv = made("A kv")
                        v.memset(st.vA[:], 0.0)
                        link(v.tensor_scalar(st.kA, kv[:, 0:CTX], w("abk"), None, ALU.add))
                        v.tensor_tensor(st.kTmA[:], st.kA[:, None, :].broadcast_to([P, HEADS, CTX]),
                                        c("headmask")[:, :, None].broadcast_to([P, HEADS, CTX]), ALU.mult)
                        v.tensor_tensor(st.vA[0:CTX, :, 0:HD], kv[0:CTX, P:2 * P].rearrange("p (h d) -> p h d", h=HEADS),
                                        w("abv", CTX).rearrange("p (h d) -> p h d", h=HEADS), ALU.add
                                        ).then_inc(M.empty("A kv"), 1)
                        dve.wait_ge(*M.emptied("A kv"))
                        v.tensor_copy(st.small[:, 5:6], st.small[:, 4:5]).then_inc(st.prepared.sem, 1)
                        yield "A q"
                        v.tensor_scalar(st.QT[:], made("A q"), w("abq"), SCALE, ALU.add, ALU.mult).then_inc(M.empty("A q"), 1)
                        dve.wait_ge(*st.mask_scaled.done("A"))
                        for i in range(NA + 5):
                            if i >= 5 + USE and (i - USE) % 4 == 1:
                                t = (i - 5 - USE) // 4
                                if t == 0:
                                    dve.wait_ge(*st.biased.done("A"))
                                add_tile(("A wo", t), x, t)
                                if t + 1 < TILES:
                                    dve.wait_ge(*T.emptied(("A wo", t)))
                                    v.bn_stats(st.stats[:, t], x[:, t])
                            if i >= 4 + USE and i % 4 == USE % 4:
                                normalize("A", (i - 4 - USE) // 4)
                            if i >= USE and (i - USE) % 4 == 3:
                                spread_out("A", (i - USE) // 4)
                            if TURN <= i < NA + TURN:
                                u, key = i - TURN, ("A p", i - TURN)
                                v.tensor_copy(st.probsT[0:CTX, u % 2, :], made(key, T)[0:CTX, :]).then_inc(T.empty(key), 1)
                            if i < NA:
                                t, key = i // 4, ("A s", i)
                                k = i % 2
                                if i >= 2:
                                    dve.wait_ge(*T.filled(("A p", i - 2)))
                                dve.wait_ge(*S.filled(key))
                                for n in range(4):
                                    last = v.tensor_tensor_reduce(
                                        probs[:, k, n * CTX:(n + 1) * CTX], S.bank(key)[:, n * CTX:(n + 1) * CTX], st.maskb[:, t, :],
                                        1.0, SENTINEL, ALU.add, ALU.max, mx[:, k, n:n + 1])
                                last.then_inc(S.empty(key), 1)
                                dve.wait_ge(*S.emptied(key))
                                v.tensor_scalar(nm[:, k, :], mx[:, k, :], -1.0, None, ALU.mult).then_inc(st.maxima.sem, 1)
                            if 4 <= i <= NA and i % 4 == 0:
                                reciprocals("A", (i - 1) // 4, i - 1)
                            yield ("A", i)
                        if last_stage == "A":
                            return

                        dve.wait_ge(*T.emptied(("A wo", TILES - 1)))
                        yield from layer_norm("B", lambda t: x[:, t], y, first=TILES - 1)
                        v.memset(hT[64:P, 0:1], 0.0)
                        link(v.memset(st.vmix[0:WIN, 0, :], 0.0))
                        v.memset(st.vnat_heads[:, :, :, LHD:LHD + 1], 1.0)
                        v.memset(st.vmix_heads[:, :, :, LHD:LHD + 1], 1.0).then_inc(st.ones.sem, 1)
                        for l in range(LAYERS):
                            yield ("B y", l)
                            yield ("B shift", l)

                            for i in range(TILES + 1):
                                if i >= 1:
                                    dve.wait_ge(*S.emptied(("B q", l, i - 1)))
                                    link(v.tensor_tensor(st.t1[(i - 1) % 2][:, 0], st.t1[(i - 1) % 2][:, 0], st.t2[:, 0], ALU.add))
                                    dve.wait_ge(*st.turns_added.done((l, i - 1)))
                                    t1 = st.t1[(i - 1) % 2].rearrange("p a (h d) -> p (a h) d", d=LHD)
                                    v.tensor_tensor(t1, t1, st.rn[:, (i - 1) % 2, :, None].broadcast_to([P, 2 * LHEADS, LHD]), ALU.mult
                                                    ).then_inc(st.rotated.sem, 1)
                                if i < TILES:
                                    dve.wait_ge(*st.squares.done((l, i, 1)))
                                    v.tensor_reduce(st.ss[:, i % 2, :], st.sq.rearrange("p a (h d) -> p (a h) d", d=LHD), X_AXIS,
                                                    ALU.add).then_inc(st.sums.sem, 1)
                                    if i >= 2:
                                        dve.wait_ge(*T.filled(("B qk", l, i - 2, 1)))
                                    if i == 0:
                                        dve.wait_ge(rotary_made, LAYERS)
                                    for j, name in enumerate(("B q", "B k")):
                                        src = S.bank((name, l, i)).rearrange("p (h d) -> p h d", d=LHD)
                                        v.tensor_tensor(st.t1[i % 2][:, j].rearrange("p (h d) -> p h d", d=LHD), src,
                                                        rot[l][:, i, j, 0, None, :].broadcast_to([P, LHEADS, LHD]), ALU.mult)
                                        out = st.t2[:, j].rearrange("p (h d) -> p h d", d=LHD)
                                        for o, n in ((0, 32), (32, 0)):
                                            last = v.tensor_tensor(out[:, :, o:o + 32], src[:, :, n:n + 32],
                                                                   rot[l][:, i, j, 1, None, o:o + 32].broadcast_to([P, LHEADS, 32]),
                                                                   ALU.mult)
                                        last.then_inc(S.empty((name, l, i)), 1)
                                yield ("B qk", l, i)
                            for i in range(2 * TILES + 4):
                                if USE < i <= 2 * TILES + USE:
                                    u = i - USE - 1
                                    t, half = divmod(u, 2)
                                    if half == 0 and t:
                                        dve.wait_ge(*T.filled(("B o", l, t - 1)))
                                    key = ("B o", l, u)
                                    src = made(key)[:, 0:4 * VN].rearrange("p (h d) -> p h d", h=4)
                                    link(v.reciprocal(st.rden[:, half, 0:4], src[:, :, LHD]))
                                    v.tensor_tensor(st.o8.rearrange("p (a h d) -> p a h d", a=2, h=4)[:, half],
                                                    src[:, :, 0:LHD], st.rden[:, half, 0:4, None].broadcast_to([P, 4, LHD]),
                                                    ALU.mult).then_inc(M.empty(key), 1)
                                if i < 2 * TILES:
                                    key = ("B s", l, i)
                                    k = i % 2
                                    if i >= 2:
                                        dve.wait_ge(*T.filled(("B p", l, i - 2)))
                                    dve.wait_ge(*S.filled(key))
                                    mask = c("local")[:, (0 if i < 2 else P):(P if i < 2 else 2 * P)]
                                    for n in range(4):
                                        last = v.tensor_tensor_reduce(
                                            probs[:, k, n * P:(n + 1) * P], S.bank(key)[:, n * P:(n + 1) * P], mask,
                                            1.0, SENTINEL, ALU.add, ALU.max, mx[:, k, n:n + 1])
                                    last.then_inc(S.empty(key), 1)
                                    dve.wait_ge(*S.emptied(key))
                                    v.tensor_scalar(nm[:, k, :], mx[:, k, :], -QK_SCALE, None, ALU.mult).then_inc(st.maxima.sem, 1)
                                yield ("B s", l, i)
                            yield ("B wo", l)
                            add_tokens(("B wo", l), y)
                            yield ("B y2", l)
                            yield ("B tok", l)
                            key = ("B tok", l)
                            src = made(key, T).rearrange("p (t d) -> p t d", t=TILES)
                            yield from layer_norm(("F", l), lambda t: src[:, t], ntok)
                            dve.wait_ge(*st.normed.done(("F", l)))
                            v.tensor_copy(st.small[:, 5:6], st.small[:, 4:5]).then_inc(T.empty(key), 1)
                            yield ("B n", l)
                            yield ("B nT", l)
                            for i in range(3):
                                key = ("B w1", l, i, 0)
                                dve.wait_ge(*S.emptied(("B w1", l, i, 1)))
                                dve.wait_ge(*S.filled(key))
                                v.scalar_tensor_tensor(out=st.hidB[:, i, :], in0=S.bank(key), scalar=w(f"b1a{l}")[:, i:i + 1],
                                                       in1=st.gl[:, i % 2, :], op0=ALU.add, op1=ALU.mult).then_inc(S.empty(key), 1)
                                yield ("B w1", l, i)
                            dve.wait_ge(*st.biased.done(("B", l)))
                            yield ("B w2", l)
                            add_tokens(("B w2", l), y)
                        if last_stage == "B":
                            return

                        yield "C kv"
                        kv = made("C kv")
                        link(v.memset(st.kvtok[:], 0.0))
                        v.tensor_tensor(st.ktok[0:CTX], kv[0:CTX, 0:P], w("cbk", CTX), ALU.add)
                        v.tensor_tensor(st.vtok[0:CTX], kv[0:CTX, P:2 * P], w("cbv", CTX), ALU.add).then_inc(M.empty("C kv"), 1)
                        dve.wait_ge(*st.ffn_added.done("B"))
                        yield from layer_norm("C", lambda t: x[:, t], ntok)
                        yield "C kf"
                        yield "C n"
                        yield "C q"
                        v.tensor_tensor(hT[:].rearrange("p (t d) -> p t d", t=TILES), made("C q").rearrange("p (t d) -> p t d", t=TILES),
                                        w("cbq")[:, None, :].broadcast_to([P, TILES, P]), ALU.add).then_inc(M.empty("C q"), 1)
                        yield "C qf"

                        def multiply_spectra(first, second, cd_first):
                            dve.wait_ge(*M.emptied(second))
                            psum, sbuf = made(first), st.wf
                            v.tensor_tensor(st.p1, psum, sbuf, ALU.mult)
                            ab, cd = (sbuf, psum) if cd_first else (psum, sbuf)
                            v.tensor_tensor(st.p2[:, 0:HALF], ab[:, HALF:], cd[:, 0:HALF], ALU.mult)
                            v.tensor_tensor(st.p2[:, HALF:], ab[:, 0:HALF], cd[:, HALF:], ALU.mult).then_inc(M.empty(first), 1)
                            dve.wait_ge(*M.emptied(first))
                            v.memset(st.p2[:, HALF:HALF + 1], 0.0)
                            link(v.tensor_copy(st.p2[:, 0:1], st.p1[:, HALF:HALF + 1]))
                            v.memset(st.p1[:, HALF:HALF + 1], 0.0).then_inc(st.spectra.sem, 1)

                        multiply_spectra("C qf", "C kf", False)
                        yield "C g"
                        v.tensor_copy(st.G[:], made("C g")[:, 0:4 * HEADS].rearrange("p (i h) -> p i h", i=4)
                                      ).then_inc(M.empty("C g"), 1)
                        yield "C corr"
                        top, rep, ew, corr = st.top, st.rep, st.ew, st.corr
                        v.tensor_copy(corr[:, 0:SEQ], made("C corr")[0:HEADS, :]).then_inc(M.empty("C corr"), 1)
                        dve.wait_ge(*M.emptied("C corr"))
                        link(v.max(top[:, 0:8], corr[:, 0:SEQ]))
                        v.tensor_scalar(top[:, 16:17], top[:, 0:1], -1.0, None, ALU.mult).then_inc(st.peak.sem, 1)
                        link(v.tensor_copy(top[:, 8:8 + TOPK], top[:, 0:TOPK]))
                        link(v.match_replace(rep[:], top[:, 8:16], corr[:], REPLACED))
                        link(v.tensor_tensor(rep[:, 0:SEQ], rep[:, 0:SEQ], corr[:, 0:SEQ], ALU.not_equal))
                        dve.wait_ge(*st.selection_exps.done("C"))
                        link(v.tensor_tensor(ew[:], ew[:], rep[:, 0:SEQ], ALU.mult))
                        link(v.tensor_reduce(top[:, 17:18], ew[:], X_AXIS, ALU.add))
                        link(v.reciprocal(top[:, 18:19], top[:, 17:18]))
                        v.tensor_scalar(ew[:], ew[:], top[:, 18:19], None, ALU.mult).then_inc(st.selection.sem, 1)
                        yield "C vf"
                        yield "C w"
                        yield "C wf"
                        multiply_spectra("C wf", "C vf", True)
                        yield "C of"
                        yield "C out"
                        yield "C wo"
                        dve.wait_ge(*st.biased.done("C"))
                        add_tokens("C wo", x)
                        if last_stage == "C":
                            return

                        dve.wait_ge(*M.emptied("C wo"))
                        yield from layer_norm("D0", lambda t: x[:, t], y)
                        dve.wait_ge(*st.normed.done("D0"))
                        yield from layer_norm("D1", lambda t: y[:, t], ntok)
                        yield "D n"
                        yield "D k"
                        dve.wait_ge(*M.emptied("D k"))
                        mask_keys(v, st, 0).then_inc(st.prepared.sem, 1)
                        yield "D q"
                        yield "D v"
                        dve.wait_ge(*st.cleared.done("D"))
                        v.tensor_tensor(st.vD[:, :, :, 0:HD], made("D v").rearrange("p (t h d) -> p t h d", t=TILES, h=HEADS),
                                        w("dbv").rearrange("p (h d) -> p h d", h=HEADS)[:, None, :, :].broadcast_to([P, TILES, HEADS, HD]),
                                        ALU.add).then_inc(M.empty("D v"), 1)
                        for i in range(ND + 5):
                            if i - USE - 2 in LAST_UNIT:
                                t = LAST_UNIT.index(i - USE - 2)
                                if t == 0:
                                    dve.wait_ge(*st.biased.done("D"))
                                add_tile(("D wo", t), y, t)
                                if t + 1 < TILES:
                                    dve.wait_ge(*T.emptied(("D wo", t)))
                                    v.bn_stats(st.stats[:, t], y[:, t])
                            if i - USE - 1 in LAST_UNIT:
                                normalize("D", LAST_UNIT.index(i - USE - 1))
                            if i - USE in LAST_UNIT:
                                spread_out("D", LAST_UNIT.index(i - USE))
                            if i < ND:
                                t, heads = CAUSAL_UNITS[i]
                                wide = (t + 1) * P
                                key = ("D s", i)
                                k = i % 2
                                if i >= 2:
                                    dve.wait_ge(*T.filled(("D p", i - 2)))
                                dve.wait_ge(*S.filled(key))
                                mask = c("causal")[:, SEQ - wide:SEQ]
                                for n in range(len(heads)):
                                    last = v.tensor_tensor_reduce(
                                        probs[:, k, n * wide:(n + 1) * wide], S.bank(key)[:, n * wide:(n + 1) * wide], mask,
                                        1.0, SENTINEL, ALU.add, ALU.max, mx[:, k, n:n + 1])
                                last.then_inc(S.empty(key), 1)
                                dve.wait_ge(*S.emptied(key))
                                n = len(heads)
                                v.tensor_scalar(nm[:, k, 0:n], mx[:, k, 0:n], -SCALE, None, ALU.mult).then_inc(st.maxima.sem, 1)
                            if i - 1 in LAST_UNIT:
                                reciprocals("D", LAST_UNIT.index(i - 1), i - 1)
                            yield ("D", i)
                        dve.wait_ge(*T.emptied(("D wo", TILES - 1)))
                        yield from layer_norm("D2", lambda t: y[:, t], ntok, first=TILES - 1)
                        yield "D n2"
                        yield "D gate"
                        logit, gtop, gtwo, gex, lrep = st.logit, st.gtop, st.gtwo, st.gex, st.lrep
                        v.tensor_copy(logit[:, :, 0:8], made("D gate")[:, 0:TILES * EXPERTS].rearrange("p (t e) -> p t e", t=TILES)
                                      ).then_inc(M.empty("D gate"), 1)
                        dve.wait_ge(*M.emptied("D gate"))
                        for t in range(TILES):
                            last = v.max(gtop[:, t, :], logit[:, t, 0:8])
                        link(last)
                        v.tensor_tensor(gex[:], logit[:, :, 0:8], gtop[:, :, 0:1].broadcast_to([P, TILES, 8]), ALU.subtract
                                        ).then_inc(st.peak.sem, 1)
                        link(v.tensor_copy(gtwo[:, :, 0:2], gtop[:, :, 0:2]))
                        for t in range(TILES):
                            last = v.match_replace(lrep[:, t, :], gtwo[:, t, :], logit[:, t, :], REPLACED)
                        link(last)
                        link(v.tensor_tensor(lrep[:, :, 0:8], lrep[:, :, 0:8], logit[:, :, 0:8], ALU.not_equal))
                        yield "D peak"
                        dve.wait_ge(*st.selection_exps.done("D"))
                        link(v.tensor_tensor(gex[:], gex[:], lrep[:, :, 0:8], ALU.mult))
                        link(v.tensor_reduce(st.gsum[:], gex[:], X_AXIS, ALU.add))
                        link(v.reciprocal(st.gsum[:], st.gsum[:]))
                        v.tensor_tensor(st.gates[:], gex[:], st.gsum[:, :, None].broadcast_to([P, TILES, 8]), ALU.mult
                                        ).then_inc(st.selection.sem, 1)
                        yield "D up"
                        yield "D g"
                        yield "D b2"
                        add_tokens("D b2", y)
                        dve.wait_ge(*M.emptied("D b2"))
                        dve.wait_ge(*st.selection.done("D"))
                        for e in range(EXPERTS):
                            key = ("D f2", e)
                            if e:
                                dve.wait_ge(*M.emptied(("D f2", e - 1)))
                            src = made(key)
                            for t in range(TILES):
                                last = v.scalar_tensor_tensor(out=y[:, t], in0=src[:, t * P:(t + 1) * P], scalar=st.gates[:, t, e:e + 1],
                                                              in1=y[:, t], op0=ALU.mult, op1=ALU.add)
                            last.then_inc(M.empty(key), 1)
                            yield ("D e", e)
                        dve.wait_ge(*M.emptied(("D f2", EXPERTS - 1)))
                        v.tensor_tensor(x[:], x[:], y[:], ALU.add).then_inc(st.finished.sem, 1)

                    alternate("dve", stream_program)

                @block.gpsimd
                def _(pool):
                    g = nc.gpsimd
                    chained = [0]

                    def link(instruction):
                        chained[0] += 1
                        instruction.then_inc(pool_chain, 1)
                        pool.wait_ge(pool_chain, chained[0])

                    def rotary_tables():
                        pool.wait_ge(rotary_in, 16)
                        pool.wait_ge(autocorrelation_in, 16)
                        for l in range(LAYERS):
                            for j, name in enumerate(("qs", "ks")):
                                scale = w(f"{name}{l}")
                                g.tensor_tensor(rot[l][:, :, j, 0, :], rot_base[:, :, j, 0, :],
                                                scale[:, None, :].broadcast_to([P, TILES, LHD]), ALU.mult)
                                for o, i in ((0, 32), (32, 0)):
                                    last = g.tensor_tensor(rot[l][:, :, j, 1, o:o + 32], rot_base[:, :, j, 1, o:o + 32],
                                                           scale[:, None, i:i + 32].broadcast_to([P, TILES, 32]), ALU.mult)
                            last.then_inc(rotary_made, 1)
                            pool.wait_ge(rotary_made, l + 1)

                    def stream_program(st):
                        S, T, M, x, y = st.S, st.T, st.M, st.x, st.y

                        def rsqrt(key):
                            pool.wait_ge(*st.stats_ready.done(key))
                            link(g.tensor_scalar(st.small[:, 0:TILES], st.mv[:, :, 1], EPS, None, ALU.add))
                            g.tensor_tensor(st.rstd[:], st.small[:, 0:TILES], mhalf[:, 0:TILES], ALU.pow).then_inc(st.rstd_ready.sem, 1)

                        def widen(stage, t):
                            pool.wait_ge(*st.reciprocals.done((stage, t)))
                            if t:
                                pool.wait_ge(*T.filled((stage + " r", t - 1)))
                            g.tensor_copy(st.rwide.rearrange("p (h r) -> p h r", h=HEADS),
                                          st.rsum[:, :, None].broadcast_to([P, HEADS, 32])).then_inc(st.widened.sem, 1)

                        def add_bias(stream, name):
                            g.tensor_tensor(stream[:], stream[:], w(name)[:, None, :].broadcast_to([P, TILES, P]), ALU.add
                                            ).then_inc(st.biased.sem, 1)

                        rsqrt("A")
                        yield "statistics", "A"
                        yield "A n"
                        pool.wait_ge(st.mask_in, 16)
                        g.tensor_scalar(st.maskb[:], st.maskb[:], NEG, None, ALU.mult).then_inc(st.mask_scaled.sem, 1)
                        pool.wait_ge(*st.normed.done("A"))
                        pool.wait_ge(weights_in, 16)
                        add_bias(x, "abo")
                        if st.index == 0:
                            rotary_tables()
                        yield "A q"
                        for i in range(NA + 5):
                            if 4 <= i <= NA and i % 4 == 0:
                                widen("A", (i - 1) // 4)
                            yield ("A", i)
                        if last_stage == "A":
                            return

                        rsqrt("B")
                        yield "statistics", "B"
                        pool.wait_ge(*st.ones.done("B"))
                        g.memset(st.kTz[:], 0.0).then_inc(st.cleared.sem, 1)
                        for l in range(LAYERS):
                            yield ("B y", l)
                            yield ("B shift", l)
                            for i in range(TILES + 1):
                                if i < TILES:
                                    pool.wait_ge(*st.sums.done((l, i)))
                                    link(g.tensor_scalar(st.rn[:, i % 2, :], st.ss[:, i % 2, :], 1e-24, None, ALU.max))
                                    g.tensor_tensor(st.rn[:, i % 2, :], st.rn[:, i % 2, :], mhalf[:], ALU.pow).then_inc(st.norms.sem, 1)
                                    pool.wait_ge(*S.emptied(("B k", l, i)))
                                    g.tensor_tensor(st.t1[i % 2][:, 1], st.t1[i % 2][:, 1], st.t2[:, 1], ALU.add).then_inc(st.turns_added.sem, 1)
                                yield ("B qk", l, i)
                            for i in range(2 * TILES + 4):
                                yield ("B s", l, i)
                            yield ("B wo", l)
                            yield ("B y2", l)
                            yield ("B tok", l)
                            rsqrt(("F", l))
                            yield "statistics", ("F", l)
                            pool.wait_ge(*T.filled(("B y2", l)))
                            add_bias(y, f"b2{l}")
                            yield ("B n", l)
                            yield ("B nT", l)
                            for i in range(3):
                                yield ("B w1", l, i)
                            yield ("B w2", l)
                        pool.wait_ge(*M.emptied(("B w2", LAYERS - 1)))
                        g.tensor_tensor(x[:], x[:], y[:], ALU.add).then_inc(st.ffn_added.sem, 1)
                        if last_stage == "B":
                            return

                        yield "C kv"
                        rsqrt("C")
                        yield "statistics", "C"
                        pool.wait_ge(*st.normed.done("C"))
                        add_bias(x, "cbo")
                        g.memset(st.vD[:], 0.0).then_inc(st.cleared.sem, 1)
                        for name in ("kf", "n", "q", "qf", "g", "corr", "vf", "w", "wf", "of", "out", "wo"):
                            yield "C " + name
                        if last_stage == "C":
                            return

                        rsqrt("D0")
                        yield "statistics", "D0"
                        rsqrt("D1")
                        yield "statistics", "D1"
                        pool.wait_ge(*st.normed.done("D1"))
                        pool.wait_ge(causal_in, 16)
                        add_bias(y, "dbo")
                        yield "D n"
                        yield "D k"
                        pool.wait_ge(*M.emptied("D k"))
                        for t in range(1, TILES):
                            mask_keys(g, st, t).then_inc(st.masked_keys.sem, 1)
                        yield "D q"
                        yield "D v"
                        for i in range(ND + 5):
                            if i - 1 in LAST_UNIT:
                                widen("D", LAST_UNIT.index(i - 1))
                            yield ("D", i)
                        rsqrt("D2")
                        yield "statistics", "D2"
                        for name in ("n2", "gate", "peak", "up", "g", "b2"):
                            yield "D " + name
                        for e in range(EXPERTS):
                            yield ("D e", e)

                    alternate("pool", stream_program)

                @block.sync
                def _(sp):
                    def batches(dram, st):
                        return dram.rearrange("(r s) n d -> s r n d", s=STREAMS)[st.index]

                    for st in streams:
                        here = bass.ds(round_no, 1)
                        sp.dma_start(st.x[:], batches(x_dram, st)[here, :, :].rearrange("o (t p) d -> p (o t) d", p=P)).then_inc(st.x_in, 16)
                        sp.dma_start(st.ctxT[:], batches(ctxT_dram, st)[here, :, :].rearrange("o p k -> p (o k)")).then_inc(st.ctx_in, 16)
                        sp.dma_start(st.maskb[:], batches(mask_dram, st)[here, :, :].rearrange("o (t p) k -> p (o t) k", p=P)).then_inc(st.mask_in, 16)
                    a, b = CCOL["rot"]
                    sp.dma_start(c("rot"), consts_dram[:, a:b]).then_inc(rotary_in, 16)
                    a = WCOL["qs0"][0]
                    sp.dma_start(wt[:, a:STAY], weights_dram[:, a:STAY]).then_inc(autocorrelation_in, 16)
                    for l in range(LAYERS):
                        a = STAY + l * LAYER_COLS
                        sp.dma_start(place[l][:, 0:LAYER_COLS], weights_dram[:, a:a + LAYER_COLS]).then_inc(layer_in[l], 16)
                    if last_stage in "CD":
                        for st in streams:
                            sp.wait_ge(*st.M.filled(("B w2", 0)))
                            sp.wait_ge(*st.biased.done(("B", 0)))
                        sp.dma_start(place[0][:, 0:2 * TILES * SEQ], consts_dram[:, CCOL["dft"][0]:]).then_inc(fourier_in, 16)
                    if last_stage == "D":
                        for st in streams:
                            sp.wait_ge(*st.M.filled(("B w2", 1)))
                            sp.wait_ge(*st.biased.done(("B", 1)))
                        a = WCOL["ln1w"][0]
                        sp.dma_start(place[1][:, 0:WTOTAL - a], weights_dram[:, a:]).then_inc(causal_in, 16)
                        for st in streams:
                            sp.wait_ge(*st.M.filled("C out"))
                        for e in range(EXPERTS):
                            if e >= EXPERT_SLOTS:
                                for st in streams:
                                    sp.wait_ge(*st.M.filled(("D f2", e - EXPERT_SLOTS)))
                            sp.dma_start(experts[:, e % EXPERT_SLOTS, :], experts_dram[e]).then_inc(expert_in[e % EXPERT_SLOTS], 16)
                    for st in streams:
                        if last_stage == "D":
                            sp.wait_ge(*st.finished.done("D"))
                        elif last_stage == "A":
                            sp.wait_ge(*st.T.emptied(("A wo", TILES - 1)))
                        elif last_stage == "B":
                            sp.wait_ge(*st.ffn_added.done("B"))
                        else:
                            sp.wait_ge(*st.M.emptied("C wo"))
                        sp.dma_start(batches(out_dram, st)[bass.ds(round_no, 1), :, :].rearrange("o (t p) d -> p (o t) d", p=P),
                                     st.x[:]).then_inc(st.x_out, 16)
                    for st in streams:
                        sp.wait_ge(st.x_out, 16)
            nc.all_engine_barrier()
            first, n = batch_sems[0].num, len(batch_sems)
            assert [s.num for s in batch_sems] == list(range(first, first + n))
            nc.gpsimd.sem_clear(range(first, first + n))
            nc.all_engine_barrier()


def constants():
    import numpy as np
    out = np.zeros((P, CTOTAL), np.float32)

    def put(name, value):
        a, b = CCOL[name]
        out[:, a:b] = np.asarray(value).reshape(P, b - a)

    part = np.arange(P)
    put("ident", np.eye(P))
    put("nident", -np.eye(P))
    put("headmask", part[:, None] // HD == np.arange(HEADS)[None, :])
    ind = (part[:, None] // HD == np.arange(HEADS)[None, :]) / HD
    put("ind", ind)
    put("nind", -ind)
    i, j = (part % WIN)[:, None], np.arange(P)[None, :]
    allowed = (i <= j) & (j <= i + WIN)
    first = allowed & ((part >= WIN)[:, None] | (j >= WIN))
    put("local", np.where(np.concatenate([first, allowed], 1), 0.0, -1e37))
    q, k = part[:, None], np.arange(SEQ)[None, :]
    put("causal", np.where(k - (SEQ - P) <= q, 0.0, -1e37))
    half = np.arange(0, LHD, 2, dtype=np.float32)
    inv = (1.0 / np.float32(10000.0) ** (half / LHD)).astype(np.float32)
    pos = np.arange(SEQ, dtype=np.float32)
    freqs = np.tile(pos[:, None] * inv[None, :], (1, 2)).astype(np.float32)
    base = (half + 0.4 * LHD) / (1.4 * LHD)
    scale = np.tile(base[None, :] ** ((pos - SEQ // 2) / (WIN // 2))[:, None], (1, 2)).astype(np.float64)
    cos, sin = np.cos(freqs.astype(np.float64)), np.sin(freqs.astype(np.float64))
    sin[:, :LHD // 2] *= -1
    rot = np.stack([np.stack([cos * scale, sin * scale], 1), np.stack([cos / scale, sin / scale], 1)], 1)
    put("rot", rot.reshape(TILES, P, 2, 2, LHD).transpose(1, 0, 2, 3, 4))
    n = np.arange(SEQ)[:, None]
    f = np.arange(HALF)[None, :]
    angle = 2 * np.pi * ((n * f) % SEQ) / SEQ
    cosines, sines = np.cos(angle), np.sin(angle)
    sines[:, 0] = (-1.0) ** n[:, 0]
    table = np.concatenate([cosines, sines], 1)
    put("dft", table.reshape(TILES, P, SEQ).transpose(1, 0, 2))
    weight = np.full((SEQ, 1), 2.0 / SEQ)
    weight[0] = weight[HALF] = 1.0 / SEQ
    put("idft", (table.T * weight).reshape(TILES, P, SEQ).transpose(1, 0, 2))
    return out


def pack_weights(a):
    import numpy as np
    out = np.zeros((P, WTOTAL), np.float32)

    def put(name, value, rows=P):
        lo, hi = WCOL[name]
        out[:rows, lo:hi] = np.asarray(value).reshape(rows, hi - lo)

    def row(v):
        return np.broadcast_to(np.asarray(v)[None, :], (P, len(v)))

    def spread(v):
        wide = np.zeros((4, 32, 4, P), np.float32)
        wide[:, :HD] = np.asarray(v).reshape(4, 4, HD, P).transpose(1, 2, 0, 3)
        return wide

    for s, k in (("a", "L0_xattn_"), ("c", "L1_xattn_")):
        for n in "qkvo":
            put(s + n, spread(a[f"{k}W{n}"]) if s + n == "ao" else a[f"{k}W{n}"])
    put("abq", a["L0_xattn_bq"])
    put("abk", a["L0_xattn_bk"])
    put("abv", row(a["L0_xattn_bv"]))
    put("abo", row(a["L0_xattn_bo"]))
    for n in "qkvo":
        put("cb" + n, row(a[f"L1_xattn_b{n}"]))
    f = {k[len("L0_ffn_"):]: np.asarray(v) for k, v in a.items() if k.startswith("L0_ffn_")}
    for l in range(LAYERS):
        put(f"qkv{l}", f["wqkv"][l])
        put(f"qs{l}", row(f["q_scale"][l]))
        put(f"ks{l}", row(f["k_scale"][l]))
        put(f"bwo{l}", f["wo"][l].reshape(PAIRS, P, P).transpose(1, 0, 2))
        put(f"lng{l}", f["ln_g"][l])
        put(f"lnb{l}", f["ln_b"][l])
        w1 = np.zeros((P, 2, 3 * P), np.float32)
        w1[:, :, :HID] = f["w1"][l].reshape(P, 2, HID)
        put(f"w1{l}", w1)
        b1 = np.zeros((2, 3 * P), np.float32)
        b1[:, :HID] = f["b1"][l].reshape(2, HID)
        put(f"b1a{l}", b1[0].reshape(3, P).T)
        put(f"b1g{l}", b1[1].reshape(3, P).T)
        w2 = np.zeros((3 * P, P), np.float32)
        w2[:HID] = f["w2"][l]
        put(f"w2{l}", w2.reshape(3, P, P).transpose(1, 0, 2))
        put(f"b2{l}", row(f["b2"][l]))
    d = {k[len("L1_ffn_"):]: np.asarray(v) for k, v in a.items() if k.startswith("L1_ffn_")}
    put("ln1w", d["ln1_w"])
    put("ln1b", d["ln1_b"])
    put("ln2w", d["ln2_w"])
    put("ln2b", d["ln2_b"])
    put("dqkv", d["Wqkv"])
    put("dbq", d["bqkv"][0:P])
    put("dbk", d["bqkv"][P:2 * P])
    put("dbv", row(d["bqkv"][2 * P:]))
    put("dwo", spread(d["Wo"]))
    put("dbo", row(d["bo"]))
    put("gate", d["gate_W"])
    put("fc2b", d["fc2_b"], EXPERTS)
    put("fc1b", d["fc1_b"].reshape(EXPERTS, FC, P).transpose(2, 0, 1))
    return out


def pack_experts(fc1_w, fc2_w):
    import numpy as np
    fc1 = np.asarray(fc1_w).transpose(0, 2, 1)
    fc2 = np.asarray(fc2_w).reshape(EXPERTS, P, FC, P).transpose(0, 3, 2, 1).reshape(EXPERTS, P, FFN)
    return np.ascontiguousarray(np.concatenate([fc1, fc2], 2))


def kernel(**inputs):
    import numpy as np
    import concourse.bacc as bacc
    from concourse.bass_utils import run_bass_kernel_spmd

    nc = bacc.Bacc("TRN2", target_bir_lowering=False, num_devices=1)
    arrays = {
        "x_in": np.ascontiguousarray(inputs["x"]),
        "ctxT_in": np.ascontiguousarray(np.asarray(inputs["ctx_1024"]).transpose(0, 2, 1)),
        "mask_in": np.ascontiguousarray(np.asarray(inputs["mask_Bx1xSxS2_fk0"])[:, 0]),
        "weights": pack_weights(inputs),
        "experts_in": pack_experts(inputs["L1_ffn_fc1_w"], inputs["L1_ffn_fc2_w"]),
        "constants": constants(),
    }
    args = [nc.dram_tensor(n, v.shape, F32, kind="ExternalInput").ap() for n, v in arrays.items()]
    args.append(nc.dram_tensor("x_result", (BATCH, SEQ, P), F32, kind="ExternalOutput").ap())
    program(nc, *args)
    r = run_bass_kernel_spmd(nc, [arrays], core_ids=[0])
    return r.results[0]["x_result"]
```
